# Optimizing a Trainium2 kernel written in Bass

```python
import numpy as np
import jax
import jax.numpy as jnp

def _softmax(x, axis=-1):
    return jax.nn.softmax(x, axis=axis)

def _gelu(x):
    return jax.nn.gelu(x, approximate=True)

def _silu(x):
    return jax.nn.silu(x)

def _sigmoid(x):
    return jax.nn.sigmoid(x)

def _layernorm(x, axis=-1, eps=1e-05):
    m = jnp.mean(x, axis=axis, keepdims=True)
    v = jnp.var(x, axis=axis, keepdims=True)
    return (x - m) / jnp.sqrt(v + eps)

def _scatter_add(tgt, idx, src, axis=0):
    return tgt.at[idx].add(src)

def _segment_sum(src, seg, n):
    return jax.ops.segment_sum(src, seg, n)
kernel_name = 'mk_decoder_preln_d1_seqx_r4_cde750'

def setup_inputs(seed: int=0):
    np.random.seed(seed)
    _w = jnp.asarray

    def _rec_inputs():
        import jax
        import jax.numpy as jnp
        _rk = jax.random.key(seed)
        x = 0.0003765 + 1 * jax.random.normal(jax.random.fold_in(_rk, 1), (8, 100, 256), jnp.float32)
        _lenS = 100 - jax.random.randint(jax.random.fold_in(_rk, 7), (8,), 0, max(1, 100 // 4) + 1, jnp.int32)
        _lenS2 = 361 - jax.random.randint(jax.random.fold_in(_rk, 8), (8,), 0, max(1, 361 // 4) + 1, jnp.int32)
        _ctx_1024P = jax.random.normal(jax.random.fold_in(_rk, 11), (8, 16, 256), jnp.float32)
        _ctx_1024c = jax.random.dirichlet(jax.random.fold_in(_rk, 511), 0.3 * jnp.ones((16,), jnp.float32), (8, 361))
        _ctx_1024t = jnp.einsum('bsk,bkd->bsd', _ctx_1024c, _ctx_1024P)
        _ctx_1024t = _ctx_1024t * jax.lax.rsqrt(jnp.mean(jnp.square(_ctx_1024t)) + 1e-12) * 0.953939
        ctx_1024 = -0.000292821 + 1.00034 * (_ctx_1024t + 0.3 * jax.random.normal(jax.random.fold_in(_rk, 611), (8, 361, 256), jnp.float32))
        return (x, ctx_1024)
    x, ctx_1024 = _rec_inputs()

    def _L0_attn_setup():
        import jax, jax.numpy as jnp
        import numpy as np
        D_MODEL = 256
        D_STATE = 32
        D_CONV = 4
        EXPAND = 2
        D_INNER = EXPAND * D_MODEL
        DT_RANK = D_MODEL // 16
        BATCH = 8
        SEQ = 256

        def _silu(x):
            return x * jax.nn.sigmoid(x)

        def _layernorm(x, g, b, eps=1e-05):
            m = x.mean(-1, keepdims=True)
            v = x.var(-1, keepdims=True)
            return (x - m) / jnp.sqrt(v + eps) * g + b

        def _mamba(x, Win, convw, convb, Wx, Wdt, bdt, Alog, Dp, Wout):
            Bn, Ln, _ = x.shape
            xz = jnp.einsum('bld,ed->ble', x, Win)
            u, z = jnp.split(xz, 2, axis=-1)
            up = jnp.pad(u, ((0, 0), (D_CONV - 1, 0), (0, 0)))
            uc = convb
            for k in range(D_CONV):
                uc = uc + up[:, k:k + Ln, :] * convw[:, k]
            uc = _silu(uc)
            x_dbl = jnp.einsum('bld,ed->ble', uc, Wx)
            dt = jax.nn.softplus(jnp.einsum('blr,dr->bld', x_dbl[..., :DT_RANK], Wdt) + bdt)
            Bv = x_dbl[..., DT_RANK:DT_RANK + D_STATE]
            Cv = x_dbl[..., DT_RANK + D_STATE:]
            A = -jnp.exp(Alog)

            def step(h, ins):
                dt_t, B_t, C_t, u_t = ins
                dA = jnp.exp(dt_t[..., None] * A)
                h = dA * h + (dt_t * u_t)[..., None] * B_t[:, None, :]
                y = jnp.einsum('bdn,bn->bd', h, C_t)
                return (h, y)
            h0 = jnp.zeros((Bn, D_INNER, D_STATE), x.dtype)
            xs = (dt.transpose(1, 0, 2), Bv.transpose(1, 0, 2), Cv.transpose(1, 0, 2), uc.transpose(1, 0, 2))
            _, ys = jax.lax.scan(step, h0, xs)
            y = ys.transpose(1, 0, 2) + uc * Dp
            y = y * _silu(z)
            return jnp.einsum('bld,ed->ble', y, Wout)
        key = jax.random.key(seed)
        ks = iter(jax.random.split(key, 64))

        def rn(shape, scale):
            return jax.random.normal(next(ks), shape, jnp.float32) * scale

        def direction_params():
            return dict(Win=rn((2 * D_INNER, D_MODEL), 0.02), convw=rn((D_INNER, D_CONV), 0.1), convb=jnp.zeros((D_INNER,), jnp.float32), Wx=rn((DT_RANK + 2 * D_STATE, D_INNER), 0.02), Wdt=rn((D_INNER, DT_RANK), 0.02), bdt=rn((D_INNER,), 0.5), Alog=jnp.log(jnp.broadcast_to(jnp.arange(1, D_STATE + 1, dtype=jnp.float32), (D_INNER, D_STATE))), Dp=jnp.ones((D_INNER,), jnp.float32), Wout=rn((D_MODEL, D_INNER), 0.02), ln_g=jnp.ones((D_MODEL,), jnp.float32), ln_b=jnp.zeros((D_MODEL,), jnp.float32))
        f = direction_params()
        b = direction_params()
        inp = {'x': rn((BATCH, SEQ, D_MODEL), 1.0)}
        for k, v in f.items():
            inp[k + '_f'] = v
        for k, v in b.items():
            inp[k + '_b'] = v
        inp['Wfuse'] = rn((D_MODEL, 2 * D_MODEL), 0.02)
        inp['bfuse'] = jnp.zeros((D_MODEL,), jnp.float32)
        return inp
    _L0_attn_all = _L0_attn_setup()
    _L0_attn_in = {k: v for k, v in _L0_attn_all.items() if k in ('Win_f', 'convw_f', 'convb_f', 'Wx_f', 'Wdt_f', 'bdt_f', 'Alog_f', 'Dp_f', 'Wout_f', 'ln_g_f', 'ln_b_f', 'Win_b', 'convw_b', 'convb_b', 'Wx_b', 'Wdt_b', 'bdt_b', 'Alog_b', 'Dp_b', 'Wout_b', 'ln_g_b', 'ln_b_b', 'Wfuse', 'bfuse')}
    del _L0_attn_all

    def _L0_xattn_setup():
        import jax, jax.numpy as jnp
        import numpy as np
        EMBED = 256
        HEADS = 16
        HEAD_DIM = EMBED // HEADS
        key = jax.random.key(seed)
        ks = jax.random.split(key, 8)
        B, S = (2, 512)
        return {'values': jax.random.normal(ks[0], (B, S, EMBED), jnp.float32), 'keys': jax.random.normal(ks[1], (B, S, EMBED), jnp.float32), 'query': jax.random.normal(ks[2], (B, S, EMBED), jnp.float32), 'Wv': jax.random.normal(ks[3], (EMBED, EMBED), jnp.float32) * EMBED ** (-0.5), 'Wk': jax.random.normal(ks[4], (EMBED, EMBED), jnp.float32) * EMBED ** (-0.5), 'Wq': jax.random.normal(ks[5], (EMBED, EMBED), jnp.float32) * EMBED ** (-0.5), 'Wo': jax.random.normal(ks[6], (EMBED, EMBED), jnp.float32) * EMBED ** (-0.5), 'bo': jnp.zeros((EMBED,), jnp.float32)}
    _L0_xattn_all = _L0_xattn_setup()
    _L0_xattn_in = {k: v for k, v in _L0_xattn_all.items() if k in ('Wv', 'Wk', 'Wq', 'Wo', 'bo')}
    del _L0_xattn_all

    def _L0_ffn_setup():
        import jax, jax.numpy as jnp
        import numpy as np
        B, S, H = (2, 512, 256)
        F = 1024
        E = 8
        TOP_K = 2
        SHARED_SCALE = 0.1
        EPS = 1e-09

        def _moe_forward(x3, Wg, W1, b1, W2, b2, Ws1, bs1, Ws2, bs2):
            b, s, h = x3.shape
            x = x3.reshape(-1, h)
            T = x.shape[0]
            logits = x @ Wg
            probs = jax.nn.softmax(logits, axis=-1)
            vals, idx = jax.lax.top_k(probs, TOP_K)
            weights = vals / (jnp.sum(vals, axis=-1, keepdims=True) + EPS)
            cw = jnp.zeros((T, E), dtype=x.dtype).at[jnp.arange(T)[:, None], idx].set(weights)
            hpre = jnp.einsum('th,ehf->tef', x, W1) + b1
            act = jax.nn.silu(hpre)
            y = jnp.einsum('tef,efh->teh', act, W2) + b2
            out = jnp.einsum('te,teh->th', cw, y)
            shared = jax.nn.silu(x @ Ws1 + bs1) @ Ws2 + bs2
            out = out + SHARED_SCALE * shared
            return out.reshape(b, s, h)
        key = jax.random.key(seed)
        ks = jax.random.split(key, 10)
        sc = 0.02
        return {'hidden_states': jax.random.normal(ks[0], (B, S, H), dtype=jnp.float32), 'Wg': jax.random.normal(ks[1], (H, E), dtype=jnp.float32) * sc, 'W1': jax.random.normal(ks[2], (E, H, F), dtype=jnp.float32) * sc, 'b1': jnp.zeros((E, F), dtype=jnp.float32), 'W2': jax.random.normal(ks[3], (E, F, H), dtype=jnp.float32) * sc, 'b2': jnp.zeros((E, H), dtype=jnp.float32), 'Ws1': jax.random.normal(ks[4], (H, F), dtype=jnp.float32) * sc, 'bs1': jnp.zeros((F,), dtype=jnp.float32), 'Ws2': jax.random.normal(ks[5], (F, H), dtype=jnp.float32) * sc, 'bs2': jnp.zeros((H,), dtype=jnp.float32)}
    _L0_ffn_all = _L0_ffn_setup()
    _L0_ffn_in = {k: v for k, v in _L0_ffn_all.items() if k in ('Wg', 'W1', 'b1', 'W2', 'b2', 'Ws1', 'bs1', 'Ws2', 'bs2')}
    del _L0_ffn_all
    return {'x': x, 'ctx_1024': ctx_1024, 'L0_attn_Win_f': _L0_attn_in['Win_f'], 'L0_attn_convw_f': _L0_attn_in['convw_f'], 'L0_attn_convb_f': _L0_attn_in['convb_f'], 'L0_attn_Wx_f': _L0_attn_in['Wx_f'], 'L0_attn_Wdt_f': _L0_attn_in['Wdt_f'], 'L0_attn_bdt_f': _L0_attn_in['bdt_f'], 'L0_attn_Alog_f': _L0_attn_in['Alog_f'], 'L0_attn_Dp_f': _L0_attn_in['Dp_f'], 'L0_attn_Wout_f': _L0_attn_in['Wout_f'], 'L0_attn_ln_g_f': _L0_attn_in['ln_g_f'], 'L0_attn_ln_b_f': _L0_attn_in['ln_b_f'], 'L0_attn_Win_b': _L0_attn_in['Win_b'], 'L0_attn_convw_b': _L0_attn_in['convw_b'], 'L0_attn_convb_b': _L0_attn_in['convb_b'], 'L0_attn_Wx_b': _L0_attn_in['Wx_b'], 'L0_attn_Wdt_b': _L0_attn_in['Wdt_b'], 'L0_attn_bdt_b': _L0_attn_in['bdt_b'], 'L0_attn_Alog_b': _L0_attn_in['Alog_b'], 'L0_attn_Dp_b': _L0_attn_in['Dp_b'], 'L0_attn_Wout_b': _L0_attn_in['Wout_b'], 'L0_attn_ln_g_b': _L0_attn_in['ln_g_b'], 'L0_attn_ln_b_b': _L0_attn_in['ln_b_b'], 'L0_attn_Wfuse': _L0_attn_in['Wfuse'], 'L0_attn_bfuse': _L0_attn_in['bfuse'], 'L0_xattn_Wv': _L0_xattn_in['Wv'], 'L0_xattn_Wk': _L0_xattn_in['Wk'], 'L0_xattn_Wq': _L0_xattn_in['Wq'], 'L0_xattn_Wo': _L0_xattn_in['Wo'], 'L0_xattn_bo': _L0_xattn_in['bo'], 'L0_ffn_Wg': _L0_ffn_in['Wg'], 'L0_ffn_W1': _L0_ffn_in['W1'], 'L0_ffn_b1': _L0_ffn_in['b1'], 'L0_ffn_W2': _L0_ffn_in['W2'], 'L0_ffn_b2': _L0_ffn_in['b2'], 'L0_ffn_Ws1': _L0_ffn_in['Ws1'], 'L0_ffn_bs1': _L0_ffn_in['bs1'], 'L0_ffn_Ws2': _L0_ffn_in['Ws2'], 'L0_ffn_bs2': _L0_ffn_in['bs2']}

def reference(x, ctx_1024, L0_attn_Win_f, L0_attn_convw_f, L0_attn_convb_f, L0_attn_Wx_f, L0_attn_Wdt_f, L0_attn_bdt_f, L0_attn_Alog_f, L0_attn_Dp_f, L0_attn_Wout_f, L0_attn_ln_g_f, L0_attn_ln_b_f, L0_attn_Win_b, L0_attn_convw_b, L0_attn_convb_b, L0_attn_Wx_b, L0_attn_Wdt_b, L0_attn_bdt_b, L0_attn_Alog_b, L0_attn_Dp_b, L0_attn_Wout_b, L0_attn_ln_g_b, L0_attn_ln_b_b, L0_attn_Wfuse, L0_attn_bfuse, L0_xattn_Wv, L0_xattn_Wk, L0_xattn_Wq, L0_xattn_Wo, L0_xattn_bo, L0_ffn_Wg, L0_ffn_W1, L0_ffn_b1, L0_ffn_W2, L0_ffn_b2, L0_ffn_Ws1, L0_ffn_bs1, L0_ffn_Ws2, L0_ffn_bs2):
    import jax
    import jax.numpy as jnp

    def _L0_attn_ref(x, Win_f, convw_f, convb_f, Wx_f, Wdt_f, bdt_f, Alog_f, Dp_f, Wout_f, ln_g_f, ln_b_f, Win_b, convw_b, convb_b, Wx_b, Wdt_b, bdt_b, Alog_b, Dp_b, Wout_b, ln_g_b, ln_b_b, Wfuse, bfuse):
        import jax, jax.numpy as jnp
        import numpy as np
        D_MODEL = 256
        D_STATE = 32
        D_CONV = 4
        EXPAND = 2
        D_INNER = EXPAND * D_MODEL
        DT_RANK = D_MODEL // 16
        BATCH = 8
        SEQ = 256

        def _silu(x):
            return x * jax.nn.sigmoid(x)

        def _layernorm(x, g, b, eps=1e-05):
            m = x.mean(-1, keepdims=True)
            v = x.var(-1, keepdims=True)
            return (x - m) / jnp.sqrt(v + eps) * g + b

        def _mamba(x, Win, convw, convb, Wx, Wdt, bdt, Alog, Dp, Wout):
            Bn, Ln, _ = x.shape
            xz = jnp.einsum('bld,ed->ble', x, Win)
            u, z = jnp.split(xz, 2, axis=-1)
            up = jnp.pad(u, ((0, 0), (D_CONV - 1, 0), (0, 0)))
            uc = convb
            for k in range(D_CONV):
                uc = uc + up[:, k:k + Ln, :] * convw[:, k]
            uc = _silu(uc)
            x_dbl = jnp.einsum('bld,ed->ble', uc, Wx)
            dt = jax.nn.softplus(jnp.einsum('blr,dr->bld', x_dbl[..., :DT_RANK], Wdt) + bdt)
            Bv = x_dbl[..., DT_RANK:DT_RANK + D_STATE]
            Cv = x_dbl[..., DT_RANK + D_STATE:]
            A = -jnp.exp(Alog)

            def step(h, ins):
                dt_t, B_t, C_t, u_t = ins
                dA = jnp.exp(dt_t[..., None] * A)
                h = dA * h + (dt_t * u_t)[..., None] * B_t[:, None, :]
                y = jnp.einsum('bdn,bn->bd', h, C_t)
                return (h, y)
            h0 = jnp.zeros((Bn, D_INNER, D_STATE), x.dtype)
            xs = (dt.transpose(1, 0, 2), Bv.transpose(1, 0, 2), Cv.transpose(1, 0, 2), uc.transpose(1, 0, 2))
            _, ys = jax.lax.scan(step, h0, xs)
            y = ys.transpose(1, 0, 2) + uc * Dp
            y = y * _silu(z)
            return jnp.einsum('bld,ed->ble', y, Wout)
        fo = _mamba(x, Win_f, convw_f, convb_f, Wx_f, Wdt_f, bdt_f, Alog_f, Dp_f, Wout_f)
        fo = _layernorm(fo, ln_g_f, ln_b_f)
        xr = x[:, ::-1, :]
        bo = _mamba(xr, Win_b, convw_b, convb_b, Wx_b, Wdt_b, bdt_b, Alog_b, Dp_b, Wout_b)
        bo = _layernorm(bo[:, ::-1, :], ln_g_b, ln_b_b)
        combined = jnp.concatenate([fo, bo], axis=-1)
        return jnp.einsum('ble,de->bld', combined, Wfuse) + bfuse

    def _L0_xattn_ref(values, keys, query, Wv, Wk, Wq, Wo, bo):
        import jax, jax.numpy as jnp
        import numpy as np
        EMBED = 256
        HEADS = 16
        HEAD_DIM = EMBED // HEADS
        N, Q, _ = query.shape
        v = (values @ Wv.T).reshape(N, -1, HEADS, HEAD_DIM)
        k = (keys @ Wk.T).reshape(N, -1, HEADS, HEAD_DIM)
        q = (query @ Wq.T).reshape(N, -1, HEADS, HEAD_DIM)
        energy = jnp.einsum('nqhd,nkhd->nhqk', q, k)
        attn = jax.nn.softmax(energy / HEAD_DIM ** 0.5, axis=-1)
        out = jnp.einsum('nhqk,nkhd->nqhd', attn, v).reshape(N, Q, EMBED)
        return out @ Wo.T + bo

    def _L0_ffn_ref(hidden_states, Wg, W1, b1, W2, b2, Ws1, bs1, Ws2, bs2):
        import jax, jax.numpy as jnp
        import numpy as np
        B, S, H = (2, 512, 256)
        F = 1024
        E = 8
        TOP_K = 2
        SHARED_SCALE = 0.1
        EPS = 1e-09

        def _moe_forward(x3, Wg, W1, b1, W2, b2, Ws1, bs1, Ws2, bs2):
            b, s, h = x3.shape
            x = x3.reshape(-1, h)
            T = x.shape[0]
            logits = x @ Wg
            probs = jax.nn.softmax(logits, axis=-1)
            vals, idx = jax.lax.top_k(probs, TOP_K)
            weights = vals / (jnp.sum(vals, axis=-1, keepdims=True) + EPS)
            cw = jnp.zeros((T, E), dtype=x.dtype).at[jnp.arange(T)[:, None], idx].set(weights)
            hpre = jnp.einsum('th,ehf->tef', x, W1) + b1
            act = jax.nn.silu(hpre)
            y = jnp.einsum('tef,efh->teh', act, W2) + b2
            out = jnp.einsum('te,teh->th', cw, y)
            shared = jax.nn.silu(x @ Ws1 + bs1) @ Ws2 + bs2
            out = out + SHARED_SCALE * shared
            return out.reshape(b, s, h)
        return _moe_forward(hidden_states, Wg, W1, b1, W2, b2, Ws1, bs1, Ws2, bs2)
    x = x + _L0_attn_ref(_layernorm(x, axis=-1), L0_attn_Win_f, L0_attn_convw_f, L0_attn_convb_f, L0_attn_Wx_f, L0_attn_Wdt_f, L0_attn_bdt_f, L0_attn_Alog_f, L0_attn_Dp_f, L0_attn_Wout_f, L0_attn_ln_g_f, L0_attn_ln_b_f, L0_attn_Win_b, L0_attn_convw_b, L0_attn_convb_b, L0_attn_Wx_b, L0_attn_Wdt_b, L0_attn_bdt_b, L0_attn_Alog_b, L0_attn_Dp_b, L0_attn_Wout_b, L0_attn_ln_g_b, L0_attn_ln_b_b, L0_attn_Wfuse, L0_attn_bfuse)
    x = x + _L0_xattn_ref(ctx_1024, ctx_1024, _layernorm(x, axis=-1), L0_xattn_Wv, L0_xattn_Wk, L0_xattn_Wq, L0_xattn_Wo, L0_xattn_bo)
    x = x + _L0_ffn_ref(_layernorm(x, axis=-1), L0_ffn_Wg, L0_ffn_W1, L0_ffn_b1, L0_ffn_W2, L0_ffn_b2, L0_ffn_Ws1, L0_ffn_bs1, L0_ffn_Ws2, L0_ffn_bs2)
    return x

_drawn_inputs = setup_inputs


def setup_inputs(seed=0):
    import zlib

    import numpy as np

    out = dict(_drawn_inputs(seed))
    spreads = {'L0_attn_convb_f': (0.0, 0.1),
     'L0_attn_Dp_f': (1.0, 0.2),
     'L0_attn_ln_g_f': (1.0, 0.2),
     'L0_attn_ln_b_f': (0.0, 0.1),
     'L0_attn_convb_b': (0.0, 0.1),
     'L0_attn_Dp_b': (1.0, 0.2),
     'L0_attn_ln_g_b': (1.0, 0.2),
     'L0_attn_ln_b_b': (0.0, 0.273),
     'L0_attn_bfuse': (0.0, 0.1),
     'L0_xattn_bo': (0.0, 0.1),
     'L0_ffn_b1': (0.0, 0.384),
     'L0_ffn_b2': (0.0, 0.1),
     'L0_ffn_bs1': (0.0, 0.8),
     'L0_ffn_bs2': (0.0, 0.8)}
    factors = {'L0_attn_Wx_f': 8.0,
     'L0_attn_Wdt_f': 46.386,
     'L0_attn_bdt_f': 8.0,
     'L0_attn_Alog_f': 64.0,
     'L0_attn_Wx_b': 8.0,
     'L0_attn_Wdt_b': 64.0,
     'L0_attn_bdt_b': 8.0,
     'L0_attn_Alog_b': 64.0,
     'L0_ffn_Ws1': 6.623,
     'L0_ffn_Ws2': 6.201}
    for name, (base, spread) in spreads.items():
        noise = np.random.default_rng([zlib.crc32(name.encode()), seed]).standard_normal(out[name].shape)
        drawn = base * np.exp(spread * noise) if base else spread * noise
        out[name] = jnp.asarray(drawn.astype(out[name].dtype))
    for name, factor in factors.items():
        out[name] = (out[name] * factor).astype(out[name].dtype)
    return out
```

```python
from contextlib import ExitStack

import numpy as np

import concourse.bass as bass
from concourse import mybir

F32 = mybir.dt.float32
BF16 = mybir.dt.bfloat16
ALU = mybir.AluOpType
ACT = mybir.ActivationFunctionType
AX = mybir.AxisListType

P = 128
B, L, D = 8, 100, 256
T = B * L
KD = D // P
DI = 2 * D
CT = DI // P
N = 32
R = D // 16
TAPS = 4
S = 361
KT = -(-S // P)
SL = S - (KT - 1) * P
H = 16
HD = D // H
HT = H // KD
F = 1024
FT = F // P
E = 8
EA = E + 1
EPS = 1e-5
SHARED = 0.1
LOG_MAX = 82.0
Q = 2
BQ = B // Q
TQ = T // Q
DIRS = 2
RING = 4
SEG = DIRS * Q
BANK = 512
UNITS = FT * Q
LAG = 3
GROUPS = H // 2
KEY_BANK = 7
CONSTS = 11 + E
MIXW, MOEW = 16 * 11, 16 * 2
LOADED = 16 * 3

V_TAP, V_CONVB, V_BDT, V_D, V_ALOG = 0, TAPS, TAPS + 1, TAPS + 2, TAPS + 3
VEC = TAPS + 3 + N


def bank_jobs():
    jobs = []
    for d in range(DIRS):
        for k in range(KD):
            for q in range(Q):
                jobs.append((("xnT", d, k, q), "v" if q else "a"))
    for d in range(DIRS):
        for c in range(CT):
            for q in range(Q):
                jobs.append((("u", d, c, q), "a"))
        for c in range(CT):
            for q in range(Q):
                jobs.append((("z", d, c, q), "a"))
    for d in range(DIRS):
        for q in range(Q):
            jobs.append((("rank", d, q), "a"))
        for w in "BC":
            for q in range(Q):
                jobs.append(((w, d, q), "v"))
        for c in range(CT):
            for q in range(Q):
                jobs.append((("dt", d, c, q), "v"))
    for d in range(DIRS):
        for h in range(B // 2):
            jobs.append((("mix", d, h), "a"))
    for d in range(DIRS):
        for k in range(KD):
            for q in range(Q):
                jobs.append((("mixT", d, k, q), "a" if q else "v"))
    for h in range(B // 2):
        jobs.append((("fuse", h), "v"))
    for k in range(KD):
        for q in range(Q):
            jobs.append((("xn2T", k, q), "a" if q else "v"))
    for m in range(KD):
        for q in range(Q):
            jobs.append((("qT", m, q), "a" if q else "v"))
    for k in range(KD):
        for q in range(Q):
            jobs.append((("xn3T", k, q), "a" if q else "v"))
    jobs.append((("logits",), "v"))
    for q in range(Q):
        jobs.append((("cwT", q), "v"))
    for e in range(EA):
        for q in range(Q):
            jobs.append((("cwb", e, q), "a" if q else "v"))
    for h in range(B // 2):
        jobs.append((("out", h), "v"))
    return jobs


JOBS = bank_jobs()
JOB = {key: n for n, (key, _) in enumerate(JOBS)}
OWNER = [owner for _, owner in JOBS]
COPIED = [OWNER[:n + 1].count(OWNER[n]) for n in range(len(JOBS))]


def decoder_layer(nc, x, ctxT, winT, wxT, wdtT, woutT, vec, ln_g, ln_b, wfuseT, bfuse,
                  wqT, wkT, wvT, woT, bo, wg, w1, b1, w2, b2, out):
    stack = ExitStack()
    with stack:
        def sb(name, shape, dt=F32, scope=stack):
            return scope.enter_context(nc.sbuf_tensor(name, shape, dt))

        def sem(name):
            return stack.enter_context(nc.semaphore(name))

        ps = stack.enter_context(nc.psum_tensor("ps", [P, 8, BANK], F32))

        ident = sb("ident", [P, P])
        flip = sb("flip", [L, L])
        row_sel = sb("row_sel", [96, N, P], BF16)
        head_mask = sb("head_mask", [P, HT])
        prefer = sb("prefer", [L, E])
        x_tok = sb("x_tok", [L, B, D])
        xn_tok = sb("xn_tok", [L, B, D])
        stats = sb("stats", [L, DIRS * B, 6])
        moments = sb("moments", [L, DIRS * B, 2])
        var_eps = sb("var_eps", [L, DIRS * B])
        std = sb("std", [L, DIRS * B])
        rstd = sb("rstd", [L, DIRS * B])
        xT = sb("xT", [P, 4, T])
        wx_sb = [sb(f"wx{d}", [P, CT, R + 2 * N]) for d in range(DIRS)]
        wdt_sb = [sb(f"wdt{d}", [R, DI]) for d in range(DIRS)]
        wout_sb = [sb(f"wout{d}", [P, CT, D]) for d in range(DIRS)]
        wfuse_sb = sb("wfuse_sb", [P, DIRS * KD, D])
        vec_sb = [sb(f"vec{d}", [P, CT, VEC]) for d in range(DIRS)]
        neg_a = [sb(f"neg_a{d}", [P, CT * N]) for d in range(DIRS)]
        diag_d = [sb(f"diag_d{d}", [P, CT, P]) for d in range(DIRS)]
        lng_sb = sb("lng_sb", [P, DIRS * KD])
        lnb_sb = sb("lnb_sb", [P, DIRS * KD])
        bias_tok = sb("bias_tok", [L, 2, D])

        mixer = ExitStack()
        dt_sb = [sb(f"dt{d}", [P, CT, T], scope=mixer) for d in range(DIRS)]
        dtu = [sb(f"dtu{d}", [P, CT, T], scope=mixer) for d in range(DIRS)]
        u_sb = [sb(f"u{d}", [P, CT, T], scope=mixer) for d in range(DIRS)]
        gate = [sb(f"gate{d}", [P, CT, T], scope=mixer) for d in range(DIRS)]
        b_parts = [sb(f"b_parts{d}", [96, T], BF16, scope=mixer) for d in range(DIRS)]
        c_parts = [sb(f"c_parts{d}", [96, T], BF16, scope=mixer) for d in range(DIRS)]
        parts = {"B": b_parts, "C": c_parts}
        early = ExitStack()
        win_sb = [sb(f"win{d}", [P, KD, 2 * DI], scope=early) for d in range(DIRS)]
        u_pad = [sb(f"u_pad{r}", [P, B, L + TAPS - 1], scope=early) for r in range(2)]
        early.close()
        softp = ExitStack()
        pre = [sb(f"pre{r}", [P, T], scope=softp) for r in range(2)]
        ex = [sb(f"ex{r}", [P, T], scope=softp) for r in range(2)]
        lg = [sb(f"lg{r}", [P, T], scope=softp) for r in range(2)]
        part_mid = sb("part_mid", [N, T], BF16, scope=softp)
        softp.close()
        rank_sb = xT[0:R, 0:2, :]
        rows_f = xT[0:N, 2, :]
        rest_f = xT[0:N, 3, :]
        states = [sb(f"states{r}", [P, CT * TQ], scope=mixer) for r in range(RING)]
        c_row = [sb(f"c_row{r}", [P, TQ], scope=mixer) for r in range(2)]
        mixer.close()

        late = ExitStack()
        mix_tok = [sb(f"mix_tok{d}", [L, B, D], scope=late) for d in range(DIRS)]
        w1_sb = [sb(f"w1s_{r}", [P, KD, F], scope=late) for r in range(2)]
        w2_sb = [sb(f"w2s_{r}", [P, FT, D], scope=late) for r in range(2)]
        b1_sb = [sb(f"b1_{r}", [P, FT], scope=late) for r in range(2)]
        attn = ExitStack()
        xn2T = sb("xn2T", [P, KD, T], scope=attn)
        qT = sb("qT", [P, KD, T], scope=attn)
        q_blk = [sb(f"q_blk{r}", [P, KD, HT, L], scope=attn) for r in range(2)]
        ctx_sb = [sb(f"ctx{r}", [P, KD, S], scope=attn) for r in range(2)]
        wq_sb, wk_sb, wv_sb, wo_sb = (sb(n, [P, KD, D], scope=attn) for n in ("wq_sb", "wk_sb", "wv_sb", "wo_sb"))
        kT = [sb(f"kT{r}", [P, KD, S], scope=attn) for r in range(2)]
        v_sb = [sb(f"v{r}", [P, KT, D], scope=attn) for r in range(2)]
        probs = [sb(f"probs{r}", [L, 2, KT * P], scope=attn) for r in range(2)]
        probsT = [[sb(f"probsT{r}{j}", [P, KT * L], scope=attn) for j in range(2)] for r in range(2)]
        neg_max, shift, mass, inv_mass = (sb(n, [L, 2, H], scope=attn) for n in ("neg_max", "shift", "mass", "inv_mass"))
        heads_tok = sb("heads_tok", [L, D], scope=attn)
        headsT = sb("headsT", [P, KD, L], scope=attn)
        attn.close()
        moe = ExitStack()
        xn3T = sb("xn3T", [P, KD, T], scope=moe)
        expert_sel = sb("expert_sel", [EA, EA, P], scope=moe)
        wg_sb = sb("wg_sb", [P, KD, E], scope=moe)
        b2_sb = sb("b2_sb", [EA, D], scope=moe)
        cw_b = sb("cw_b", [P, EA * T], scope=moe)
        cw_tok = sb("cw_tok", [L, B, EA], scope=moe)
        cwT = sb("cwT", [EA, T], scope=moe)
        route = {n: sb(f"route_{n}", [L, B, E], scope=moe)
                 for n in ("shifted", "exp", "prob", "tie", "first", "rest", "second", "both", "kept")}
        per_tok = {n: sb(f"tok_{n}", [L, B, 1], scope=moe)
                   for n in ("max", "sum", "inv", "top1", "pick1", "top2", "pick2", "den", "inv_den")}
        hidden = [sb(f"hidden{r}", [P, TQ], scope=moe) for r in range(8)]
        yT = sb("yT", [P, KD, T], scope=moe)
        out_tok = sb("out_tok", [L, B, D], scope=moe)
        moe.close()
        late.close()
        HRING = len(hidden)

        consts = sem("consts")
        x_in = sem("x_in")
        win_in = [sem(f"win_in{d}") for d in range(DIRS)]
        vec_in = sem("vec_in")
        mixw_in = sem("mixw_in")
        attnw_in = sem("attnw_in")
        ctx_in = [sem(f"ctx_in{r}") for r in range(2)]
        moew_in = sem("moew_in")
        w_in = [sem(f"w_in{r}") for r in range(2)]
        out_stored = sem("out_stored")
        job_done = sem("job_done")
        copied = {"a": sem("copied_by_act"), "v": sem("copied_by_dve")}
        moments_ready = sem("moments_ready")
        std_ready = sem("std_ready")
        xn_ready = sem("xn_ready")
        dve_step = sem("dve_step")
        act_step = sem("act_step")
        bias_added = sem("bias_added")
        pad_zeroed = sem("pad_zeroed")
        conv_ready = sem("conv_ready")
        u_ready = sem("u_ready")
        log_ready = sem("log_ready")
        dt_ready = sem("dt_ready")
        dtu_ready = sem("dtu_ready")
        log_a_ready = sem("log_a_ready")
        rate_ready = sem("rate_ready")
        neg_a_ready = sem("neg_a_ready")
        diag_ready = sem("diag_ready")
        parts_ready = sem("parts_ready")
        decay_zeroed = sem("decay_zeroed")
        b_bank_ready = sem("b_bank_ready")
        c_bank_ready = sem("c_bank_ready")
        c_row_ready = sem("c_row_ready")
        decay_ready = sem("decay_ready")
        inflow_ready = sem("inflow_ready")
        scan_done = sem("scan_done")
        product_ready = sem("product_ready")
        y_summed = sem("y_summed")
        y_gated = sem("y_gated")
        probs_zeroed = sem("probs_zeroed")
        q_blk_ready = sem("q_blk_ready")
        k_done = sem("k_done")
        v_done = sem("v_done")
        k_copied = sem("k_copied")
        v_copied = sem("v_copied")
        scores_ready = sem("scores_ready")
        max_ready = sem("max_ready")
        shift_ready = sem("shift_ready")
        probs_ready = sem("probs_ready")
        probsT_ready = sem("probsT_ready")
        probsT_copied = [sem("probsT_copied_by_dve"), sem("probsT_copied_by_act")]
        pv_done = sem("pv_done")
        inv_mass_ready = sem("inv_mass_ready")
        heads_ready = sem("heads_ready")
        headsT_done = sem("headsT_done")
        headsT_copied = sem("headsT_copied")
        wo_done = sem("wo_done")
        x2_ready = sem("x2_ready")
        sel_ready = sem("sel_ready")
        shifted_ready = sem("shifted_ready")
        exp_ready = sem("exp_ready")
        cw_ready = sem("cw_ready")
        hid_ready = sem("hid_ready")
        silu_done = sem("silu_done")
        hid_scaled = sem("hid_scaled")
        hid_used = sem("hid_used")
        yT_ready = sem("yT_ready")
        out_ready = sem("out_ready")

        def bank(key):
            return ps[:, JOB[key] % 8, :]

        def job_bank_free(eng, key):
            before = JOB[key] - 8
            if before >= 0:
                eng.wait_ge(copied[OWNER[before]], COPIED[before])

        def job_result(eng, key):
            eng.wait_ge(job_done, JOB[key] + 1)

        def job_copied(eng, key):
            eng.wait_ge(copied[OWNER[JOB[key]]], COPIED[JOB[key]])

        def chunk(q):
            return slice(q * TQ, (q + 1) * TQ)

        def pair(h):
            return slice(2 * h, 2 * h + 2)

        def tile(k):
            return slice(k * P, (k + 1) * P)

        def seqs(ap):
            return ap.rearrange("p (b t) -> p b t", t=L)

        def spread(per_token, width):
            return per_token.broadcast_to([L, B, width])

        block = stack.enter_context(nc.Block())

        @block.sync
        def _(sp):
            sp.dma_start(x_tok[:], x.rearrange("b l d -> l b d")).then_inc(x_in, 16)
            for d in range(DIRS):
                sp.dma_start(win_sb[d][:], winT[d].rearrange("(k p) e -> p k e", p=P)).then_inc(win_in[d], 16)
                sp.dma_start(vec_sb[d][:], vec[d]).then_inc(vec_in, 16)
            for d in range(DIRS):
                sp.dma_start(wx_sb[d][:], wxT[d].rearrange("(c p) e -> p c e", p=P)).then_inc(mixw_in, 16)
                sp.dma_start(wdt_sb[d][:], wdtT[d]).then_inc(mixw_in, 16)
                sp.dma_start(wout_sb[d][:], woutT[d].rearrange("(c p) e -> p c e", p=P)).then_inc(mixw_in, 16)
            sp.dma_start(wfuse_sb[:], wfuseT.rearrange("(k p) e -> p k e", p=P)).then_inc(mixw_in, 16)
            sp.dma_start(lng_sb[:], ln_g).then_inc(mixw_in, 16)
            sp.dma_start(lnb_sb[:], ln_b).then_inc(mixw_in, 16)
            sp.dma_start(bias_tok[:, 0, :], bfuse.partition_broadcast(L)).then_inc(mixw_in, 16)
            sp.dma_start(bias_tok[:, 1, :], bo.partition_broadcast(L)).then_inc(mixw_in, 16)
            job_result(sp, ("mix", DIRS - 1, B // 2 - 1))
            for w_dram, w_sbuf in ((wqT, wq_sb), (wkT, wk_sb), (wvT, wv_sb), (woT, wo_sb)):
                sp.dma_start(w_sbuf[:], w_dram.rearrange("(k p) e -> p k e", p=P)).then_inc(attnw_in, 16)
            for b in range(2):
                sp.dma_start(ctx_sb[b][:], ctxT[b].rearrange("(k p) s -> p k s", p=P)).then_inc(ctx_in[b], 16)

            def load_expert(e, r):
                sp.dma_start(w1_sb[r][:], w1[e].rearrange("(k p) f -> p k f", p=P)).then_inc(w_in[r], 16)
                sp.dma_start(w2_sb[r][:], w2[e].rearrange("(f p) d -> p f d", p=P)).then_inc(w_in[r], 16)
                sp.dma_start(b1_sb[r][:], b1[e]).then_inc(w_in[r], 16)

            load_expert(0, 0)
            load_expert(1, 1)
            with sp.Fori(1, B // 2) as i:
                for r in range(2):
                    sp.wait_ge(v_done, 4 * i + (2 * r - 2))
                    sp.dma_start(ctx_sb[r][:], ctxT[bass.ds(2 * i + r, 1)].rearrange("b (k p) s -> p (b k) s", p=P)
                                 ).then_inc(ctx_in[r], 16)
            sp.wait_ge(x2_ready, B)
            sp.dma_start(wg_sb[:], wg.rearrange("(k p) e -> p k e", p=P)).then_inc(moew_in, 16)
            sp.dma_start(b2_sb[:], b2).then_inc(moew_in, 16)
            with sp.Fori(1, E // 2) as i:
                for r in range(2):
                    sp.wait_ge(hid_used, UNITS * 2 * i + UNITS * (r - 1))
                    sp.dma_start(w1_sb[r][:], w1[bass.ds(2 * i + r, 1)].rearrange("e (k p) f -> p (e k) f", p=P)
                                 ).then_inc(w_in[r], 16)
                    sp.dma_start(w2_sb[r][:], w2[bass.ds(2 * i + r, 1)].rearrange("e (f p) d -> p (e f) d", p=P)
                                 ).then_inc(w_in[r], 16)
                    sp.dma_start(b1_sb[r][:], b1[bass.ds(2 * i + r, 1)].rearrange("e p f -> p (e f)")
                                 ).then_inc(w_in[r], 16)
            sp.wait_ge(hid_used, UNITS * (E - 1))
            load_expert(E, 0)
            for h in range(B // 2):
                sp.wait_ge(out_ready, h + 1)
                sp.dma_start(out[pair(h)].rearrange("b l d -> l b d"), out_tok[:, pair(h), :]).then_inc(out_stored, 16)
            sp.wait_ge(out_stored, 16 * (B // 2))

        @block.gpsimd
        def _(pool):
            made = 0

            def fill(t, value):
                nonlocal made
                nc.gpsimd.memset(t, value).then_inc(consts, 1)
                made += 1
                pool.wait_ge(consts, made)

            def where(t, compare, value, base, pattern, step):
                nonlocal made
                nc.gpsimd.affine_select(out=t, in_=t, compare_op=compare, fill=value, base=base, pattern=pattern,
                                        channel_multiplier=step).then_inc(consts, 1)
                made += 1
                pool.wait_ge(consts, made)

            fill(ident[:], 0.0)
            where(ident[:], ALU.not_equal, 1.0, 0, [[-1, P]], 1)
            fill(flip[:], 0.0)
            where(flip[:], ALU.not_equal, 1.0, 1 - L, [[1, L]], 1)
            fill(row_sel[:], 0.0)
            for part in range(3):
                where(row_sel[:], ALU.not_equal, 1.0, -part * N, [[-1, N], [0, P]], 1)
            fill(head_mask[:], 1.0)
            where(head_mask[:], ALU.is_ge, 0.0, 0, [[-HD, HT]], 1)
            where(head_mask[:], ALU.is_ge, 0.0, HD - 1, [[HD, HT]], -1)
            for e in range(E):
                fill(prefer[:, e:e + 1], float(E - e))
            assert made == CONSTS
            pool.wait_ge(mixw_in, MIXW)
            pool.wait_ge(xn_ready, B)
            nc.gpsimd.tensor_tensor(x_tok[:], x_tok[:], bias_tok[:, 0:1, :].broadcast_to([L, B, D]), ALU.add
                                    ).then_inc(bias_added, 1)
            for d in range(DIRS):
                for c in range(CT):
                    pool.wait_ge(dt_ready, d * CT + c + 1)
                    pool.wait_ge(u_ready, d * CT + c + 1)
                    nc.gpsimd.tensor_tensor(dtu[d][:, c, :], dt_sb[d][:, c, :], u_sb[d][:, c, :], ALU.mult
                                            ).then_inc(dtu_ready, 1)

            def state_times_c(n, r):
                pool.wait_ge(scan_done, CT * n + CT)
                pool.wait_ge(c_row_ready, n + 1)
                st = states[r][:].rearrange("p (c t) -> p c t", c=CT)
                nc.gpsimd.tensor_tensor(st, st, c_row[r % 2][:].unsqueeze(1).broadcast_to([P, CT, TQ]),
                                        ALU.mult).then_inc(product_ready, 1)

            for s in range(SEG):
                with pool.Fori(0, N // RING) as i:
                    for r in range(RING):
                        state_times_c(i * RING + (s * N + r), r)
            pool.wait_ge(xn_ready, (1 + DIRS + 1) * B)
            nc.gpsimd.tensor_tensor(x_tok[:], x_tok[:], bias_tok[:, 1:2, :].broadcast_to([L, B, D]), ALU.add
                                    ).then_inc(bias_added, 1)
            for r in range(2):
                nc.gpsimd.memset(probs[r][:, :, S:], 0.0).then_inc(probs_zeroed, 1)
            def spread_queries(b, r):
                for m in range(KD):
                    for q in range(Q):
                        job_copied(pool, ("qT", m, q))
                    nc.gpsimd.tensor_tensor(
                        q_blk[r][:, m], qT[:, m, bass.ds(b * L, L)].unsqueeze(1).broadcast_to([P, HT, L]),
                        head_mask[:].unsqueeze(2).broadcast_to([P, HT, L]), ALU.mult).then_inc(q_blk_ready, 1)

            for b in range(2):
                spread_queries(b, b)
            with pool.Fori(1, B // 2) as i:
                for r in range(2):
                    pool.wait_ge(scores_ready, 2 * GROUPS * i + GROUPS * (r - 1))
                    spread_queries(2 * i + r, r)
            pool.wait_ge(x2_ready, B)
            nc.gpsimd.memset(expert_sel[:], 0.0).then_inc(sel_ready, 1)
            pool.wait_ge(sel_ready, 1)
            nc.gpsimd.affine_select(out=expert_sel[:], in_=expert_sel[:], compare_op=ALU.not_equal, fill=1.0, base=0,
                                    pattern=[[-1, EA], [0, P]], channel_multiplier=1).then_inc(sel_ready, 1)

        @block.scalar
        def _(act):
            def root(norm, count):
                act.wait_ge(moments_ready, norm)
                nc.scalar.activation(std[:, 0:count], var_eps[:, 0:count], ACT.Sqrt).then_inc(std_ready, 1)

            def copy_out(key, dst, src, func=ACT.Copy, **how):
                job_result(act, key)
                nc.scalar.activation(dst, src, func, **how).then_inc(copied["a"], 1)

            root(1, B)
            for d in range(DIRS):
                for k in range(KD):
                    copy_out(("xnT", d, k, 0), xT[:, d * KD + k, chunk(0)], bank(("xnT", d, k, 0))[:, 0:TQ])
            act.wait_ge(pad_zeroed, 2)

            def copy_u(d, c):
                if d * CT + c >= 2:
                    act.wait_ge(conv_ready, d * CT + c - 1)
                for q in range(Q):
                    copy_out(("u", d, c, q), u_pad[c % 2][:, q * BQ:(q + 1) * BQ, TAPS - 1:],
                             seqs(bank(("u", d, c, q))[:, 0:TQ]))

            def silu_u(d, c):
                act.wait_ge(conv_ready, d * CT + c + 1)
                nc.scalar.activation(u_sb[d][:, c, :], u_sb[d][:, c, :], ACT.Silu).then_inc(u_ready, 1)

            for d in range(DIRS):
                copy_u(d, 0)
                for c in range(1, CT):
                    copy_u(d, c)
                    silu_u(d, c - 1)
                for c in range(CT):
                    for q in range(Q):
                        copy_out(("z", d, c, q), gate[d][:, c, chunk(q)], bank(("z", d, c, q))[:, 0:TQ], ACT.Silu)
                silu_u(d, CT - 1)
            nc.scalar.preload_act_table_set("natural_log_exp_and_others")
            for d in range(DIRS):
                act.wait_ge(log_a_ready, d + 1)
                nc.scalar.activation(neg_a[d][:], neg_a[d][:], ACT.Exp).then_inc(rate_ready, 1)
            steps = 0
            for d in range(DIRS):
                for q in range(Q):
                    copy_out(("rank", d, q), rank_sb[:, d, chunk(q)], bank(("rank", d, q))[0:R, 0:TQ])
                for c in range(CT):
                    g = d * CT + c
                    job_copied(act, ("dt", d, c, Q - 1))
                    if g >= 2:
                        act.wait_ge(dt_ready, g - 1)
                    nc.scalar.activation(ex[g % 2][:], pre[g % 2][:], ACT.Abs).then_inc(act_step, 1)
                    act.wait_ge(act_step, steps + 1)
                    nc.scalar.activation(ex[g % 2][:], ex[g % 2][:], ACT.Exp, scale=-1.0).then_inc(act_step, 1)
                    act.wait_ge(act_step, steps + 2)
                    steps += 2
                    nc.scalar.activation(lg[g % 2][:], ex[g % 2][:], ACT.Ln, bias=1.0).then_inc(log_ready, 1)

            act.wait_ge(decay_zeroed, 1)

            def decays(d, q, first, n, r):
                act.wait_ge(c_bank_ready, n + 1)
                if not (isinstance(n, int) and n < 2):
                    act.wait_ge(product_ready, n - 1)
                nc.scalar.activation(c_row[r % 2][:], ps[:, 7, 0:TQ], ACT.Copy).then_inc(c_row_ready, 1)
                for c in range(CT):
                    act.wait_ge(neg_a_ready, DIRS)
                    if not (isinstance(n, int) and CT * n + c < 2):
                        act.wait_ge(scan_done, CT * n + (c - 1))
                    nc.scalar.activation(
                        seqs(ps[:, 4 + c % 2, 0:TQ])[:, :, 1:], seqs(dt_sb[d][:, c, chunk(q)])[:, :, 1:],
                        ACT.Exp, scale=neg_a[d][:, bass.ds(n + (c * N - first), 1)]).then_inc(decay_ready, 1)

            for r in range(RING):
                decays(0, 0, 0, r, r)
            for s in range(SEG):
                with act.Fori(s == 0, N // RING) as i:
                    for r in range(RING):
                        decays(*divmod(s, Q), s * N, i * RING + (s * N + r), r)

            for d in range(DIRS):
                for h in range(B // 2):
                    copy_out(("mix", d, h), mix_tok[d][:, pair(h), :].rearrange("l b d -> l (b d)"),
                             bank(("mix", d, h))[0:L, :])
            root(2, DIRS * B)
            for d in range(DIRS):
                for k in range(KD):
                    j = d * KD + k
                    copy_out(("mixT", d, k, 1), xT[:, j, chunk(1)], bank(("mixT", d, k, 1))[:, 0:TQ], ACT.Identity,
                             scale=lng_sb[:, j:j + 1], bias=lnb_sb[:, j:j + 1])
            root(3, B)
            for k in range(KD):
                copy_out(("xn2T", k, 1), xn2T[:, k, chunk(1)], bank(("xn2T", k, 1))[:, 0:TQ])
            for m in range(KD):
                copy_out(("qT", m, 1), qT[:, m, chunk(1)], bank(("qT", m, 1))[:, 0:TQ])
            act.wait_ge(probs_zeroed, 2)

            def copy_keys(b, r, m):
                act.wait_ge(k_done, 2 * b + (m + 1))
                nc.scalar.activation(kT[r][:, m, :], ps[:, KEY_BANK, 0:S], ACT.Copy).then_inc(k_copied, 1)

            def exponentials(b, r, g):
                act.wait_ge(shift_ready, GROUPS * b + (g + 1))
                if not isinstance(b, int) or GROUPS * b + g >= 2:
                    act.wait_ge(probsT_ready, GROUPS * b + (g - 1))
                for j in range(2):
                    h = 2 * g + j
                    nc.scalar.activation(probs[g % 2][:, j, 0:S], ps[0:L, g % 2 * 2 + j, 0:S], ACT.Exp,
                                         bias=shift[:, r, h:h + 1], scale=HD ** -0.5,
                                         accum_out=mass[:, r, h:h + 1]).then_inc(probs_ready, 1)

            def copy_probs(b, g):
                act.wait_ge(probsT_ready, GROUPS * b + (g + 1))
                if not isinstance(b, int) or GROUPS * b + g >= 2:
                    act.wait_ge(pv_done, GROUPS * b + (g - 1))
                nc.scalar.activation(probsT[g % 2][1][:], ps[:, 5, 0:KT * L], ACT.Copy).then_inc(probsT_copied[1], 1)

            def attend(b, r, last=False):
                for g in range(2, GROUPS):
                    copy_probs(b, g)
                    if g + 2 < GROUPS:
                        exponentials(b, r, g + 2)
                    elif not last:
                        exponentials(b + 1, 1 - r, g + 2 - GROUPS)
                    if g - 2 in range(KD) and not last:
                        copy_keys(b + 1, 1 - r, g - 2)
                for g in range(0 if last else 2):
                    copy_probs(b + 1, g)
                    exponentials(b + 1, 1 - r, g + 2)

            for m in range(KD):
                copy_keys(0, 0, m)
            exponentials(0, 0, 0)
            exponentials(0, 0, 1)
            for g in range(2):
                copy_probs(0, g)
                exponentials(0, 0, g + 2)
            with act.Fori(0, B // 2 - 1) as i:
                for r in range(2):
                    attend(2 * i + r, r)
            attend(B - 2, 0)
            attend(B - 1, 1, last=True)
            root(4, B)
            for k in range(KD):
                copy_out(("xn3T", k, 1), xn3T[:, k, chunk(1)], bank(("xn3T", k, 1))[:, 0:TQ])
            act.wait_ge(shifted_ready, 1)
            nc.scalar.activation(route["exp"][:], route["shifted"][:], ACT.Exp).then_inc(exp_ready, 1)
            for e in range(EA):
                copy_out(("cwb", e, 1), cw_b[:, e * T + TQ:(e + 1) * T], bank(("cwb", e, 1))[:, 0:TQ])

            def silu_expert(e, r, loads, start):
                act.wait_ge(w_in[r], LOADED * loads)
                for u in range(UNITS):
                    ft, q = divmod(u, Q)
                    act.wait_ge(hid_ready, UNITS * e + (u + 1))
                    if start + u >= HRING:
                        act.wait_ge(hid_used, UNITS * e + (u - HRING + 1))
                    nc.scalar.activation(hidden[u % HRING][:], ps[:, u % 4, 0:TQ], ACT.Silu,
                                         bias=b1_sb[r][:, ft:ft + 1]).then_inc(silu_done, 1)

            with act.Fori(0, E // 2) as i:
                for r in range(2):
                    silu_expert(2 * i + r, r, i + 1, r * UNITS)
            silu_expert(E, 0, E // 2 + 1, 0)
            act.wait_ge(hid_used, UNITS * EA)
            for q in range(Q):
                nc.scalar.activation(yT[:, 1, chunk(q)], ps[:, 4 + 2 * q + 1, 0:TQ], ACT.Copy).then_inc(yT_ready, 1)

        @block.tensor
        def _(pe):
            def turned(key, src, how):
                job_bank_free(pe, key)
                q = key[-1]
                for b in range(BQ):
                    mm = nc.tensor.matmul(bank(key)[:, b * L:(b + 1) * L], src(q * BQ + b), how, start=True, stop=True)
                mm.then_inc(job_done, 1)

            def product(key, rows, cols, pairs):
                job_bank_free(pe, key)
                for n, (lhsT, rhs) in enumerate(pairs):
                    mm = nc.tensor.matmul(bank(key)[0:rows, 0:cols], lhsT, rhs, start=(n == 0),
                                          stop=(n == len(pairs) - 1))
                mm.then_inc(job_done, 1)

            def pair_product(key, pairs):
                job_bank_free(pe, key)
                for j in range(2):
                    b = 2 * key[-1] + j
                    for n, (lhsT, rhs) in enumerate(pairs):
                        mm = nc.tensor.matmul(bank(key)[0:L, j * D:(j + 1) * D], lhsT[:, b * L:(b + 1) * L], rhs,
                                              start=(n == 0), stop=(n == len(pairs) - 1))
                mm.then_inc(job_done, 1)

            order = (ident[0:L, 0:L], flip[:])
            pe.wait_ge(consts, CONSTS)
            pe.wait_ge(xn_ready, B)
            for d in range(DIRS):
                for k in range(KD):
                    for q in range(Q):
                        turned(("xnT", d, k, q), lambda b: xn_tok[:, b, tile(k)], order[d])
            for d in range(DIRS):
                pe.wait_ge(win_in[d], 16)
                for k in range(KD):
                    for q in range(Q):
                        job_copied(pe, ("xnT", d, k, q))
                for half, name in enumerate("uz"):
                    for c in range(CT):
                        for q in range(Q):
                            product((name, d, c, q), P, TQ, [
                                (win_sb[d][:, k, half * DI + c * P:half * DI + (c + 1) * P],
                                 xT[:, d * KD + k, chunk(q)]) for k in range(KD)])
            pe.wait_ge(mixw_in, MIXW)
            for d in range(DIRS):
                pe.wait_ge(u_ready, (d + 1) * CT)
                for name, at, rows in (("rank", 0, R), ("B", R, N), ("C", R + N, N)):
                    for q in range(Q):
                        product((name, d, q), rows, TQ, [
                            (wx_sb[d][:, c, at:at + rows], u_sb[d][:, c, chunk(q)]) for c in range(CT)])
                for q in range(Q):
                    job_copied(pe, ("rank", d, q))
                for c in range(CT):
                    for q in range(Q):
                        product(("dt", d, c, q), P, TQ, [(wdt_sb[d][:, tile(c)], rank_sb[:, d, chunk(q)])])

            for key, _ in JOBS[JOB[("dt", DIRS - 1, CT - 1, Q - 1)] - 7:][:8]:
                job_copied(pe, key)
            pe.wait_ge(parts_ready, 2 * DIRS)
            pe.wait_ge(diag_ready, DIRS)

            def rows(d, q, first, n):
                if not (isinstance(n, int) and n < 1):
                    pe.wait_ge(inflow_ready, n)
                nc.tensor.matmul(ps[:, 6, 0:TQ], row_sel[:, bass.ds(n - first, 1), :].rearrange("p n m -> p (n m)"),
                                 b_parts[d][:, chunk(q)], start=True, stop=True).then_inc(b_bank_ready, 1)
                if not (isinstance(n, int) and n < 1):
                    pe.wait_ge(c_row_ready, n)
                nc.tensor.matmul(ps[:, 7, 0:TQ], row_sel[:, bass.ds(n - first, 1), :].rearrange("p n m -> p (n m)"),
                                 c_parts[d][:, chunk(q)], start=True, stop=True).then_inc(c_bank_ready, 1)

            def sum_state(n, r, last=False):
                pe.wait_ge(product_ready, n + 1)
                for c in range(CT):
                    mm = nc.tensor.matmul(ps[:, c, 0:TQ], ident[:], states[r][:, c * TQ:(c + 1) * TQ],
                                          start=False, stop=last, skip_group_check=True)
                mm.then_inc(y_summed, 1)

            for s in range(SEG):
                d, q = divmod(s, Q)
                rows(d, q, s * N, s * N)
                rows(d, q, s * N, s * N + 1)
                if s:
                    pe.wait_ge(y_gated, CT * s)
                for c in range(CT):
                    nc.tensor.matmul(ps[:, c, 0:TQ], diag_d[d][:, c, :], u_sb[d][:, c, chunk(q)], start=True,
                                     stop=False, skip_group_check=True)
                with pe.Fori(0, N // RING - 1) as i:
                    for r in range(RING):
                        rows(d, q, s * N, i * RING + (s * N + r + 2))
                        sum_state(i * RING + (s * N + r), r)
                for r in range(RING):
                    n = s * N + N - RING + r
                    if r + 2 < RING:
                        rows(d, q, s * N, n + 2)
                    sum_state(n, r, r == RING - 1)

            pe.wait_ge(y_gated, CT * SEG)
            for d in range(DIRS):
                for h in range(B // 2):
                    pair_product(("mix", d, h), [(u_sb[d][:, c, :], wout_sb[d][:, c, :]) for c in range(CT)])
            pe.wait_ge(xn_ready, (1 + DIRS) * B)
            for d in range(DIRS):
                for k in range(KD):
                    for q in range(Q):
                        turned(("mixT", d, k, q), lambda b: mix_tok[d][:, b, tile(k)], order[d])
            for d in range(DIRS):
                for k in range(KD):
                    for q in range(Q):
                        job_copied(pe, ("mixT", d, k, q))
            for h in range(B // 2):
                pair_product(("fuse", h), [(xT[:, j, :], wfuse_sb[:, j, :]) for j in range(DIRS * KD)])
            pe.wait_ge(xn_ready, (1 + DIRS + 1) * B)
            for k in range(KD):
                for q in range(Q):
                    turned(("xn2T", k, q), lambda b: xn_tok[:, b, tile(k)], order[0])
            pe.wait_ge(attnw_in, 16 * 4)
            for k in range(KD):
                for q in range(Q):
                    job_copied(pe, ("xn2T", k, q))
            for m in range(KD):
                for q in range(Q):
                    product(("qT", m, q), P, TQ, [(wq_sb[:, k, tile(m)], xn2T[:, k, chunk(q)]) for k in range(KD)])
            for m in range(KD):
                for q in range(Q):
                    job_copied(pe, ("qT", m, q))

            def keys(b, r, loads, m):
                if m == 0:
                    pe.wait_ge(ctx_in[r], 16 * loads)
                    if not isinstance(b, int) or b > 0:
                        pe.wait_ge(x2_ready, b - 1)
                else:
                    pe.wait_ge(k_copied, 2 * b + m)
                for k in range(KD):
                    mm = nc.tensor.matmul(ps[:, KEY_BANK, 0:S], wk_sb[:, k, tile(m)], ctx_sb[r][:, k, :],
                                          start=(k == 0), stop=(k == KD - 1))
                mm.then_inc(k_done, 1)

            def values(b, r, part):
                if part == 0:
                    pe.wait_ge(k_copied, 2 * b + KD)
                else:
                    pe.wait_ge(v_copied, 2 * b + part)
                for kt in ((0, 1), (2,))[part]:
                    size = P if kt < KT - 1 else SL
                    for k in range(KD):
                        mm = nc.tensor.matmul(ps[0:size, KEY_BANK, kt % 2 * D:(kt % 2 + 1) * D],
                                              ctx_sb[r][:, k, kt * P:kt * P + size], wv_sb[:, k, :],
                                              start=(k == 0), stop=(k == KD - 1))
                mm.then_inc(v_done, 1)

            def scores(b, r, g):
                m = 2 * g // HT
                pe.wait_ge(q_blk_ready, KD * b + (m + 1))
                if g % (GROUPS // KD) == 0:
                    pe.wait_ge(k_copied, 2 * b + (m + 1))
                if not isinstance(b, int) or GROUPS * b + g >= 2:
                    pe.wait_ge(probs_ready, 2 * GROUPS * b + (2 * g - 2))
                for j in range(2):
                    mm = nc.tensor.matmul(ps[0:L, g % 2 * 2 + j, 0:S], q_blk[r][:, m, (2 * g + j) % HT, :],
                                          kT[r][:, m, :], start=True, stop=True)
                mm.then_inc(scores_ready, 1)

            def turn_probs(b, g):
                pe.wait_ge(probs_ready, 2 * GROUPS * b + (2 * g + 2))
                if not isinstance(b, int) or GROUPS * b + g >= 1:
                    for by in probsT_copied:
                        pe.wait_ge(by, GROUPS * b + g)
                for j in range(2):
                    for kt in range(KT):
                        mm = nc.tensor.transpose(ps[:, 4 + j, kt * L:(kt + 1) * L], probs[g % 2][:, j, tile(kt)],
                                                 ident[0:L, 0:L])
                mm.then_inc(probsT_ready, 1)

            def weigh_values(b, r, g):
                for by in probsT_copied:
                    pe.wait_ge(by, GROUPS * b + (g + 1))
                if g == 0:
                    pe.wait_ge(v_copied, 2 * b + 2)
                    if not isinstance(b, int) or b > 0:
                        pe.wait_ge(heads_ready, b)
                for j in range(2):
                    h = 2 * g + j
                    for kt in range(KT):
                        size = P if kt < KT - 1 else SL
                        mm = nc.tensor.matmul(ps[0:L, 6, h * HD:(h + 1) * HD],
                                              probsT[g % 2][j][0:size, kt * L:(kt + 1) * L],
                                              v_sb[r][0:size, kt, h * HD:(h + 1) * HD],
                                              start=(kt == 0), stop=(kt == KT - 1))
                mm.then_inc(pv_done, 1)

            def turn_heads(b):
                pe.wait_ge(heads_ready, b + 1)
                for m in range(KD):
                    mm = nc.tensor.transpose(ps[:, KEY_BANK, m * L:(m + 1) * L], heads_tok[:, tile(m)],
                                             ident[0:L, 0:L])
                mm.then_inc(headsT_done, 1)

            def project_heads(b):
                pe.wait_ge(headsT_copied, b + 1)
                for m in range(KD):
                    mm = nc.tensor.matmul(ps[0:L, KEY_BANK, 0:D], headsT[:, m, :], wo_sb[:, m, :], start=(m == 0),
                                          stop=(m == KD - 1))
                mm.then_inc(wo_done, 1)

            def attend(b, r, next_loads=None):
                nxt = (b + 1, 1 - r)
                for g in range(2, GROUPS):
                    turn_probs(b, g)
                    if g + 2 < GROUPS:
                        scores(b, r, g + 2)
                    elif next_loads is not None:
                        scores(*nxt, g + 2 - GROUPS)
                    weigh_values(b, r, g)
                    if next_loads is not None:
                        if g - 2 < KD:
                            keys(*nxt, next_loads, g - 2)
                        elif g - 4 < 2:
                            values(*nxt, g - 4)
                if next_loads is None:
                    turn_heads(b)
                    project_heads(b)
                else:
                    turn_probs(b + 1, 0)
                    scores(*nxt, 2)
                    turn_heads(b)
                    weigh_values(*nxt, 0)
                    turn_probs(b + 1, 1)
                    scores(*nxt, 3)
                    project_heads(b)
                    weigh_values(*nxt, 1)

            for m in range(KD):
                keys(0, 0, 1, m)
            for part in range(2):
                values(0, 0, part)
            scores(0, 0, 0)
            scores(0, 0, 1)
            for g in range(2):
                turn_probs(0, g)
                scores(0, 0, g + 2)
                weigh_values(0, 0, g)
            with pe.Fori(0, B // 2 - 1) as i:
                attend(2 * i, 0, i + 1)
                attend(2 * i + 1, 1, i + 2)
            attend(B - 2, 0, B // 2)
            attend(B - 1, 1)

            pe.wait_ge(xn_ready, (1 + DIRS + 2) * B)
            for k in range(KD):
                for q in range(Q):
                    turned(("xn3T", k, q), lambda b: xn_tok[:, b, tile(k)], order[0])
            for k in range(KD):
                for q in range(Q):
                    job_copied(pe, ("xn3T", k, q))
            pe.wait_ge(moew_in, MOEW)
            job_bank_free(pe, ("logits",))
            for b in range(B):
                for k in range(KD):
                    mm = nc.tensor.matmul(bank(("logits",))[0:L, b * E:(b + 1) * E], xn3T[:, k, b * L:(b + 1) * L],
                                          wg_sb[:, k, :], start=(k == 0), stop=(k == KD - 1))
            mm.then_inc(job_done, 1)
            pe.wait_ge(cw_ready, 1)
            for q in range(Q):
                job_bank_free(pe, ("cwT", q))
                for b in range(BQ):
                    mm = nc.tensor.matmul(bank(("cwT", q))[0:EA, b * L:(b + 1) * L], cw_tok[:, q * BQ + b, :],
                                          ident[0:L, 0:L], start=True, stop=True)
                mm.then_inc(job_done, 1)
            for q in range(Q):
                job_copied(pe, ("cwT", q))
            pe.wait_ge(sel_ready, 2)
            for e in range(EA):
                for q in range(Q):
                    product(("cwb", e, q), P, TQ, [(expert_sel[:, e, :], cwT[:, chunk(q)])])
            for key, _ in JOBS[JOB[("cwb", EA - 1, Q - 1)] - 7:][:8]:
                job_copied(pe, key)

            for q in range(Q):
                for m in range(KD):
                    nc.tensor.matmul(ps[:, 4 + 2 * q + m, 0:TQ], b2_sb[:, tile(m)], cwT[:, chunk(q)], start=True,
                                     stop=False, skip_group_check=True)

            def experts(turns, final):
                units = [(e, r, loads, u) for e, r, loads in turns for u in range(UNITS)]

                def into_hidden(at):
                    e, r, loads, u = units[at]
                    ft, q = divmod(u, Q)
                    if u == 0:
                        pe.wait_ge(w_in[r], LOADED * loads)
                    if at >= 4:
                        pe.wait_ge(silu_done, UNITS * e + (u - 3))
                    for k in range(KD):
                        mm = nc.tensor.matmul(ps[:, u % 4, 0:TQ], w1_sb[r][:, k, tile(ft)], xn3T[:, k, chunk(q)],
                                              start=(k == 0), stop=(k == KD - 1))
                    mm.then_inc(hid_ready, 1)

                def out_of_hidden(at):
                    e, r, _, u = units[at]
                    ft, q = divmod(u, Q)
                    pe.wait_ge(hid_scaled, UNITS * e + (u + 1))
                    for m in range(KD):
                        mm = nc.tensor.matmul(ps[:, 4 + 2 * q + m, 0:TQ], w2_sb[r][:, ft, tile(m)],
                                              hidden[u % HRING][:], start=False,
                                              stop=(final and ft == FT - 1), skip_group_check=True)
                    mm.then_inc(hid_used, 1)

                for at in range(len(units) + LAG):
                    if at < len(units):
                        into_hidden(at)
                    if at >= LAG:
                        out_of_hidden(at - LAG)

            with pe.Fori(0, E // 2) as i:
                experts([(2 * i, 0, i + 1), (2 * i + 1, 1, i + 1)], False)
            experts([(E, 0, E // 2 + 1)], True)
            pe.wait_ge(yT_ready, 2 * KD)
            for h in range(B // 2):
                key = ("out", h)
                for j in range(2):
                    b = 2 * h + j
                    for m in range(KD):
                        mm = nc.tensor.transpose(bank(key)[0:L, j * D + m * P:j * D + (m + 1) * P],
                                                 yT[:, m, b * L:(b + 1) * L], ident[:])
                mm.then_inc(job_done, 1)

        @block.vector
        def _(dve):
            steps = 0

            def step(ins):
                nonlocal steps
                ins.then_inc(dve_step, 1)
                steps += 1
                dve.wait_ge(dve_step, steps)

            def later(ins):
                nonlocal steps
                ins.then_inc(dve_step, 1)
                steps += 1

            norms = 0

            def layer_norm(pairs):
                nonlocal norms
                norms += 1
                n = len(pairs)
                for j, (src, _) in enumerate(pairs):
                    later(nc.vector.bn_stats(stats[:, j, :], src))
                dve.wait_ge(dve_step, steps)
                for j in range(n):
                    later(nc.vector.bn_aggr(moments[:, j, :], stats[:, j, :]))
                dve.wait_ge(dve_step, steps)
                nc.vector.tensor_scalar(var_eps[:, 0:n], moments[:, 0:n, 1], EPS, None, ALU.add
                                        ).then_inc(moments_ready, 1)
                dve.wait_ge(std_ready, norms)
                step(nc.vector.reciprocal(rstd[:, 0:n], std[:, 0:n]))
                for j, (src, dst) in enumerate(pairs):
                    nc.vector.tensor_scalar(dst, src, moments[:, j, 0:1], rstd[:, j:j + 1], ALU.subtract, ALU.mult
                                            ).then_inc(xn_ready, 1)

            def copy_out(key, dst, src):
                job_result(dve, key)
                nc.vector.tensor_copy(dst, src).then_inc(copied["v"], 1)

            for r in range(2):
                nc.vector.memset(u_pad[r][:, :, 0:TAPS - 1], 0.0).then_inc(pad_zeroed, 1)
            dve.wait_ge(x_in, 16)
            layer_norm([(x_tok[:, b, :], xn_tok[:, b, :]) for b in range(B)])
            for d in range(DIRS):
                for k in range(KD):
                    copy_out(("xnT", d, k, 1), xT[:, d * KD + k, chunk(1)], bank(("xnT", d, k, 1))[:, 0:TQ])
            dve.wait_ge(vec_in, 16 * DIRS)
            dve.wait_ge(consts, CONSTS)
            for d in range(DIRS):
                for c in range(CT):
                    ins = nc.vector.tensor_scalar(diag_d[d][:, c, :], ident[:], vec_sb[d][:, c, V_D:V_D + 1], None,
                                                  ALU.mult)
                ins.then_inc(diag_ready, 1)
            for d in range(DIRS):
                nc.vector.tensor_scalar(neg_a[d][:].rearrange("p (c n) -> p c n", c=CT), vec_sb[d][:, :, V_ALOG:],
                                        LOG_MAX, None, ALU.min).then_inc(log_a_ready, 1)
            dve.wait_ge(pad_zeroed, 2)
            for d in range(DIRS):
                for c in range(CT):
                    for q in range(Q):
                        job_copied(dve, ("u", d, c, q))
                    padded, to = u_pad[c % 2], seqs(u_sb[d][:, c, :])
                    tap = [vec_sb[d][:, c, V_TAP + k:V_TAP + k + 1] for k in range(TAPS)]
                    step(nc.vector.tensor_scalar(to, padded[:, :, TAPS - 1:], tap[TAPS - 1],
                                                 vec_sb[d][:, c, V_CONVB:V_CONVB + 1], ALU.mult, ALU.add))
                    for k in range(TAPS - 1):
                        ins = nc.vector.scalar_tensor_tensor(to, padded[:, :, k:k + L], tap[k], to, ALU.mult, ALU.add)
                        if k < TAPS - 2:
                            step(ins)
                    ins.then_inc(conv_ready, 1)
            for d in range(DIRS):
                dve.wait_ge(rate_ready, d + 1)
                nc.vector.tensor_scalar(neg_a[d][:], neg_a[d][:], -1.0, None, ALU.mult
                                        ).then_inc(neg_a_ready, 1)

            def step_size(g):
                d, c = divmod(g, CT)
                p, e, l = pre[g % 2][:], ex[g % 2][:], lg[g % 2][:]
                dve.wait_ge(log_ready, g + 1)
                step(nc.vector.scalar_tensor_tensor(l, p, 0.0, l, ALU.max, ALU.add))
                step(nc.vector.tensor_scalar(p, e, 1.0, -1.0, ALU.add, ALU.add))
                step(nc.vector.tensor_tensor(e, e, p, ALU.subtract))
                nc.vector.tensor_tensor(dt_sb[d][:, c, :], l, e, ALU.add).then_inc(dt_ready, 1)

            for d in range(DIRS):
                for name in "BC":
                    part = parts[name][d]
                    for q in range(Q):
                        copy_out((name, d, q), rows_f[:, chunk(q)], bank((name, d, q))[0:N, 0:TQ])
                    job_copied(dve, (name, d, Q - 1))
                    step(nc.vector.tensor_copy(part[0:N, :], rows_f))
                    step(nc.vector.tensor_tensor(rest_f, rows_f, part[0:N, :], ALU.subtract))
                    step(nc.vector.tensor_copy(part_mid[:], rest_f))
                    later(nc.vector.tensor_copy(part[N:2 * N, :], part_mid[:]))
                    dve.wait_ge(dve_step, steps)
                    nc.vector.tensor_tensor(part[2 * N:3 * N, :], rest_f, part_mid[:], ALU.subtract
                                            ).then_inc(parts_ready, 1)
                for c in range(CT):
                    g = d * CT + c
                    for q in range(Q):
                        key = ("dt", d, c, q)
                        job_result(dve, key)
                        nc.vector.tensor_scalar(pre[g % 2][:, chunk(q)], bank(key)[:, 0:TQ],
                                                vec_sb[d][:, c, V_BDT:V_BDT + 1], None, ALU.add
                                                ).then_inc(copied["v"], 1)
                    if g:
                        step_size(g - 1)
            step_size(DIRS * CT - 1)
            nc.vector.memset(ps[:, 4:6, 0:TQ].rearrange("p k (b t) -> p k b t", t=L)[:, :, :, 0:1], 0.0
                             ).then_inc(decay_zeroed, 1)
            dve.wait_ge(decay_zeroed, 1)

            def recur(d, q, n, r):
                dve.wait_ge(b_bank_ready, n + 1)
                if not (isinstance(n, int) and n < RING):
                    dve.wait_ge(y_summed, n - (RING - 1))
                nc.vector.tensor_tensor(states[r][:].rearrange("p (c t) -> p c t", c=CT), dtu[d][:, :, chunk(q)],
                                        ps[:, 6:7, 0:TQ].broadcast_to([P, CT, TQ]), ALU.mult
                                        ).then_inc(inflow_ready, 1)
                dve.wait_ge(inflow_ready, n + 1)
                for c in range(CT):
                    dve.wait_ge(decay_ready, CT * n + (c + 1))
                    st = states[r][:, c * TQ:(c + 1) * TQ]
                    nc.vector.tensor_tensor_scan(st, ps[:, 4 + c % 2, 0:TQ], st, 0.0, ALU.mult, ALU.add
                                                 ).then_inc(scan_done, 1)

            dve.wait_ge(dtu_ready, DIRS * CT)
            for r in range(RING):
                recur(0, 0, r, r)
            for s in range(SEG):
                d, q = divmod(s, Q)
                with dve.Fori(s == 0, N // RING) as i:
                    for r in range(RING):
                        recur(d, q, i * RING + (s * N + r), r)
                dve.wait_ge(y_summed, (s + 1) * N)
                for c in range(CT):
                    nc.vector.tensor_tensor(u_sb[d][:, c, chunk(q)], ps[:, c, 0:TQ], gate[d][:, c, chunk(q)], ALU.mult
                                            ).then_inc(y_gated, 1)

            for d in range(DIRS):
                for h in range(B // 2):
                    job_copied(dve, ("mix", d, h))
            layer_norm([(mix_tok[d][:, b, :], mix_tok[d][:, b, :]) for d in range(DIRS) for b in range(B)])
            for d in range(DIRS):
                for k in range(KD):
                    j, key = d * KD + k, ("mixT", d, k, 0)
                    job_result(dve, key)
                    nc.vector.tensor_scalar(xT[:, j, chunk(0)], bank(key)[:, 0:TQ], lng_sb[:, j:j + 1],
                                            lnb_sb[:, j:j + 1], ALU.mult, ALU.add).then_inc(copied["v"], 1)

            def add_to(dst, src, key):
                job_result(dve, key)
                h = pair(key[-1])
                return nc.vector.tensor_tensor(dst[:, h, :].rearrange("l b d -> l (b d)"),
                                               src[:, h, :].rearrange("l b d -> l (b d)"), bank(key)[0:L, :], ALU.add)

            dve.wait_ge(bias_added, 1)
            for h in range(B // 2):
                add_to(x_tok, x_tok, ("fuse", h)).then_inc(copied["v"], 1)
            job_copied(dve, ("fuse", B // 2 - 1))
            layer_norm([(x_tok[:, b, :], xn_tok[:, b, :]) for b in range(B)])
            for k in range(KD):
                copy_out(("xn2T", k, 0), xn2T[:, k, chunk(0)], bank(("xn2T", k, 0))[:, 0:TQ])
            for m in range(KD):
                copy_out(("qT", m, 0), qT[:, m, chunk(0)], bank(("qT", m, 0))[:, 0:TQ])
            dve.wait_ge(bias_added, 2)

            def copy_values(b, r, part):
                dve.wait_ge(v_done, 2 * b + (part + 1))
                if part == 0:
                    ins = nc.vector.tensor_copy(v_sb[r][:, 0:2, :].rearrange("p k d -> p (k d)"), ps[:, KEY_BANK, :])
                else:
                    ins = nc.vector.tensor_copy(v_sb[r][0:SL, 2, :], ps[0:SL, KEY_BANK, 0:D])
                ins.then_inc(v_copied, 1)

            def maxima(b, r, g):
                dve.wait_ge(scores_ready, GROUPS * b + (g + 1))
                nc.vector.tensor_reduce(neg_max[:, r, 2 * g:2 * g + 2], ps[0:L, g % 2 * 2:g % 2 * 2 + 2, 0:S],
                                        AX.X, ALU.max).then_inc(max_ready, 1)
                dve.wait_ge(max_ready, GROUPS * b + (g + 1))
                nc.vector.tensor_scalar(shift[:, r, 2 * g:2 * g + 2], neg_max[:, r, 2 * g:2 * g + 2],
                                        -HD ** -0.5, None, ALU.mult).then_inc(shift_ready, 1)

            def copy_probs(b, g):
                dve.wait_ge(probsT_ready, GROUPS * b + (g + 1))
                if not isinstance(b, int) or GROUPS * b + g >= 2:
                    dve.wait_ge(pv_done, GROUPS * b + (g - 1))
                nc.vector.tensor_copy(probsT[g % 2][0][:], ps[:, 4, 0:KT * L]).then_inc(probsT_copied[0], 1)

            def normalise_heads(b, r):
                dve.wait_ge(probs_ready, 2 * GROUPS * b + 2 * GROUPS)
                nc.vector.reciprocal(inv_mass[:, r, :], mass[:, r, :]).then_inc(inv_mass_ready, 1)
                dve.wait_ge(inv_mass_ready, b + 1)
                dve.wait_ge(pv_done, GROUPS * b + GROUPS)
                nc.vector.tensor_tensor(heads_tok[:].rearrange("l (h e) -> l h e", h=H),
                                        ps[0:L, 6, 0:D].rearrange("l (h e) -> l h e", h=H),
                                        inv_mass[:, r, :].unsqueeze(2).broadcast_to([L, H, HD]), ALU.mult
                                        ).then_inc(heads_ready, 1)

            def copy_heads(b):
                dve.wait_ge(headsT_done, b + 1)
                nc.vector.tensor_copy(headsT[:].rearrange("p m t -> p (m t)"), ps[:, KEY_BANK, 0:KD * L]
                                      ).then_inc(headsT_copied, 1)

            def add_attention(b):
                dve.wait_ge(wo_done, b + 1)
                x2 = x_tok[:, bass.ds(b, 1), :].rearrange("l b d -> l (b d)")
                nc.vector.tensor_tensor(x2, x2, ps[0:L, KEY_BANK, 0:D], ALU.add).then_inc(x2_ready, 1)

            def attend(b, r, last=False):
                for g in range(2, GROUPS):
                    copy_probs(b, g)
                    if g + 2 < GROUPS:
                        maxima(b, r, g + 2)
                    elif not last:
                        maxima(b + 1, 1 - r, g + 2 - GROUPS)
                    if g - 4 in range(2) and not last:
                        copy_values(b + 1, 1 - r, g - 4)
                normalise_heads(b, r)
                if not last:
                    copy_probs(b + 1, 0)
                    maxima(b + 1, 1 - r, 2)
                copy_heads(b)
                if not last:
                    copy_probs(b + 1, 1)
                    maxima(b + 1, 1 - r, 3)
                add_attention(b)

            for part in range(2):
                copy_values(0, 0, part)
            maxima(0, 0, 0)
            maxima(0, 0, 1)
            for g in range(2):
                copy_probs(0, g)
                maxima(0, 0, g + 2)
            with dve.Fori(0, B // 2 - 1) as i:
                for r in range(2):
                    attend(2 * i + r, r)
            attend(B - 2, 0)
            attend(B - 1, 1, last=True)
            dve.wait_ge(x2_ready, B)
            layer_norm([(x_tok[:, b, :], xn_tok[:, b, :]) for b in range(B)])
            for k in range(KD):
                copy_out(("xn3T", k, 0), xn3T[:, k, chunk(0)], bank(("xn3T", k, 0))[:, 0:TQ])

            job_result(dve, ("logits",))
            logits = bank(("logits",))[0:L, 0:B * E].rearrange("l (b e) -> l b e", e=E)
            rt, tk = route, per_tok
            step(nc.vector.tensor_reduce(tk["max"][:, :, 0], logits, AX.X, ALU.max))
            nc.vector.tensor_tensor(rt["shifted"][:], logits, spread(tk["max"][:], E), ALU.subtract
                                    ).then_inc(copied["v"], 1)
            job_copied(dve, ("logits",))
            nc.vector.memset(cw_tok[:, :, E:EA], SHARED).then_inc(shifted_ready, 1)
            dve.wait_ge(exp_ready, 1)
            step(nc.vector.tensor_reduce(tk["sum"][:, :, 0], rt["exp"][:], AX.X, ALU.add))
            step(nc.vector.reciprocal(tk["inv"][:], tk["sum"][:]))
            step(nc.vector.tensor_tensor(rt["prob"][:], rt["exp"][:], spread(tk["inv"][:], E), ALU.mult))
            prefer_all = prefer[:].unsqueeze(1).broadcast_to([L, B, E])

            def largest(src, top, pick, chosen):
                step(nc.vector.tensor_reduce(top[:, :, 0], src, AX.X, ALU.max))
                step(nc.vector.tensor_tensor(rt["tie"][:], src, spread(top[:], E), ALU.is_equal))
                step(nc.vector.tensor_tensor(rt["tie"][:], rt["tie"][:], prefer_all, ALU.mult))
                step(nc.vector.tensor_reduce(pick[:, :, 0], rt["tie"][:], AX.X, ALU.max))
                step(nc.vector.tensor_tensor(chosen, rt["tie"][:], spread(pick[:], E), ALU.is_equal))

            largest(rt["prob"][:], tk["top1"], tk["pick1"], rt["first"][:])
            step(nc.vector.scalar_tensor_tensor(rt["rest"][:], rt["first"][:], -4.0, rt["prob"][:], ALU.mult, ALU.add))
            largest(rt["rest"][:], tk["top2"], tk["pick2"], rt["second"][:])
            step(nc.vector.tensor_tensor(rt["both"][:], rt["first"][:], rt["second"][:], ALU.add))
            step(nc.vector.tensor_tensor(rt["kept"][:], rt["both"][:], rt["prob"][:], ALU.mult))
            step(nc.vector.scalar_tensor_tensor(tk["den"][:, :, 0], tk["top1"][:, :, 0], 1e-9, tk["top2"][:, :, 0],
                                                ALU.add, ALU.add))
            step(nc.vector.reciprocal(tk["inv_den"][:], tk["den"][:]))
            nc.vector.tensor_tensor(cw_tok[:, :, 0:E], rt["kept"][:], spread(tk["inv_den"][:], E), ALU.mult
                                    ).then_inc(cw_ready, 1)
            for q in range(Q):
                copy_out(("cwT", q), cwT[:, chunk(q)], bank(("cwT", q))[0:EA, 0:TQ])
            for e in range(EA):
                copy_out(("cwb", e, 0), cw_b[:, e * T:e * T + TQ], bank(("cwb", e, 0))[:, 0:TQ])
            job_copied(dve, ("cwb", EA - 1, 0))
            job_copied(dve, ("cwb", EA - 1, 1))

            def scale_expert(e):
                for u in range(UNITS):
                    dve.wait_ge(silu_done, UNITS * e + (u + 1))
                    h = hidden[u % HRING][:]
                    nc.vector.tensor_tensor(h, h, cw_b[:, bass.ds(T * e + TQ * (u % Q), TQ)], ALU.mult
                                            ).then_inc(hid_scaled, 1)

            with dve.Fori(0, E // 2) as i:
                for r in range(2):
                    scale_expert(2 * i + r)
            scale_expert(E)
            dve.wait_ge(hid_used, UNITS * EA)
            for q in range(Q):
                nc.vector.tensor_copy(yT[:, 0, chunk(q)], ps[:, 4 + 2 * q, 0:TQ]).then_inc(yT_ready, 1)
            for h in range(B // 2):
                add_to(out_tok, x_tok, ("out", h)).then_inc(out_ready, 1)


_OUT = (B, L, D)


def _laid_out(inputs):
    a = {k: np.asarray(v) for k, v in inputs.items()}

    def per_channel(*columns):
        rows = np.concatenate([c.reshape(DI, -1) for c in columns], axis=1)
        return rows.reshape(CT, P, -1).transpose(1, 0, 2)

    def both(make):
        return np.stack([make(lambda name: a[f"L0_attn_{name}_{s}"]) for s in "fb"])

    def per_feature(name):
        return both(lambda w: w(name)).reshape(DIRS * KD, P).T

    def with_shared(routed, shared):
        return np.concatenate([a[f"L0_ffn_{routed}"], a[f"L0_ffn_{shared}"][None]])

    arrays = {
        "x": a["x"],
        "ctxT": a["ctx_1024"].transpose(0, 2, 1),
        "winT": both(lambda w: w("Win").T),
        "wxT": both(lambda w: w("Wx").T),
        "wdtT": both(lambda w: w("Wdt").T),
        "woutT": both(lambda w: w("Wout").T),
        "vec": both(lambda w: per_channel(w("convw"), w("convb"), w("bdt"), w("Dp"), w("Alog"))),
        "ln_g": per_feature("ln_g"),
        "ln_b": per_feature("ln_b"),
        "wfuseT": a["L0_attn_Wfuse"].T,
        "bfuse": a["L0_attn_bfuse"],
        "wqT": a["L0_xattn_Wq"].T,
        "wkT": a["L0_xattn_Wk"].T,
        "wvT": a["L0_xattn_Wv"].T,
        "woT": a["L0_xattn_Wo"].T,
        "bo": a["L0_xattn_bo"],
        "wg": a["L0_ffn_Wg"],
        "w1": with_shared("W1", "Ws1"),
        "b1": with_shared("b1", "bs1").reshape(EA, FT, P).transpose(0, 2, 1),
        "w2": with_shared("W2", "Ws2"),
        "b2": with_shared("b2", "bs2"),
    }
    return {k: np.ascontiguousarray(v) for k, v in arrays.items()}


def kernel(**inputs):
    from concourse import bacc
    from concourse.bass_utils import run_bass_kernel_spmd

    arrays = _laid_out(inputs)
    nc = bacc.Bacc("TRN2", target_bir_lowering=False, num_devices=1)
    aps = {k: nc.dram_tensor(f"in_{k}", v.shape, mybir.dt.from_np(v.dtype), kind="ExternalInput").ap()
           for k, v in arrays.items()}
    out = nc.dram_tensor("out_x", _OUT, F32, kind="ExternalOutput").ap()
    decoder_layer(nc, **aps, out=out)
    result = run_bass_kernel_spmd(nc, [{f"in_{k}": v for k, v in arrays.items()}], core_ids=[0])
    return result.results[0]["out_x"]
```

```python
from contextlib import ExitStack

import numpy as np

import concourse.bass as bass
from concourse import mybir

F32 = mybir.dt.float32
F32R = mybir.dt.float32r
BF16 = mybir.dt.bfloat16
ALU = mybir.AluOpType
ACT = mybir.ActivationFunctionType
AX = mybir.AxisListType

P = 128
B, L, D = 8, 100, 256
T = B * L
KD = D // P
DI = 2 * D
CT = DI // P
N = 32
R = D // 16
TAPS = 4
S = 361
KT = -(-S // P)
SL = S - (KT - 1) * P
H = 16
HD = D // H
HT = H // KD
F = 1024
FT = F // P
E = 8
EA = E + 1
EPS = 1e-5
SHARED = 0.1
LOG_MAX = 82.0
Q = 2
BQ = B // Q
TQ = T // Q
DIRS = 2
RING = 4
SEG = DIRS * Q
BANK = 512
UNITS = FT * Q
HRING = 4
LAG = 2
GROUPS = H // 2
KEY_BANK = 7
CONSTS = 12 + E
MIXW, MOEW = 16 * 11, 16 * 2
LOADED = 16 * 3

V_TAP, V_CONVB, V_BDT, V_D, V_ALOG = 0, TAPS, TAPS + 1, TAPS + 2, TAPS + 3
VEC = TAPS + 3 + N


def bank_jobs():
    jobs = []
    for d in range(DIRS):
        for k in range(KD):
            for q in range(Q):
                jobs.append((("xnT", d, k, q), "v" if q else "a"))
    for d in range(DIRS):
        for c in range(CT):
            for q in range(Q):
                jobs.append((("u", d, c, q), "a"))
        for c in range(CT):
            for q in range(Q):
                jobs.append((("z", d, c, q), "a"))
    for d in range(DIRS):
        for q in range(Q):
            jobs.append((("rank", d, q), "a"))
        for w in "BC":
            for q in range(Q):
                jobs.append(((w, d, q), "v"))
        for c in range(CT):
            for q in range(Q):
                jobs.append((("dt", d, c, q), "v"))
    for d in range(DIRS):
        for h in range(B // 2):
            jobs.append((("mix", d, h), "a"))
    for d in range(DIRS):
        for k in range(KD):
            for q in range(Q):
                jobs.append((("mixT", d, k, q), "a" if q else "v"))
    for h in range(B // 2):
        jobs.append((("fuse", h), "v"))
    for k in range(KD):
        for q in range(Q):
            jobs.append((("xn2T", k, q), "a" if q else "v"))
    for m in range(KD):
        for q in range(Q):
            jobs.append((("qT", m, q), "a" if q else "v"))
    for k in range(KD):
        for q in range(Q):
            jobs.append((("xn3T", k, q), "a" if q else "v"))
    jobs.append((("logits",), "v"))
    for q in range(Q):
        jobs.append((("cwT", q), "v"))
    for e in range(EA):
        for q in range(Q):
            jobs.append((("cwb", e, q), "a" if q else "v"))
    for h in range(B // 2):
        jobs.append((("out", h), "v"))
    return jobs


JOBS = bank_jobs()
JOB = {key: n for n, (key, _) in enumerate(JOBS)}
OWNER = [owner for _, owner in JOBS]
COPIED = [OWNER[:n + 1].count(OWNER[n]) for n in range(len(JOBS))]


def decoder_layer(nc, x, ctxT, winT, wxT, wdtT, woutT, vec, ln_g, ln_b, wfuseT, bfuse,
                  wqT, wkT, wvT, woT, bo, wg, w1, b1, w2, b2, out):
    stack = ExitStack()
    with stack:
        def sb(name, shape, dt=F32, scope=stack):
            return scope.enter_context(nc.sbuf_tensor(name, shape, dt))

        def sem(name):
            return stack.enter_context(nc.semaphore(name))

        ps = stack.enter_context(nc.psum_tensor("ps", [P, 8, BANK], F32))

        ident = sb("ident", [P, P])
        flip = sb("flip", [L, L])
        head_mask = sb("head_mask", [P, HT])
        one = sb("one", [P, 1])
        prefer = sb("prefer", [L, E])
        x_tok = sb("x_tok", [L, B, D])
        xn_tok = sb("xn_tok", [L, B, D])
        stats = sb("stats", [L, DIRS * B, 6])
        moments = sb("moments", [L, DIRS * B, 2])
        var_eps = sb("var_eps", [L, DIRS * B])
        std = sb("std", [L, DIRS * B])
        rstd = sb("rstd", [L, DIRS * B])
        bias_tok = sb("bias_tok", [L, 2, D])

        mixing = ExitStack()
        row_sel = sb("row_sel", [96, N, P], BF16, scope=mixing)
        wx_sb = [sb(f"wx{d}", [P, CT, R + 2 * N], scope=mixing) for d in range(DIRS)]
        wdt_sb = [sb(f"wdt{d}", [R, DI], scope=mixing) for d in range(DIRS)]
        diag_d = [sb(f"diag_d{d}", [P, CT, P], scope=mixing) for d in range(DIRS)]
        vec_sb = [sb(f"vec{d}", [P, CT, VEC], scope=mixing) for d in range(DIRS)]
        neg_a = [sb(f"neg_a{d}", [P, CT * N], scope=mixing) for d in range(DIRS)]
        wout_sb = [sb(f"wout{d}", [P, CT, D], scope=mixing) for d in range(DIRS)]
        wfuse_sb = sb("wfuse_sb", [P, DIRS * KD, D], scope=mixing)
        lng_sb = sb("lng_sb", [P, DIRS * KD], scope=mixing)
        lnb_sb = sb("lnb_sb", [P, DIRS * KD], scope=mixing)
        xT = sb("xT", [P, 4, T], scope=mixing)

        mixer = ExitStack()
        dt_sb = [sb(f"dt{d}", [P, CT, T], scope=mixer) for d in range(DIRS)]
        dtu = [sb(f"dtu{d}", [P, CT, T], scope=mixer) for d in range(DIRS)]
        u_sb = [sb(f"u{d}", [P, CT, T], scope=mixer) for d in range(DIRS)]
        gate = [sb(f"gate{d}", [P, CT, T], scope=mixer) for d in range(DIRS)]
        b_parts = [sb(f"b_parts{d}", [96, T], BF16, scope=mixer) for d in range(DIRS)]
        c_parts = [sb(f"c_parts{d}", [96, T], BF16, scope=mixer) for d in range(DIRS)]
        parts = {"B": b_parts, "C": c_parts}
        early = ExitStack()
        win_sb = [sb(f"win{d}", [P, KD, 2 * DI], scope=early) for d in range(DIRS)]
        u_pad = [sb(f"u_pad{r}", [P, B, L + TAPS - 1], scope=early) for r in range(2)]
        early.close()
        softp = ExitStack()
        pre = [sb(f"pre{r}", [P, T], scope=softp) for r in range(2)]
        ex = [sb(f"ex{r}", [P, T], scope=softp) for r in range(2)]
        lg = [sb(f"lg{r}", [P, T], scope=softp) for r in range(2)]
        part_mid = sb("part_mid", [N, T], BF16, scope=softp)
        softp.close()
        rank_sb = xT[0:R, 0:2, :]
        rows_f = xT[0:N, 2, :]
        rest_f = xT[0:N, 3, :]
        states = [sb(f"states{r}", [P, CT * TQ], scope=mixer) for r in range(RING)]
        c_row = [sb(f"c_row{r}", [P, TQ], scope=mixer) for r in range(2)]
        decay_sb = [sb(f"decay{r}", [P, TQ], scope=mixer) for r in range(CT - 2)]
        decay = [ps[:, 4, 0:TQ], ps[:, 5, 0:TQ], *(t[:] for t in decay_sb)]
        mixer.close()

        late = ExitStack()
        mix_tok = [sb(f"mix_tok{d}", [L, B, D], scope=late) for d in range(DIRS)]
        attn = ExitStack()
        xn2T = sb("xn2T", [P, KD, T], scope=attn)
        qT = sb("qT", [P, KD, T], scope=attn)
        q_blk = [sb(f"q_blk{r}", [P, KD, HT, L], scope=attn) for r in range(2)]
        ctx_sb = [sb(f"ctx{r}", [P, KD, S], scope=attn) for r in range(2)]
        wq_sb, wk_sb, wv_sb, wo_sb = (sb(n, [P, KD, D], scope=attn) for n in ("wq_sb", "wk_sb", "wv_sb", "wo_sb"))
        kT = [sb(f"kT{r}", [P, KD, S], scope=attn) for r in range(2)]
        v_sb = [sb(f"v{r}", [P, KT, D], scope=attn) for r in range(2)]
        probs = [sb(f"probs{r}", [L, 2, KT * P], scope=attn) for r in range(2)]
        probsT = [[sb(f"probsT{r}{j}", [P, KT * L], scope=attn) for j in range(2)] for r in range(2)]
        neg_max, shift, mass, inv_mass = (sb(n, [L, 2, H], scope=attn) for n in ("neg_max", "shift", "mass", "inv_mass"))
        heads_tok = sb("heads_tok", [L, D], scope=attn)
        headsT = sb("headsT", [P, KD, L], scope=attn)
        attn.close()
        late.close()
        mixing.close()

        moe = ExitStack()
        w1_raw = sb("w1_raw", [P, KD, F], scope=moe)
        w2_raw = sb("w2_raw", [P, FT, D], scope=moe)
        b1_sb = [sb(f"b1_{r}", [P, FT], scope=moe) for r in range(2)]
        w1_part = [[sb(f"w1_{n}{r}", [P, KD, F], F32R, scope=moe) for n in "hl"] for r in range(2)]
        w2_part = [[sb(f"w2_{n}{r}", [P, FT, D], F32R, scope=moe) for n in "hl"] for r in range(2)]
        xn3_part = [sb(f"xn3_{n}", [P, KD, T], F32R, scope=moe) for n in "hl"]
        xn3T = sb("xn3T", [P, KD, T], scope=moe)
        expert_sel = sb("expert_sel", [EA, EA, P], scope=moe)
        wg_sb = sb("wg_sb", [P, KD, E], scope=moe)
        b2_sb = sb("b2_sb", [EA, D], scope=moe)
        cw_b = sb("cw_b", [P, EA * T], scope=moe)
        cw_tok = sb("cw_tok", [L, B, EA], scope=moe)
        cwT = sb("cwT", [EA, T], scope=moe)
        route = {n: sb(f"route_{n}", [L, B, E], scope=moe)
                 for n in ("shifted", "exp", "prob", "tie", "first", "rest", "second", "both", "kept")}
        per_tok = {n: sb(f"tok_{n}", [L, B, 1], scope=moe)
                   for n in ("max", "sum", "inv", "top1", "pick1", "top2", "pick2", "den", "inv_den")}
        hidden = [sb(f"hidden{r}", [P, TQ], scope=moe) for r in range(HRING)]
        hid_part = [[sb(f"hidden_{n}{r}", [P, TQ], F32R, scope=moe) for n in "hl"] for r in range(HRING)]
        weighted = sb("weighted", [P, KD, TQ], scope=moe)
        yT = sb("yT", [P, KD, T], scope=moe)
        out_tok = sb("out_tok", [L, B, D], scope=moe)
        moe.close()

        consts = sem("consts")
        x_in = sem("x_in")
        win_in = [sem(f"win_in{d}") for d in range(DIRS)]
        vec_in = sem("vec_in")
        mixw_in = sem("mixw_in")
        attnw_in = sem("attnw_in")
        ctx_in = [sem(f"ctx_in{r}") for r in range(2)]
        moew_in = sem("moew_in")
        raw_in = sem("raw_in")
        split_done = sem("split_done")
        xn3_split = sem("xn3_split")
        bias_summed = sem("bias_summed")
        out_stored = sem("out_stored")
        job_done = sem("job_done")
        copied = {"a": sem("copied_by_act"), "v": sem("copied_by_dve")}
        moments_ready = sem("moments_ready")
        std_ready = sem("std_ready")
        xn_ready = sem("xn_ready")
        dve_step = sem("dve_step")
        act_step = sem("act_step")
        bias_added = sem("bias_added")
        pad_zeroed = sem("pad_zeroed")
        conv_ready = sem("conv_ready")
        u_ready = sem("u_ready")
        log_ready = sem("log_ready")
        dt_ready = sem("dt_ready")
        dtu_ready = sem("dtu_ready")
        log_a_ready = sem("log_a_ready")
        rate_ready = sem("rate_ready")
        neg_a_ready = sem("neg_a_ready")
        diag_ready = sem("diag_ready")
        parts_ready = sem("parts_ready")
        decay_zeroed = sem("decay_zeroed")
        b_bank_ready = sem("b_bank_ready")
        c_bank_ready = sem("c_bank_ready")
        c_row_ready = sem("c_row_ready")
        decay_ready = sem("decay_ready")
        inflow_ready = sem("inflow_ready")
        scan_done = sem("scan_done")
        product_ready = sem("product_ready")
        y_summed = sem("y_summed")
        y_gated = sem("y_gated")
        probs_zeroed = sem("probs_zeroed")
        q_blk_ready = sem("q_blk_ready")
        k_done = sem("k_done")
        v_done = sem("v_done")
        k_copied = sem("k_copied")
        v_copied = sem("v_copied")
        scores_ready = sem("scores_ready")
        max_ready = sem("max_ready")
        shift_ready = sem("shift_ready")
        probs_ready = sem("probs_ready")
        probsT_ready = sem("probsT_ready")
        probsT_copied = [sem("probsT_copied_by_dve"), sem("probsT_copied_by_act")]
        pv_done = sem("pv_done")
        inv_mass_ready = sem("inv_mass_ready")
        heads_ready = sem("heads_ready")
        headsT_done = sem("headsT_done")
        headsT_copied = sem("headsT_copied")
        wo_done = sem("wo_done")
        x2_ready = sem("x2_ready")
        sel_ready = sem("sel_ready")
        shifted_ready = sem("shifted_ready")
        exp_ready = sem("exp_ready")
        cw_ready = sem("cw_ready")
        hid_ready = sem("hid_ready")
        silu_done = sem("silu_done")
        hid_split = sem("hid_split")
        hid_used = sem("hid_used")
        y_taken = sem("y_taken")
        yT_ready = sem("yT_ready")
        out_ready = sem("out_ready")

        def bank(key):
            return ps[:, JOB[key] % 8, :]

        def job_bank_free(eng, key):
            before = JOB[key] - 8
            if before >= 0:
                eng.wait_ge(copied[OWNER[before]], COPIED[before])

        def job_result(eng, key):
            eng.wait_ge(job_done, JOB[key] + 1)

        def job_copied(eng, key):
            eng.wait_ge(copied[OWNER[JOB[key]]], COPIED[JOB[key]])

        def chunk(q):
            return slice(q * TQ, (q + 1) * TQ)

        def pair(h):
            return slice(2 * h, 2 * h + 2)

        def tile(k):
            return slice(k * P, (k + 1) * P)

        def seqs(ap):
            return ap.rearrange("p (b t) -> p b t", t=L)

        def spread(per_token, width):
            return per_token.broadcast_to([L, B, width])

        block = stack.enter_context(nc.Block())

        @block.sync
        def _(sp):
            sp.dma_start(x_tok[:], x.rearrange("b l d -> l b d")).then_inc(x_in, 16)
            for d in range(DIRS):
                sp.dma_start(win_sb[d][:], winT[d].rearrange("(k p) e -> p k e", p=P)).then_inc(win_in[d], 16)
                sp.dma_start(vec_sb[d][:], vec[d]).then_inc(vec_in, 16)
            for d in range(DIRS):
                sp.dma_start(wx_sb[d][:], wxT[d].rearrange("(c p) e -> p c e", p=P)).then_inc(mixw_in, 16)
                sp.dma_start(wdt_sb[d][:], wdtT[d]).then_inc(mixw_in, 16)
                sp.dma_start(wout_sb[d][:], woutT[d].rearrange("(c p) e -> p c e", p=P)).then_inc(mixw_in, 16)
            sp.dma_start(wfuse_sb[:], wfuseT.rearrange("(k p) e -> p k e", p=P)).then_inc(mixw_in, 16)
            sp.dma_start(lng_sb[:], ln_g).then_inc(mixw_in, 16)
            sp.dma_start(lnb_sb[:], ln_b).then_inc(mixw_in, 16)
            sp.dma_start(bias_tok[:, 0, :], bfuse.partition_broadcast(L)).then_inc(mixw_in, 16)
            sp.dma_start(bias_tok[:, 1, :], bo.partition_broadcast(L)).then_inc(mixw_in, 16)
            job_result(sp, ("mix", DIRS - 1, B // 2 - 1))
            for w_dram, w_sbuf in ((wqT, wq_sb), (wkT, wk_sb), (wvT, wv_sb), (woT, wo_sb)):
                sp.dma_start(w_sbuf[:], w_dram.rearrange("(k p) e -> p k e", p=P)).then_inc(attnw_in, 16)
            for b in range(2):
                sp.dma_start(ctx_sb[b][:], ctxT[b].rearrange("(k p) s -> p k s", p=P)).then_inc(ctx_in[b], 16)

            def load_expert(e, r):
                at = bass.ds(e, 1)
                sp.dma_start(w1_raw[:], w1[at].rearrange("e (k p) f -> p (e k) f", p=P)).then_inc(raw_in, 16)
                sp.dma_start(w2_raw[:], w2[at].rearrange("e (f p) d -> p (e f) d", p=P)).then_inc(raw_in, 16)
                sp.dma_start(b1_sb[r][:], b1[at].rearrange("e p f -> p (e f)")).then_inc(raw_in, 16)

            job_copied(sp, ("fuse", B // 2 - 1))
            load_expert(0, 0)
            with sp.Fori(1, B // 2) as i:
                for r in range(2):
                    sp.wait_ge(v_done, 4 * i + (2 * r - 2))
                    sp.dma_start(ctx_sb[r][:], ctxT[bass.ds(2 * i + r, 1)].rearrange("b (k p) s -> p (b k) s", p=P)
                                 ).then_inc(ctx_in[r], 16)
            sp.wait_ge(x2_ready, B)
            sp.dma_start(wg_sb[:], wg.rearrange("(k p) e -> p k e", p=P)).then_inc(moew_in, 16)
            sp.dma_start(b2_sb[:], b2).then_inc(moew_in, 16)
            sp.wait_ge(split_done, 4)
            load_expert(1, 1)
            with sp.Fori(1, E // 2) as i:
                for r in range(2):
                    sp.wait_ge(split_done, 8 * i + 4 * r)
                    sp.wait_ge(hid_used, 2 * UNITS * i + UNITS * (r - 1))
                    load_expert(2 * i + r, r)
            sp.wait_ge(split_done, 4 * E)
            sp.wait_ge(hid_used, UNITS * (E - 1))
            load_expert(E, 0)
            for h in range(B // 2):
                sp.wait_ge(out_ready, h + 1)
                sp.dma_start(out[pair(h)].rearrange("b l d -> l b d"), out_tok[:, pair(h), :]).then_inc(out_stored, 16)
            sp.wait_ge(out_stored, 16 * (B // 2))

        @block.gpsimd
        def _(pool):
            made = 0

            def fill(t, value):
                nonlocal made
                nc.gpsimd.memset(t, value).then_inc(consts, 1)
                made += 1
                pool.wait_ge(consts, made)

            def where(t, compare, value, base, pattern, step):
                nonlocal made
                nc.gpsimd.affine_select(out=t, in_=t, compare_op=compare, fill=value, base=base, pattern=pattern,
                                        channel_multiplier=step).then_inc(consts, 1)
                made += 1
                pool.wait_ge(consts, made)

            fill(ident[:], 0.0)
            where(ident[:], ALU.not_equal, 1.0, 0, [[-1, P]], 1)
            fill(flip[:], 0.0)
            where(flip[:], ALU.not_equal, 1.0, 1 - L, [[1, L]], 1)
            fill(row_sel[:], 0.0)
            for part in range(3):
                where(row_sel[:], ALU.not_equal, 1.0, -part * N, [[-1, N], [0, P]], 1)
            fill(head_mask[:], 1.0)
            where(head_mask[:], ALU.is_ge, 0.0, 0, [[-HD, HT]], 1)
            where(head_mask[:], ALU.is_ge, 0.0, HD - 1, [[HD, HT]], -1)
            fill(one[:], 1.0)
            for e in range(E):
                fill(prefer[:, e:e + 1], float(E - e))
            assert made == CONSTS
            pool.wait_ge(mixw_in, MIXW)
            pool.wait_ge(xn_ready, B)
            nc.gpsimd.tensor_tensor(x_tok[:], x_tok[:], bias_tok[:, 0:1, :].broadcast_to([L, B, D]), ALU.add
                                    ).then_inc(bias_added, 1)
            for d in range(DIRS):
                for c in range(CT):
                    pool.wait_ge(dt_ready, d * CT + c + 1)
                    pool.wait_ge(u_ready, d * CT + c + 1)
                    nc.gpsimd.tensor_tensor(dtu[d][:, c, :], dt_sb[d][:, c, :], u_sb[d][:, c, :], ALU.mult
                                            ).then_inc(dtu_ready, 1)

            def state_times_c(n, r):
                pool.wait_ge(scan_done, CT * n + CT)
                pool.wait_ge(c_row_ready, n + 1)
                st = states[r][:].rearrange("p (c t) -> p c t", c=CT)
                nc.gpsimd.tensor_tensor(st, st, c_row[r % 2][:].unsqueeze(1).broadcast_to([P, CT, TQ]),
                                        ALU.mult).then_inc(product_ready, 1)

            for s in range(SEG):
                with pool.Fori(0, N // RING) as i:
                    for r in range(RING):
                        state_times_c(i * RING + (s * N + r), r)
            pool.wait_ge(xn_ready, (1 + DIRS + 1) * B)
            nc.gpsimd.tensor_tensor(x_tok[:], x_tok[:], bias_tok[:, 1:2, :].broadcast_to([L, B, D]), ALU.add
                                    ).then_inc(bias_added, 1)
            for r in range(2):
                nc.gpsimd.memset(probs[r][:, :, S:], 0.0).then_inc(probs_zeroed, 1)
            def spread_queries(b, r):
                for m in range(KD):
                    for q in range(Q):
                        job_copied(pool, ("qT", m, q))
                    nc.gpsimd.tensor_tensor(
                        q_blk[r][:, m], qT[:, m, bass.ds(b * L, L)].unsqueeze(1).broadcast_to([P, HT, L]),
                        head_mask[:].unsqueeze(2).broadcast_to([P, HT, L]), ALU.mult).then_inc(q_blk_ready, 1)

            for b in range(2):
                spread_queries(b, b)
            with pool.Fori(1, B // 2) as i:
                for r in range(2):
                    pool.wait_ge(scores_ready, 2 * GROUPS * i + GROUPS * (r - 1))
                    spread_queries(2 * i + r, r)
            pool.wait_ge(x2_ready, B)
            nc.gpsimd.memset(expert_sel[:], 0.0).then_inc(sel_ready, 1)
            pool.wait_ge(sel_ready, 1)
            nc.gpsimd.affine_select(out=expert_sel[:], in_=expert_sel[:], compare_op=ALU.not_equal, fill=1.0, base=0,
                                    pattern=[[-1, EA], [0, P]], channel_multiplier=1).then_inc(sel_ready, 1)

            def split_expert(e, r):
                pool.wait_ge(raw_in, LOADED * (e + 1))
                if not isinstance(e, int) or e >= 2:
                    pool.wait_ge(hid_used, UNITS * (e - 1))
                for n, (raw, part) in enumerate(((w1_raw, w1_part[r]), (w2_raw, w2_part[r]))):
                    nc.gpsimd.tensor_tensor(part[0][:], raw[:], one[:].unsqueeze(2).broadcast_to(raw.shape),
                                            ALU.mult).then_inc(split_done, 1)
                    pool.wait_ge(split_done, 4 * e + (2 * n + 1))
                    nc.gpsimd.tensor_tensor(part[1][:], raw[:], part[0][:].bitcast(F32), ALU.subtract
                                            ).then_inc(split_done, 1)

            for e in range(2):
                split_expert(e, e)
            with pool.Fori(1, E // 2) as i:
                for r in range(2):
                    split_expert(2 * i + r, r)
            split_expert(E, 0)

        @block.scalar
        def _(act):
            def root(norm, count):
                act.wait_ge(moments_ready, norm)
                nc.scalar.activation(std[:, 0:count], var_eps[:, 0:count], ACT.Sqrt).then_inc(std_ready, 1)

            def copy_out(key, dst, src, func=ACT.Copy, **how):
                job_result(act, key)
                nc.scalar.activation(dst, src, func, **how).then_inc(copied["a"], 1)

            root(1, B)
            for d in range(DIRS):
                for k in range(KD):
                    copy_out(("xnT", d, k, 0), xT[:, d * KD + k, chunk(0)], bank(("xnT", d, k, 0))[:, 0:TQ])
            act.wait_ge(pad_zeroed, 2)

            def copy_u(d, c):
                if d * CT + c >= 2:
                    act.wait_ge(conv_ready, d * CT + c - 1)
                for q in range(Q):
                    copy_out(("u", d, c, q), u_pad[c % 2][:, q * BQ:(q + 1) * BQ, TAPS - 1:],
                             seqs(bank(("u", d, c, q))[:, 0:TQ]))

            def silu_u(d, c):
                act.wait_ge(conv_ready, d * CT + c + 1)
                nc.scalar.activation(u_sb[d][:, c, :], u_sb[d][:, c, :], ACT.Silu).then_inc(u_ready, 1)

            for d in range(DIRS):
                copy_u(d, 0)
                for c in range(1, CT):
                    copy_u(d, c)
                    silu_u(d, c - 1)
                for c in range(CT):
                    for q in range(Q):
                        copy_out(("z", d, c, q), gate[d][:, c, chunk(q)], bank(("z", d, c, q))[:, 0:TQ], ACT.Silu)
                silu_u(d, CT - 1)
            nc.scalar.preload_act_table_set("natural_log_exp_and_others")
            for d in range(DIRS):
                act.wait_ge(log_a_ready, d + 1)
                nc.scalar.activation(neg_a[d][:], neg_a[d][:], ACT.Exp).then_inc(rate_ready, 1)
            steps = 0
            for d in range(DIRS):
                for q in range(Q):
                    copy_out(("rank", d, q), rank_sb[:, d, chunk(q)], bank(("rank", d, q))[0:R, 0:TQ])
                for c in range(CT):
                    g = d * CT + c
                    job_copied(act, ("dt", d, c, Q - 1))
                    if g >= 2:
                        act.wait_ge(dt_ready, g - 1)
                    nc.scalar.activation(ex[g % 2][:], pre[g % 2][:], ACT.Abs).then_inc(act_step, 1)
                    act.wait_ge(act_step, steps + 1)
                    nc.scalar.activation(ex[g % 2][:], ex[g % 2][:], ACT.Exp, scale=-1.0).then_inc(act_step, 1)
                    act.wait_ge(act_step, steps + 2)
                    steps += 2
                    nc.scalar.activation(lg[g % 2][:], ex[g % 2][:], ACT.Ln, bias=1.0).then_inc(log_ready, 1)

            act.wait_ge(decay_zeroed, CT)

            def decays(d, q, first, n, r):
                for c in range(CT):
                    act.wait_ge(neg_a_ready, DIRS)
                    if not (isinstance(n, int) and n < 1):
                        act.wait_ge(scan_done, CT * n + (c - CT + 1))
                    nc.scalar.activation(
                        seqs(decay[c])[:, :, 1:], seqs(dt_sb[d][:, c, chunk(q)])[:, :, 1:],
                        ACT.Exp, scale=neg_a[d][:, bass.ds(n + (c * N - first), 1)]).then_inc(decay_ready, 1)
                act.wait_ge(c_bank_ready, n + 1)
                if not (isinstance(n, int) and n < 2):
                    act.wait_ge(product_ready, n - 1)
                nc.scalar.activation(c_row[r % 2][:], ps[:, 7, 0:TQ], ACT.Copy).then_inc(c_row_ready, 1)

            for r in range(RING):
                decays(0, 0, 0, r, r)
            for s in range(SEG):
                with act.Fori(s == 0, N // RING) as i:
                    for r in range(RING):
                        decays(*divmod(s, Q), s * N, i * RING + (s * N + r), r)

            for d in range(DIRS):
                for h in range(B // 2):
                    copy_out(("mix", d, h), mix_tok[d][:, pair(h), :].rearrange("l b d -> l (b d)"),
                             bank(("mix", d, h))[0:L, :])
            root(2, DIRS * B)
            for d in range(DIRS):
                for k in range(KD):
                    j = d * KD + k
                    copy_out(("mixT", d, k, 1), xT[:, j, chunk(1)], bank(("mixT", d, k, 1))[:, 0:TQ], ACT.Identity,
                             scale=lng_sb[:, j:j + 1], bias=lnb_sb[:, j:j + 1])
            root(3, B)
            for k in range(KD):
                copy_out(("xn2T", k, 1), xn2T[:, k, chunk(1)], bank(("xn2T", k, 1))[:, 0:TQ])
            for m in range(KD):
                copy_out(("qT", m, 1), qT[:, m, chunk(1)], bank(("qT", m, 1))[:, 0:TQ])
            act.wait_ge(probs_zeroed, 2)

            def copy_keys(b, r, m):
                act.wait_ge(k_done, 2 * b + (m + 1))
                nc.scalar.activation(kT[r][:, m, :], ps[:, KEY_BANK, 0:S], ACT.Copy).then_inc(k_copied, 1)

            def exponentials(b, r, g):
                act.wait_ge(shift_ready, GROUPS * b + (g + 1))
                if not isinstance(b, int) or GROUPS * b + g >= 2:
                    act.wait_ge(probsT_ready, GROUPS * b + (g - 1))
                for j in range(2):
                    h = 2 * g + j
                    nc.scalar.activation(probs[g % 2][:, j, 0:S], ps[0:L, g % 2 * 2 + j, 0:S], ACT.Exp,
                                         bias=shift[:, r, h:h + 1], scale=HD ** -0.5,
                                         accum_out=mass[:, r, h:h + 1]).then_inc(probs_ready, 1)

            def copy_probs(b, g):
                act.wait_ge(probsT_ready, GROUPS * b + (g + 1))
                if not isinstance(b, int) or GROUPS * b + g >= 2:
                    act.wait_ge(pv_done, GROUPS * b + (g - 1))
                nc.scalar.activation(probsT[g % 2][1][:], ps[:, 5, 0:KT * L], ACT.Copy).then_inc(probsT_copied[1], 1)

            def attend(b, r, last=False):
                for g in range(2, GROUPS):
                    copy_probs(b, g)
                    if g + 2 < GROUPS:
                        exponentials(b, r, g + 2)
                    elif not last:
                        exponentials(b + 1, 1 - r, g + 2 - GROUPS)
                    if g - 2 in range(KD) and not last:
                        copy_keys(b + 1, 1 - r, g - 2)
                for g in range(0 if last else 2):
                    copy_probs(b + 1, g)
                    exponentials(b + 1, 1 - r, g + 2)

            for m in range(KD):
                copy_keys(0, 0, m)
            exponentials(0, 0, 0)
            exponentials(0, 0, 1)
            for g in range(2):
                copy_probs(0, g)
                exponentials(0, 0, g + 2)
            with act.Fori(0, B // 2 - 1) as i:
                for r in range(2):
                    attend(2 * i + r, r)
            attend(B - 2, 0)
            attend(B - 1, 1, last=True)
            root(4, B)
            for k in range(KD):
                copy_out(("xn3T", k, 1), xn3T[:, k, chunk(1)], bank(("xn3T", k, 1))[:, 0:TQ])
            act.wait_ge(shifted_ready, 1)
            nc.scalar.activation(route["exp"][:], route["shifted"][:], ACT.Exp).then_inc(exp_ready, 1)
            for e in range(EA):
                copy_out(("cwb", e, 1), cw_b[:, e * T + TQ:(e + 1) * T], bank(("cwb", e, 1))[:, 0:TQ])

            def silu_expert(e, r, start):
                act.wait_ge(raw_in, LOADED * (e + 1))
                for u in range(UNITS):
                    ft = u % FT
                    act.wait_ge(hid_ready, UNITS * e + (u + 1))
                    if start + u >= HRING:
                        act.wait_ge(hid_used, UNITS * e + (u - HRING + 1))
                    for dst in (hidden[u % HRING], hid_part[u % HRING][0]):
                        nc.scalar.activation(dst[:], ps[:, u % 4, 0:TQ], ACT.Silu, bias=b1_sb[r][:, ft:ft + 1]
                                             ).then_inc(silu_done, 1)

            with act.Fori(0, E // 2) as i:
                for r in range(2):
                    silu_expert(2 * i + r, r, r * UNITS)
            silu_expert(E, 0, 0)

        @block.tensor
        def _(pe):
            def turned(key, src, how):
                job_bank_free(pe, key)
                q = key[-1]
                for b in range(BQ):
                    mm = nc.tensor.matmul(bank(key)[:, b * L:(b + 1) * L], src(q * BQ + b), how, start=True, stop=True)
                mm.then_inc(job_done, 1)

            def product(key, rows, cols, pairs):
                job_bank_free(pe, key)
                for n, (lhsT, rhs) in enumerate(pairs):
                    mm = nc.tensor.matmul(bank(key)[0:rows, 0:cols], lhsT, rhs, start=(n == 0),
                                          stop=(n == len(pairs) - 1))
                mm.then_inc(job_done, 1)

            def pair_product(key, pairs):
                job_bank_free(pe, key)
                for j in range(2):
                    b = 2 * key[-1] + j
                    for n, (lhsT, rhs) in enumerate(pairs):
                        mm = nc.tensor.matmul(bank(key)[0:L, j * D:(j + 1) * D], lhsT[:, b * L:(b + 1) * L], rhs,
                                              start=(n == 0), stop=(n == len(pairs) - 1))
                mm.then_inc(job_done, 1)

            order = (ident[0:L, 0:L], flip[:])
            pe.wait_ge(consts, CONSTS)
            pe.wait_ge(xn_ready, B)
            for d in range(DIRS):
                for k in range(KD):
                    for q in range(Q):
                        turned(("xnT", d, k, q), lambda b: xn_tok[:, b, tile(k)], order[d])
            for d in range(DIRS):
                pe.wait_ge(win_in[d], 16)
                for k in range(KD):
                    for q in range(Q):
                        job_copied(pe, ("xnT", d, k, q))
                for half, name in enumerate("uz"):
                    for c in range(CT):
                        for q in range(Q):
                            product((name, d, c, q), P, TQ, [
                                (win_sb[d][:, k, half * DI + c * P:half * DI + (c + 1) * P],
                                 xT[:, d * KD + k, chunk(q)]) for k in range(KD)])
            pe.wait_ge(mixw_in, MIXW)
            for d in range(DIRS):
                pe.wait_ge(u_ready, (d + 1) * CT)
                for name, at, rows in (("rank", 0, R), ("B", R, N), ("C", R + N, N)):
                    for q in range(Q):
                        product((name, d, q), rows, TQ, [
                            (wx_sb[d][:, c, at:at + rows], u_sb[d][:, c, chunk(q)]) for c in range(CT)])
                for q in range(Q):
                    job_copied(pe, ("rank", d, q))
                for c in range(CT):
                    for q in range(Q):
                        product(("dt", d, c, q), P, TQ, [(wdt_sb[d][:, tile(c)], rank_sb[:, d, chunk(q)])])

            for key, _ in JOBS[JOB[("dt", DIRS - 1, CT - 1, Q - 1)] - 7:][:8]:
                job_copied(pe, key)
            pe.wait_ge(parts_ready, 2 * DIRS)
            pe.wait_ge(diag_ready, DIRS)

            def row_of(parts, ring_bank, d, q, first, n):
                return nc.tensor.matmul(ps[:, ring_bank, 0:TQ],
                                        row_sel[:, bass.ds(n - first, 1), :].rearrange("p n m -> p (n m)"),
                                        parts[d][:, chunk(q)], start=True, stop=True)

            def b_row(n, s):
                if not (isinstance(n, int) and n < 1):
                    pe.wait_ge(inflow_ready, n)
                row_of(b_parts, 6, *divmod(s, Q), s * N, n).then_inc(b_bank_ready, 1)

            def c_row_bank(n, s):
                if not (isinstance(n, int) and n < 1):
                    pe.wait_ge(c_row_ready, n)
                row_of(c_parts, 7, *divmod(s, Q), s * N, n).then_inc(c_bank_ready, 1)

            def sum_state(n, r, last=False):
                pe.wait_ge(product_ready, n + 1)
                for c in range(CT):
                    mm = nc.tensor.matmul(ps[:, c, 0:TQ], ident[:], states[r][:, c * TQ:(c + 1) * TQ],
                                          start=False, stop=last, skip_group_check=True)
                mm.then_inc(y_summed, 1)

            def step_of(n, r, s, opening=False, closing=False):
                left = N - RING + r if closing else r if isinstance(n, int) else 0
                for lead, row in ((3, b_row), (2, c_row_bank)):
                    ahead = s + (left + lead >= N)
                    if ahead < SEG:
                        row(n + lead, ahead)
                if opening:
                    if s:
                        pe.wait_ge(y_gated, CT * s)
                    d, q = divmod(s, Q)
                    for c in range(CT):
                        nc.tensor.matmul(ps[:, c, 0:TQ], diag_d[d][:, c, :], u_sb[d][:, c, chunk(q)], start=True,
                                         stop=False, skip_group_check=True)
                sum_state(n, r, closing and r == RING - 1)

            for n in range(3):
                b_row(n, 0)
                if n < 2:
                    c_row_bank(n, 0)
            for s in range(SEG):
                for r in range(RING):
                    step_of(s * N + r, r, s, opening=r == 0)
                with pe.Fori(1, N // RING - 1) as i:
                    for r in range(RING):
                        step_of(i * RING + (s * N + r), r, s)
                for r in range(RING):
                    step_of(s * N + N - RING + r, r, s, closing=True)

            pe.wait_ge(y_gated, CT * SEG)
            for d in range(DIRS):
                for h in range(B // 2):
                    pair_product(("mix", d, h), [(u_sb[d][:, c, :], wout_sb[d][:, c, :]) for c in range(CT)])
            pe.wait_ge(xn_ready, (1 + DIRS) * B)
            for d in range(DIRS):
                for k in range(KD):
                    for q in range(Q):
                        turned(("mixT", d, k, q), lambda b: mix_tok[d][:, b, tile(k)], order[d])
            for d in range(DIRS):
                for k in range(KD):
                    for q in range(Q):
                        job_copied(pe, ("mixT", d, k, q))
            for h in range(B // 2):
                pair_product(("fuse", h), [(xT[:, j, :], wfuse_sb[:, j, :]) for j in range(DIRS * KD)])
            pe.wait_ge(xn_ready, (1 + DIRS + 1) * B)
            for k in range(KD):
                for q in range(Q):
                    turned(("xn2T", k, q), lambda b: xn_tok[:, b, tile(k)], order[0])
            pe.wait_ge(attnw_in, 16 * 4)
            for k in range(KD):
                for q in range(Q):
                    job_copied(pe, ("xn2T", k, q))
            for m in range(KD):
                for q in range(Q):
                    product(("qT", m, q), P, TQ, [(wq_sb[:, k, tile(m)], xn2T[:, k, chunk(q)]) for k in range(KD)])
            for m in range(KD):
                for q in range(Q):
                    job_copied(pe, ("qT", m, q))

            def keys(b, r, loads, m):
                if m == 0:
                    pe.wait_ge(ctx_in[r], 16 * loads)
                    if not isinstance(b, int) or b > 0:
                        pe.wait_ge(x2_ready, b - 1)
                else:
                    pe.wait_ge(k_copied, 2 * b + m)
                for k in range(KD):
                    mm = nc.tensor.matmul(ps[:, KEY_BANK, 0:S], wk_sb[:, k, tile(m)], ctx_sb[r][:, k, :],
                                          start=(k == 0), stop=(k == KD - 1))
                mm.then_inc(k_done, 1)

            def values(b, r, part):
                if part == 0:
                    pe.wait_ge(k_copied, 2 * b + KD)
                else:
                    pe.wait_ge(v_copied, 2 * b + part)
                for kt in ((0, 1), (2,))[part]:
                    size = P if kt < KT - 1 else SL
                    for k in range(KD):
                        mm = nc.tensor.matmul(ps[0:size, KEY_BANK, kt % 2 * D:(kt % 2 + 1) * D],
                                              ctx_sb[r][:, k, kt * P:kt * P + size], wv_sb[:, k, :],
                                              start=(k == 0), stop=(k == KD - 1))
                mm.then_inc(v_done, 1)

            def scores(b, r, g):
                m = 2 * g // HT
                pe.wait_ge(q_blk_ready, KD * b + (m + 1))
                if g % (GROUPS // KD) == 0:
                    pe.wait_ge(k_copied, 2 * b + (m + 1))
                if not isinstance(b, int) or GROUPS * b + g >= 2:
                    pe.wait_ge(probs_ready, 2 * GROUPS * b + (2 * g - 2))
                for j in range(2):
                    mm = nc.tensor.matmul(ps[0:L, g % 2 * 2 + j, 0:S], q_blk[r][:, m, (2 * g + j) % HT, :],
                                          kT[r][:, m, :], start=True, stop=True)
                mm.then_inc(scores_ready, 1)

            def turn_probs(b, g):
                pe.wait_ge(probs_ready, 2 * GROUPS * b + (2 * g + 2))
                if not isinstance(b, int) or GROUPS * b + g >= 1:
                    for by in probsT_copied:
                        pe.wait_ge(by, GROUPS * b + g)
                for j in range(2):
                    for kt in range(KT):
                        mm = nc.tensor.transpose(ps[:, 4 + j, kt * L:(kt + 1) * L], probs[g % 2][:, j, tile(kt)],
                                                 ident[0:L, 0:L])
                mm.then_inc(probsT_ready, 1)

            def weigh_values(b, r, g):
                for by in probsT_copied:
                    pe.wait_ge(by, GROUPS * b + (g + 1))
                if g == 0:
                    pe.wait_ge(v_copied, 2 * b + 2)
                    if not isinstance(b, int) or b > 0:
                        pe.wait_ge(heads_ready, b)
                for j in range(2):
                    h = 2 * g + j
                    for kt in range(KT):
                        size = P if kt < KT - 1 else SL
                        mm = nc.tensor.matmul(ps[0:L, 6, h * HD:(h + 1) * HD],
                                              probsT[g % 2][j][0:size, kt * L:(kt + 1) * L],
                                              v_sb[r][0:size, kt, h * HD:(h + 1) * HD],
                                              start=(kt == 0), stop=(kt == KT - 1))
                mm.then_inc(pv_done, 1)

            def turn_heads(b):
                pe.wait_ge(heads_ready, b + 1)
                for m in range(KD):
                    mm = nc.tensor.transpose(ps[:, KEY_BANK, m * L:(m + 1) * L], heads_tok[:, tile(m)],
                                             ident[0:L, 0:L])
                mm.then_inc(headsT_done, 1)

            def project_heads(b):
                pe.wait_ge(headsT_copied, b + 1)
                for m in range(KD):
                    mm = nc.tensor.matmul(ps[0:L, KEY_BANK, 0:D], headsT[:, m, :], wo_sb[:, m, :], start=(m == 0),
                                          stop=(m == KD - 1))
                mm.then_inc(wo_done, 1)

            def attend(b, r, next_loads=None):
                nxt = (b + 1, 1 - r)
                for g in range(2, GROUPS):
                    turn_probs(b, g)
                    if g + 2 < GROUPS:
                        scores(b, r, g + 2)
                    elif next_loads is not None:
                        scores(*nxt, g + 2 - GROUPS)
                    weigh_values(b, r, g)
                    if next_loads is not None:
                        if g - 2 < KD:
                            keys(*nxt, next_loads, g - 2)
                        elif g - 4 < 2:
                            values(*nxt, g - 4)
                if next_loads is None:
                    turn_heads(b)
                    project_heads(b)
                else:
                    turn_probs(b + 1, 0)
                    scores(*nxt, 2)
                    turn_heads(b)
                    weigh_values(*nxt, 0)
                    turn_probs(b + 1, 1)
                    scores(*nxt, 3)
                    project_heads(b)
                    weigh_values(*nxt, 1)

            for m in range(KD):
                keys(0, 0, 1, m)
            for part in range(2):
                values(0, 0, part)
            scores(0, 0, 0)
            scores(0, 0, 1)
            for g in range(2):
                turn_probs(0, g)
                scores(0, 0, g + 2)
                weigh_values(0, 0, g)
            with pe.Fori(0, B // 2 - 1) as i:
                attend(2 * i, 0, i + 1)
                attend(2 * i + 1, 1, i + 2)
            attend(B - 2, 0, B // 2)
            attend(B - 1, 1)

            pe.wait_ge(xn_ready, (1 + DIRS + 2) * B)
            for k in range(KD):
                for q in range(Q):
                    turned(("xn3T", k, q), lambda b: xn_tok[:, b, tile(k)], order[0])
            for k in range(KD):
                for q in range(Q):
                    job_copied(pe, ("xn3T", k, q))
            pe.wait_ge(moew_in, MOEW)
            job_bank_free(pe, ("logits",))
            for b in range(B):
                for k in range(KD):
                    mm = nc.tensor.matmul(bank(("logits",))[0:L, b * E:(b + 1) * E], xn3T[:, k, b * L:(b + 1) * L],
                                          wg_sb[:, k, :], start=(k == 0), stop=(k == KD - 1))
            mm.then_inc(job_done, 1)
            pe.wait_ge(cw_ready, 1)
            for q in range(Q):
                job_bank_free(pe, ("cwT", q))
                for b in range(BQ):
                    mm = nc.tensor.matmul(bank(("cwT", q))[0:EA, b * L:(b + 1) * L], cw_tok[:, q * BQ + b, :],
                                          ident[0:L, 0:L], start=True, stop=True)
                mm.then_inc(job_done, 1)
            for q in range(Q):
                job_copied(pe, ("cwT", q))
            pe.wait_ge(sel_ready, 2)
            for e in range(EA):
                for q in range(Q):
                    product(("cwb", e, q), P, TQ, [(expert_sel[:, e, :], cwT[:, chunk(q)])])
            for key, _ in JOBS[JOB[("cwb", EA - 1, Q - 1)] - 7:][:8]:
                job_copied(pe, key)

            for q in range(Q):
                for m in range(KD):
                    mm = nc.tensor.matmul(ps[:, 4 + 2 * q + m, 0:TQ], b2_sb[:, tile(m)], cwT[:, chunk(q)], start=True,
                                          stop=True)
                mm.then_inc(bias_summed, 1)
            pe.wait_ge(xn3_split, KD)

            def three(to, w, x, first, last):
                for n, (i, j) in enumerate(((0, 0), (0, 1), (1, 0))):
                    mm = nc.tensor.matmul(to, w[i], x[j], start=(first and n == 0), stop=(last and n == 2))
                return mm

            def experts(turns):
                units = [(e, r, u) for e, r in turns for u in range(UNITS)]

                def into_hidden(at):
                    e, r, u = units[at]
                    q, ft = divmod(u, FT)
                    if u == 0:
                        pe.wait_ge(split_done, 4 * e + 4)
                    if at >= 4:
                        pe.wait_ge(silu_done, 2 * UNITS * e + 2 * (u - 3))
                    for k in range(KD):
                        mm = three(ps[:, u % 4, 0:TQ], [part[:, k, tile(ft)] for part in w1_part[r]],
                                   [part[:, k, chunk(q)] for part in xn3_part], k == 0, k == KD - 1)
                    mm.then_inc(hid_ready, 1)

                def out_of_hidden(at):
                    e, r, u = units[at]
                    q, ft = divmod(u, FT)
                    if ft == 0:
                        pe.wait_ge(y_taken, Q * e + (q + 1))
                    pe.wait_ge(hid_split, UNITS * e + (u + 1))
                    for m in range(KD):
                        mm = three(ps[:, 4 + 2 * q + m, 0:TQ], [part[:, ft, tile(m)] for part in w2_part[r]],
                                   [part[:] for part in hid_part[u % HRING]], ft == 0, ft == FT - 1)
                    mm.then_inc(hid_used, 1)

                for at in range(len(units) + LAG):
                    if at < len(units):
                        into_hidden(at)
                    if at >= LAG:
                        out_of_hidden(at - LAG)

            with pe.Fori(0, E // 2) as i:
                experts([(2 * i, 0), (2 * i + 1, 1)])
            experts([(E, 0)])
            pe.wait_ge(yT_ready, Q * EA)
            for h in range(B // 2):
                key = ("out", h)
                for j in range(2):
                    b = 2 * h + j
                    for m in range(KD):
                        mm = nc.tensor.transpose(bank(key)[0:L, j * D + m * P:j * D + (m + 1) * P],
                                                 yT[:, m, b * L:(b + 1) * L], ident[:])
                mm.then_inc(job_done, 1)

        @block.vector
        def _(dve):
            steps = 0

            def step(ins):
                nonlocal steps
                ins.then_inc(dve_step, 1)
                steps += 1
                dve.wait_ge(dve_step, steps)

            def later(ins):
                nonlocal steps
                ins.then_inc(dve_step, 1)
                steps += 1

            norms = 0

            def layer_norm(pairs):
                nonlocal norms
                norms += 1
                n = len(pairs)
                for j, (src, _) in enumerate(pairs):
                    later(nc.vector.bn_stats(stats[:, j, :], src))
                dve.wait_ge(dve_step, steps)
                for j in range(n):
                    later(nc.vector.bn_aggr(moments[:, j, :], stats[:, j, :]))
                dve.wait_ge(dve_step, steps)
                nc.vector.tensor_scalar(var_eps[:, 0:n], moments[:, 0:n, 1], EPS, None, ALU.add
                                        ).then_inc(moments_ready, 1)
                dve.wait_ge(std_ready, norms)
                step(nc.vector.reciprocal(rstd[:, 0:n], std[:, 0:n]))
                for j, (src, dst) in enumerate(pairs):
                    nc.vector.tensor_scalar(dst, src, moments[:, j, 0:1], rstd[:, j:j + 1], ALU.subtract, ALU.mult
                                            ).then_inc(xn_ready, 1)

            def copy_out(key, dst, src):
                job_result(dve, key)
                nc.vector.tensor_copy(dst, src).then_inc(copied["v"], 1)

            for r in range(2):
                nc.vector.memset(u_pad[r][:, :, 0:TAPS - 1], 0.0).then_inc(pad_zeroed, 1)
            dve.wait_ge(x_in, 16)
            layer_norm([(x_tok[:, b, :], xn_tok[:, b, :]) for b in range(B)])
            for d in range(DIRS):
                for k in range(KD):
                    copy_out(("xnT", d, k, 1), xT[:, d * KD + k, chunk(1)], bank(("xnT", d, k, 1))[:, 0:TQ])
            dve.wait_ge(vec_in, 16 * DIRS)
            dve.wait_ge(consts, CONSTS)
            for d in range(DIRS):
                for c in range(CT):
                    ins = nc.vector.tensor_scalar(diag_d[d][:, c, :], ident[:], vec_sb[d][:, c, V_D:V_D + 1], None,
                                                  ALU.mult)
                ins.then_inc(diag_ready, 1)
            for d in range(DIRS):
                nc.vector.tensor_scalar(neg_a[d][:].rearrange("p (c n) -> p c n", c=CT), vec_sb[d][:, :, V_ALOG:],
                                        LOG_MAX, None, ALU.min).then_inc(log_a_ready, 1)
            dve.wait_ge(pad_zeroed, 2)
            for d in range(DIRS):
                for c in range(CT):
                    for q in range(Q):
                        job_copied(dve, ("u", d, c, q))
                    padded, to = u_pad[c % 2], seqs(u_sb[d][:, c, :])
                    tap = [vec_sb[d][:, c, V_TAP + k:V_TAP + k + 1] for k in range(TAPS)]
                    step(nc.vector.tensor_scalar(to, padded[:, :, TAPS - 1:], tap[TAPS - 1],
                                                 vec_sb[d][:, c, V_CONVB:V_CONVB + 1], ALU.mult, ALU.add))
                    for k in range(TAPS - 1):
                        ins = nc.vector.scalar_tensor_tensor(to, padded[:, :, k:k + L], tap[k], to, ALU.mult, ALU.add)
                        if k < TAPS - 2:
                            step(ins)
                    ins.then_inc(conv_ready, 1)
            for d in range(DIRS):
                dve.wait_ge(rate_ready, d + 1)
                nc.vector.tensor_scalar(neg_a[d][:], neg_a[d][:], -1.0, None, ALU.mult
                                        ).then_inc(neg_a_ready, 1)

            def step_size(g):
                d, c = divmod(g, CT)
                p, e, l = pre[g % 2][:], ex[g % 2][:], lg[g % 2][:]
                dve.wait_ge(log_ready, g + 1)
                step(nc.vector.scalar_tensor_tensor(l, p, 0.0, l, ALU.max, ALU.add))
                step(nc.vector.tensor_scalar(p, e, 1.0, -1.0, ALU.add, ALU.add))
                step(nc.vector.tensor_tensor(e, e, p, ALU.subtract))
                nc.vector.tensor_tensor(dt_sb[d][:, c, :], l, e, ALU.add).then_inc(dt_ready, 1)

            for d in range(DIRS):
                for name in "BC":
                    part = parts[name][d]
                    for q in range(Q):
                        copy_out((name, d, q), rows_f[:, chunk(q)], bank((name, d, q))[0:N, 0:TQ])
                    job_copied(dve, (name, d, Q - 1))
                    step(nc.vector.tensor_copy(part[0:N, :], rows_f))
                    step(nc.vector.tensor_tensor(rest_f, rows_f, part[0:N, :], ALU.subtract))
                    step(nc.vector.tensor_copy(part_mid[:], rest_f))
                    later(nc.vector.tensor_copy(part[N:2 * N, :], part_mid[:]))
                    dve.wait_ge(dve_step, steps)
                    nc.vector.tensor_tensor(part[2 * N:3 * N, :], rest_f, part_mid[:], ALU.subtract
                                            ).then_inc(parts_ready, 1)
                for c in range(CT):
                    g = d * CT + c
                    for q in range(Q):
                        key = ("dt", d, c, q)
                        job_result(dve, key)
                        nc.vector.tensor_scalar(pre[g % 2][:, chunk(q)], bank(key)[:, 0:TQ],
                                                vec_sb[d][:, c, V_BDT:V_BDT + 1], None, ALU.add
                                                ).then_inc(copied["v"], 1)
                    if g:
                        step_size(g - 1)
            step_size(DIRS * CT - 1)
            for c in range(CT):
                nc.vector.memset(seqs(decay[c])[:, :, 0:1], 0.0).then_inc(decay_zeroed, 1)
            dve.wait_ge(decay_zeroed, CT)

            def inflow(d, q, n, r):
                dve.wait_ge(b_bank_ready, n + 1)
                if not (isinstance(n, int) and n < RING):
                    dve.wait_ge(y_summed, n - (RING - 1))
                nc.vector.tensor_tensor(states[r][:].rearrange("p (c t) -> p c t", c=CT), dtu[d][:, :, chunk(q)],
                                        ps[:, 6:7, 0:TQ].broadcast_to([P, CT, TQ]), ALU.mult
                                        ).then_inc(inflow_ready, 1)

            def recur(n, r):
                dve.wait_ge(inflow_ready, n + 1)
                for c in range(CT):
                    dve.wait_ge(decay_ready, CT * n + (c + 1))
                    st = states[r][:, c * TQ:(c + 1) * TQ]
                    nc.vector.tensor_tensor_scan(st, decay[c], st, 0.0, ALU.mult, ALU.add).then_inc(scan_done, 1)

            def gated(s):
                d, q = divmod(s, Q)
                dve.wait_ge(y_summed, (s + 1) * N)
                for c in range(CT):
                    nc.vector.tensor_tensor(u_sb[d][:, c, chunk(q)], ps[:, c, 0:TQ], gate[d][:, c, chunk(q)], ALU.mult
                                            ).then_inc(y_gated, 1)

            dve.wait_ge(dtu_ready, DIRS * CT)
            inflow(0, 0, 0, 0)
            for s in range(SEG):
                d, q = divmod(s, Q)
                for r in range(RING):
                    inflow(d, q, s * N + r + 1, (r + 1) % RING)
                    recur(s * N + r, r)
                    if s and r == 1:
                        gated(s - 1)
                with dve.Fori(1, N // RING - 1) as i:
                    for r in range(RING):
                        inflow(d, q, i * RING + (s * N + r + 1), (r + 1) % RING)
                        recur(i * RING + (s * N + r), r)
                for r in range(RING):
                    n = s * N + N - RING + r
                    if r + 1 < RING:
                        inflow(d, q, n + 1, r + 1)
                    elif s + 1 < SEG:
                        inflow(*divmod(s + 1, Q), n + 1, 0)
                    recur(n, r)
            gated(SEG - 1)

            for d in range(DIRS):
                for h in range(B // 2):
                    job_copied(dve, ("mix", d, h))
            layer_norm([(mix_tok[d][:, b, :], mix_tok[d][:, b, :]) for d in range(DIRS) for b in range(B)])
            for d in range(DIRS):
                for k in range(KD):
                    j, key = d * KD + k, ("mixT", d, k, 0)
                    job_result(dve, key)
                    nc.vector.tensor_scalar(xT[:, j, chunk(0)], bank(key)[:, 0:TQ], lng_sb[:, j:j + 1],
                                            lnb_sb[:, j:j + 1], ALU.mult, ALU.add).then_inc(copied["v"], 1)

            def add_to(dst, src, key):
                job_result(dve, key)
                h = pair(key[-1])
                return nc.vector.tensor_tensor(dst[:, h, :].rearrange("l b d -> l (b d)"),
                                               src[:, h, :].rearrange("l b d -> l (b d)"), bank(key)[0:L, :], ALU.add)

            dve.wait_ge(bias_added, 1)
            for h in range(B // 2):
                add_to(x_tok, x_tok, ("fuse", h)).then_inc(copied["v"], 1)
            job_copied(dve, ("fuse", B // 2 - 1))
            layer_norm([(x_tok[:, b, :], xn_tok[:, b, :]) for b in range(B)])
            for k in range(KD):
                copy_out(("xn2T", k, 0), xn2T[:, k, chunk(0)], bank(("xn2T", k, 0))[:, 0:TQ])
            for m in range(KD):
                copy_out(("qT", m, 0), qT[:, m, chunk(0)], bank(("qT", m, 0))[:, 0:TQ])
            dve.wait_ge(bias_added, 2)

            def copy_values(b, r, part):
                dve.wait_ge(v_done, 2 * b + (part + 1))
                if part == 0:
                    ins = nc.vector.tensor_copy(v_sb[r][:, 0:2, :].rearrange("p k d -> p (k d)"), ps[:, KEY_BANK, :])
                else:
                    ins = nc.vector.tensor_copy(v_sb[r][0:SL, 2, :], ps[0:SL, KEY_BANK, 0:D])
                ins.then_inc(v_copied, 1)

            def maxima(b, r, g):
                dve.wait_ge(scores_ready, GROUPS * b + (g + 1))
                nc.vector.tensor_reduce(neg_max[:, r, 2 * g:2 * g + 2], ps[0:L, g % 2 * 2:g % 2 * 2 + 2, 0:S],
                                        AX.X, ALU.max).then_inc(max_ready, 1)
                dve.wait_ge(max_ready, GROUPS * b + (g + 1))
                nc.vector.tensor_scalar(shift[:, r, 2 * g:2 * g + 2], neg_max[:, r, 2 * g:2 * g + 2],
                                        -HD ** -0.5, None, ALU.mult).then_inc(shift_ready, 1)

            def copy_probs(b, g):
                dve.wait_ge(probsT_ready, GROUPS * b + (g + 1))
                if not isinstance(b, int) or GROUPS * b + g >= 2:
                    dve.wait_ge(pv_done, GROUPS * b + (g - 1))
                nc.vector.tensor_copy(probsT[g % 2][0][:], ps[:, 4, 0:KT * L]).then_inc(probsT_copied[0], 1)

            def normalise_heads(b, r):
                dve.wait_ge(probs_ready, 2 * GROUPS * b + 2 * GROUPS)
                nc.vector.reciprocal(inv_mass[:, r, :], mass[:, r, :]).then_inc(inv_mass_ready, 1)
                dve.wait_ge(inv_mass_ready, b + 1)
                dve.wait_ge(pv_done, GROUPS * b + GROUPS)
                nc.vector.tensor_tensor(heads_tok[:].rearrange("l (h e) -> l h e", h=H),
                                        ps[0:L, 6, 0:D].rearrange("l (h e) -> l h e", h=H),
                                        inv_mass[:, r, :].unsqueeze(2).broadcast_to([L, H, HD]), ALU.mult
                                        ).then_inc(heads_ready, 1)

            def copy_heads(b):
                dve.wait_ge(headsT_done, b + 1)
                nc.vector.tensor_copy(headsT[:].rearrange("p m t -> p (m t)"), ps[:, KEY_BANK, 0:KD * L]
                                      ).then_inc(headsT_copied, 1)

            def add_attention(b):
                dve.wait_ge(wo_done, b + 1)
                x2 = x_tok[:, bass.ds(b, 1), :].rearrange("l b d -> l (b d)")
                nc.vector.tensor_tensor(x2, x2, ps[0:L, KEY_BANK, 0:D], ALU.add).then_inc(x2_ready, 1)

            def attend(b, r, last=False):
                for g in range(2, GROUPS):
                    copy_probs(b, g)
                    if g + 2 < GROUPS:
                        maxima(b, r, g + 2)
                    elif not last:
                        maxima(b + 1, 1 - r, g + 2 - GROUPS)
                    if g - 4 in range(2) and not last:
                        copy_values(b + 1, 1 - r, g - 4)
                normalise_heads(b, r)
                if not last:
                    copy_probs(b + 1, 0)
                    maxima(b + 1, 1 - r, 2)
                copy_heads(b)
                if not last:
                    copy_probs(b + 1, 1)
                    maxima(b + 1, 1 - r, 3)
                add_attention(b)

            for part in range(2):
                copy_values(0, 0, part)
            maxima(0, 0, 0)
            maxima(0, 0, 1)
            for g in range(2):
                copy_probs(0, g)
                maxima(0, 0, g + 2)
            with dve.Fori(0, B // 2 - 1) as i:
                for r in range(2):
                    attend(2 * i + r, r)
            attend(B - 2, 0)
            attend(B - 1, 1, last=True)
            dve.wait_ge(x2_ready, B)
            layer_norm([(x_tok[:, b, :], xn_tok[:, b, :]) for b in range(B)])
            for k in range(KD):
                copy_out(("xn3T", k, 0), xn3T[:, k, chunk(0)], bank(("xn3T", k, 0))[:, 0:TQ])
            for k in range(KD):
                for q in range(Q):
                    job_copied(dve, ("xn3T", k, q))
                step(nc.vector.tensor_copy(xn3_part[0][:, k, :], xn3T[:, k, :]))
                nc.vector.tensor_tensor(xn3_part[1][:, k, :], xn3T[:, k, :], xn3_part[0][:, k, :].bitcast(F32),
                                        ALU.subtract).then_inc(xn3_split, 1)

            job_result(dve, ("logits",))
            logits = bank(("logits",))[0:L, 0:B * E].rearrange("l (b e) -> l b e", e=E)
            rt, tk = route, per_tok
            step(nc.vector.tensor_reduce(tk["max"][:, :, 0], logits, AX.X, ALU.max))
            nc.vector.tensor_tensor(rt["shifted"][:], logits, spread(tk["max"][:], E), ALU.subtract
                                    ).then_inc(copied["v"], 1)
            job_copied(dve, ("logits",))
            nc.vector.memset(cw_tok[:, :, E:EA], SHARED).then_inc(shifted_ready, 1)
            dve.wait_ge(exp_ready, 1)
            step(nc.vector.tensor_reduce(tk["sum"][:, :, 0], rt["exp"][:], AX.X, ALU.add))
            step(nc.vector.reciprocal(tk["inv"][:], tk["sum"][:]))
            step(nc.vector.tensor_tensor(rt["prob"][:], rt["exp"][:], spread(tk["inv"][:], E), ALU.mult))
            prefer_all = prefer[:].unsqueeze(1).broadcast_to([L, B, E])

            def largest(src, top, pick, chosen):
                step(nc.vector.tensor_reduce(top[:, :, 0], src, AX.X, ALU.max))
                step(nc.vector.tensor_tensor(rt["tie"][:], src, spread(top[:], E), ALU.is_equal))
                step(nc.vector.tensor_tensor(rt["tie"][:], rt["tie"][:], prefer_all, ALU.mult))
                step(nc.vector.tensor_reduce(pick[:, :, 0], rt["tie"][:], AX.X, ALU.max))
                step(nc.vector.tensor_tensor(chosen, rt["tie"][:], spread(pick[:], E), ALU.is_equal))

            largest(rt["prob"][:], tk["top1"], tk["pick1"], rt["first"][:])
            step(nc.vector.scalar_tensor_tensor(rt["rest"][:], rt["first"][:], -4.0, rt["prob"][:], ALU.mult, ALU.add))
            largest(rt["rest"][:], tk["top2"], tk["pick2"], rt["second"][:])
            step(nc.vector.tensor_tensor(rt["both"][:], rt["first"][:], rt["second"][:], ALU.add))
            step(nc.vector.tensor_tensor(rt["kept"][:], rt["both"][:], rt["prob"][:], ALU.mult))
            step(nc.vector.scalar_tensor_tensor(tk["den"][:, :, 0], tk["top1"][:, :, 0], 1e-9, tk["top2"][:, :, 0],
                                                ALU.add, ALU.add))
            step(nc.vector.reciprocal(tk["inv_den"][:], tk["den"][:]))
            nc.vector.tensor_tensor(cw_tok[:, :, 0:E], rt["kept"][:], spread(tk["inv_den"][:], E), ALU.mult
                                    ).then_inc(cw_ready, 1)
            for q in range(Q):
                copy_out(("cwT", q), cwT[:, chunk(q)], bank(("cwT", q))[0:EA, 0:TQ])
            for e in range(EA):
                copy_out(("cwb", e, 0), cw_b[:, e * T:e * T + TQ], bank(("cwb", e, 0))[:, 0:TQ])
            job_copied(dve, ("cwb", EA - 1, 0))
            job_copied(dve, ("cwb", EA - 1, 1))

            for q in range(Q):
                dve.wait_ge(bias_summed, q + 1)
                nc.vector.tensor_copy(yT[:, :, chunk(q)], ps[:, 4 + 2 * q:6 + 2 * q, 0:TQ]).then_inc(y_taken, 1)
            dve.wait_ge(y_taken, Q)

            def split_hidden(e, u):
                dve.wait_ge(silu_done, 2 * UNITS * e + 2 * (u + 1))
                high, low = hid_part[u % HRING]
                nc.vector.tensor_tensor(low[:], hidden[u % HRING][:], high[:].bitcast(F32), ALU.subtract
                                        ).then_inc(hid_split, 1)

            def add_expert(e, q):
                dve.wait_ge(hid_used, UNITS * e + FT * (q + 1))
                nc.vector.tensor_tensor(
                    weighted[:], ps[:, 4 + 2 * q:6 + 2 * q, 0:TQ],
                    cw_b[:, bass.ds(T * e + TQ * q, TQ)].unsqueeze(1).broadcast_to([P, KD, TQ]), ALU.mult
                    ).then_inc(y_taken, 1)
                dve.wait_ge(y_taken, Q * e + (Q + q + 1))
                nc.vector.tensor_tensor(yT[:, :, chunk(q)], yT[:, :, chunk(q)], weighted[:], ALU.add
                                        ).then_inc(yT_ready, 1)

            def experts(turns):
                units = [(e, u) for e in turns for u in range(UNITS)]
                for at, (e, u) in enumerate(units):
                    split_hidden(e, u)
                    if at >= FT and u % FT == LAG:
                        before, v = units[at - LAG - 1]
                        add_expert(before, v // FT)
                add_expert(turns[-1], Q - 1)

            with dve.Fori(0, E // 2) as i:
                experts([2 * i, 2 * i + 1])
            experts([E])
            dve.wait_ge(yT_ready, Q * EA)
            for h in range(B // 2):
                add_to(out_tok, x_tok, ("out", h)).then_inc(out_ready, 1)


_OUT = (B, L, D)


def _laid_out(inputs):
    a = {k: np.asarray(v) for k, v in inputs.items()}

    def per_channel(*columns):
        rows = np.concatenate([c.reshape(DI, -1) for c in columns], axis=1)
        return rows.reshape(CT, P, -1).transpose(1, 0, 2)

    def both(make):
        return np.stack([make(lambda name: a[f"L0_attn_{name}_{s}"]) for s in "fb"])

    def per_feature(name):
        return both(lambda w: w(name)).reshape(DIRS * KD, P).T

    def with_shared(routed, shared):
        return np.concatenate([a[f"L0_ffn_{routed}"], a[f"L0_ffn_{shared}"][None]])

    arrays = {
        "x": a["x"],
        "ctxT": a["ctx_1024"].transpose(0, 2, 1),
        "winT": both(lambda w: w("Win").T),
        "wxT": both(lambda w: w("Wx").T),
        "wdtT": both(lambda w: w("Wdt").T),
        "woutT": both(lambda w: w("Wout").T),
        "vec": both(lambda w: per_channel(w("convw"), w("convb"), w("bdt"), w("Dp"), w("Alog"))),
        "ln_g": per_feature("ln_g"),
        "ln_b": per_feature("ln_b"),
        "wfuseT": a["L0_attn_Wfuse"].T,
        "bfuse": a["L0_attn_bfuse"],
        "wqT": a["L0_xattn_Wq"].T,
        "wkT": a["L0_xattn_Wk"].T,
        "wvT": a["L0_xattn_Wv"].T,
        "woT": a["L0_xattn_Wo"].T,
        "bo": a["L0_xattn_bo"],
        "wg": a["L0_ffn_Wg"],
        "w1": with_shared("W1", "Ws1"),
        "b1": with_shared("b1", "bs1").reshape(EA, FT, P).transpose(0, 2, 1),
        "w2": with_shared("W2", "Ws2"),
        "b2": with_shared("b2", "bs2"),
    }
    return {k: np.ascontiguousarray(v) for k, v in arrays.items()}


def kernel(**inputs):
    from concourse import bacc
    from concourse.bass_utils import run_bass_kernel_spmd

    arrays = _laid_out(inputs)
    nc = bacc.Bacc("TRN2", target_bir_lowering=False, num_devices=1)
    aps = {k: nc.dram_tensor(f"in_{k}", v.shape, mybir.dt.from_np(v.dtype), kind="ExternalInput").ap()
           for k, v in arrays.items()}
    out = nc.dram_tensor("out_x", _OUT, F32, kind="ExternalOutput").ap()
    decoder_layer(nc, **aps, out=out)
    result = run_bass_kernel_spmd(nc, [{f"in_{k}": v for k, v in arrays.items()}], core_ids=[0])
    return result.results[0]["out_x"]
```

```python
from contextlib import ExitStack

import numpy as np

import concourse.bass as bass
from concourse import mybir

F32 = mybir.dt.float32
F32R = mybir.dt.float32r
BF16 = mybir.dt.bfloat16
ALU = mybir.AluOpType
ACT = mybir.ActivationFunctionType
AX = mybir.AxisListType

P = 128
B, L, D = 8, 100, 256
T = B * L
KD = D // P
DI = 2 * D
CT = DI // P
N = 32
R = D // 16
TAPS = 4
S = 361
KT = -(-S // P)
SE = S + S % 2
SL = S - (KT - 1) * P
H = 16
HD = D // H
HT = H // KD
F = 1024
FT = F // P
E = 8
EA = E + 1
EPS = 1e-5
SHARED = 0.1
LOG_MAX = 82.0
Q = 2
BQ = B // Q
TQ = T // Q
DIRS = 2
PADS = 4
RING = 4
SEG = DIRS * Q
POOL_TILES = (0, 1)
BANK = 512
UNITS = FT * Q
SPREADS = EA + KD
HRING = 4
LAG = 3
GROUPS = H // 2
LOGITS_AT, EXP_AT, ROWS_AT = 1, 2, 8
SPREAD_AT = {10: (0, 1), 11: (2, 3), 12: (4, 5), 13: (6, 7), 14: (8, 9), 15: (10,)}
FIRST_SUM_AT = 14
assert sum(len(v) for v in SPREAD_AT.values()) == SPREADS
KEY_BANK = 7
FIRST_KEYS, FIRST_VALUES = (0, 1), (4, 5)
CONSTS = 12 + E
TURNS = 4
MIXW, MOEW = 16 * 11, 16 * 3
PIECES = 2 * (KD + 2)
LOADED = 16 * 2

V_TAP, V_CONVB, V_BDT, V_D, V_ALOG = 0, TAPS, TAPS + 1, TAPS + 2, TAPS + 3
VEC = TAPS + 3 + N


def bank_jobs():
    jobs = []
    for q in range(Q):
        for d in range(DIRS):
            for k in range(KD):
                jobs.append((("xnT", d, k, q), "v" if d else "a"))

    def channels(name, d, owner):
        for c in range(CT):
            for q in range(Q):
                jobs.append(((name, d, c, q), owner))

    for d in range(DIRS):
        channels("u", d, "a")
    for d in range(DIRS):
        for q in range(Q):
            jobs.append((("x", d, q), "a"))
        channels("dt", d, "a")
        channels("z", d, "a")
    for d in range(DIRS):
        for h in range(B // 2):
            jobs.append((("mix", d, h), "a"))
    for q in range(Q):
        for d in range(DIRS):
            for k in range(KD):
                jobs.append((("mixT", d, k, q), "v" if k else "a"))
    for h in range(B // 2):
        jobs.append((("fuse", h), "v"))
    for q in range(Q):
        for k in range(KD):
            jobs.append((("xn2T", k, q), "v" if q else "a"))
        for m in range(KD):
            jobs.append((("qT", m, q), "v"))
    for q in range(Q):
        for k in range(KD):
            jobs.append((("xn3T", k, q), "a"))
    return jobs


JOBS = bank_jobs()
JOB = {key: n for n, (key, _) in enumerate(JOBS)}
OWNER = [owner for _, owner in JOBS]
COPIED = [OWNER[:n + 1].count(OWNER[n]) for n in range(len(JOBS))]


def decoder_layer(nc, x, ctxT, winT, wxT, wdtT, woutT, vec, ln_g, ln_b, wfuseT, bfuse,
                  wqT, wkT, wvT, woT, bo, wg, w1, b1, w2, b2, out):
    stack = ExitStack()
    with stack:
        def sb(name, shape, dt=F32, scope=stack):
            return scope.enter_context(nc.sbuf_tensor(name, shape, dt))

        def sem(name):
            return stack.enter_context(nc.semaphore(name))

        ps = stack.enter_context(nc.psum_tensor("ps", [P, 8, BANK], F32))

        ident = sb("ident", [P, P])
        flip = sb("flip", [L, L])
        head_mask = sb("head_mask", [P, HT])
        one = sb("one", [P, 1])
        prefer = sb("prefer", [L, E])
        x_tok = sb("x_tok", [L, B, D])
        xn_tok = sb("xn_tok", [L, B, D])
        stats = sb("stats", [L, DIRS * B, 6])
        moments = sb("moments", [L, DIRS * B, 2])
        var_eps = sb("var_eps", [L, DIRS * B])
        std = sb("std", [L, DIRS * B])
        rstd = sb("rstd", [L, DIRS * B])
        bias_tok = sb("bias_tok", [L, 2, D])

        mixing = ExitStack()
        row_sel = sb("row_sel", [96, N, P], BF16, scope=mixing)
        wx_sb = [sb(f"wx{d}", [P, CT, R + 2 * N], scope=mixing) for d in range(DIRS)]
        wdt_sb = [sb(f"wdt{d}", [R, DI], scope=mixing) for d in range(DIRS)]
        diag_d = [sb(f"diag_d{d}", [P, CT, P], scope=mixing) for d in range(DIRS)]
        vec_sb = [sb(f"vec{d}", [P, CT, VEC], scope=mixing) for d in range(DIRS)]
        neg_a = [sb(f"neg_a{d}", [P, CT * N], scope=mixing) for d in range(DIRS)]
        wout_sb = [sb(f"wout{d}", [P, CT, D], scope=mixing) for d in range(DIRS)]
        wfuse_sb = sb("wfuse_sb", [P, DIRS * KD, D], scope=mixing)
        lng_sb = sb("lng_sb", [P, DIRS * KD], scope=mixing)
        lnb_sb = sb("lnb_sb", [P, DIRS * KD], scope=mixing)
        xT = sb("xT", [P, 4, T], scope=mixing)

        mixer = ExitStack()
        dt_sb = [sb(f"dt{d}", [P, CT, T], scope=mixer) for d in range(DIRS)]
        dtu = [sb(f"dtu{d}", [P, CT, T], scope=mixer) for d in range(DIRS)]
        u_sb = [sb(f"u{d}", [P, CT, T], scope=mixer) for d in range(DIRS)]
        gate = [sb(f"gate{d}", [P, CT, T], scope=mixer) for d in range(DIRS)]
        b_parts = [sb(f"b_parts{d}", [96, T], BF16, scope=mixer) for d in range(DIRS)]
        c_parts = [sb(f"c_parts{d}", [96, T], BF16, scope=mixer) for d in range(DIRS)]
        parts = {"B": b_parts, "C": c_parts}
        early = ExitStack()
        win_sb = [sb(f"win{d}", [P, KD, 2 * DI], scope=early) for d in range(DIRS)]
        u_pad = [sb(f"u_pad{r}", [P, B, L + TAPS - 1], scope=early) for r in range(PADS)]
        part_mid = sb("part_mid", [N, T], BF16, scope=early)
        c_rows = sb("c_rows", [N, T], scope=early)
        early.close()
        xn_flat = xn_tok[:].rearrange("p b d -> p (b d)")
        rank_sb, b_rows = xn_flat[0:R, 0:T], xn_flat[0:N, T:2 * T]
        states = [sb(f"states{r}", [P, CT * TQ], scope=mixer) for r in range(RING)]
        c_row = [sb(f"c_row{r}", [P, TQ], scope=mixer) for r in range(2)]
        decay_sb = [sb(f"decay{r}", [P, TQ], scope=mixer) for r in range(CT - 2)]
        decay = [ps[:, 4, 0:TQ], ps[:, 5, 0:TQ], *(t[:] for t in decay_sb)]
        mixer.close()

        late = ExitStack()
        mix_tok = [sb(f"mix_tok{d}", [L, B, D], scope=late) for d in range(DIRS)]
        attn = ExitStack()
        xn2T = sb("xn2T", [P, KD, T], scope=attn)
        qT_part = [sb(f"qT_{n}", [P, KD, T], F32R, scope=attn) for n in "hl"]
        q_blk = [[sb(f"q_blk_{n}{r}", [P, KD, HT, L], F32R, scope=attn) for n in "hl"] for r in range(2)]
        ctx_sb = [sb(f"ctx{r}", [P, KD, S], scope=attn) for r in range(2)]
        ctx_part = [[sb(f"ctx_{n}{r}", [P, KD, SE], F32R, scope=attn) for n in "hl"] for r in range(2)]
        wq_sb, wk_sb, wv_sb, wo_sb = (sb(n, [P, KD, D], scope=attn) for n in ("wq_sb", "wk_sb", "wv_sb", "wo_sb"))
        wk_part, wv_part = ([sb(f"{w}_{n}", [P, KD, D], F32R, scope=attn) for n in "hl"] for w in ("wk", "wv"))
        kT_part = [[sb(f"kT_{n}{r}", [P, KD, SE], F32R, scope=attn) for n in "hl"] for r in range(2)]
        v_sb = [sb(f"v{r}", [P, KT, D], scope=attn) for r in range(2)]
        probs = [sb(f"probs{r}", [L, 2, KT * P], scope=attn) for r in range(2)]
        probsT = [[sb(f"probsT{r}{j}", [P, KT * L], scope=attn) for j in range(2)] for r in range(2)]
        neg_max, shift, mass, inv_mass = (
            sb(n, [L, 2, H], scope=attn) for n in ("neg_max", "shift", "mass", "inv_mass"))
        heads_tok = sb("heads_tok", [L, D], scope=attn)
        headsT = sb("headsT", [P, KD, L], scope=attn)
        attn.close()
        late.close()
        mixing.close()

        moe = ExitStack()
        w1_raw = sb("w1_raw", [P, KD, F], scope=moe)
        w2_raw = sb("w2_raw", [P, FT, D], scope=moe)
        b1_sb = sb("b1_sb", [P, EA, FT], scope=moe)
        bias = [sb(f"bias{r}", [P, FT], scope=moe) for r in range(2)]
        w1_part, w2_part = [], []
        for r in range(2):
            w1_part.append([sb(f"w1_{n}{r}", [P, KD, F], F32R, scope=moe) for n in "hl"])
            w2_part.append([sb(f"w2_{n}{r}", [P, FT, D], F32R, scope=moe) for n in "hl"])
            if r == 0:
                wg_sb = sb("wg_sb", [P, KD, E], scope=moe)
                b2_sb = sb("b2_sb", [EA, D], scope=moe)
                sel_draft = sb("sel_draft", [EA, EA, P], scope=moe)
                expert_sel = sb("expert_sel", [EA, EA, P], F32R, scope=moe)
        xn3_part = [sb(f"xn3_{n}", [P, KD, T], F32R, scope=moe) for n in "hl"]
        xn3T = sb("xn3T", [P, KD, T], scope=moe)
        cwT_part = [sb(f"cwT_{n}", [EA, T], F32R, scope=moe) for n in "hl"]
        cw_b = sb("cw_b", [P, EA * T], scope=moe)
        cw_tok = sb("cw_tok", [L, B, EA], scope=moe)
        cwT = sb("cwT", [EA, T], scope=moe)
        route = {n: sb(f"route_{n}", [L, B, E], scope=moe)
                 for n in ("shifted", "exp", "prob", "tie", "first", "rest", "second", "both", "kept")}
        per_tok = {n: sb(f"tok_{n}", [L, B, 1], scope=moe)
                   for n in ("max", "sum", "inv", "top1", "pick1", "top2", "pick2", "den", "inv_den")}
        hidden = [sb(f"hidden{r}", [P, TQ], scope=moe) for r in range(HRING)]
        hid_part = [[sb(f"hidden_{n}{r}", [P, TQ], F32R, scope=moe) for n in "hl"] for r in range(HRING)]
        weighted = sb("weighted", [P, KD, TQ], scope=moe)
        yT = sb("yT", [P, KD, T], scope=moe)
        out_tok = sb("out_tok", [L, B, D], scope=moe)
        moe.close()

        consts = sem("consts")
        x_in = [sem(f"x_in{q}") for q in range(Q)]
        win_in = [sem(f"win_in{d}") for d in range(DIRS)]
        vec_in = sem("vec_in")
        mixw_in = sem("mixw_in")
        attnw_in = sem("attnw_in")
        ctx_in = [sem(f"ctx_in{r}") for r in range(2)]
        moew_in = sem("moew_in")
        raw_in = sem("raw_in")
        split_done = sem("split_done")
        xn3_split = sem("xn3_split")
        conv_opened = sem("conv_opened")
        rank_ready = sem("rank_ready")
        rows_ready = sem("rows_ready")
        soft_ready = sem("soft_ready")
        out_stored = sem("out_stored")
        job_done = sem("job_done")
        copied = {"a": sem("copied_by_act"), "v": sem("copied_by_dve")}
        moments_ready = sem("moments_ready")
        std_ready = sem("std_ready")
        xn_ready = sem("xn_ready")
        dve_step = sem("dve_step")
        act_step = sem("act_step")
        bias_added = sem("bias_added")
        pad_zeroed = sem("pad_zeroed")
        conv_ready = sem("conv_ready")
        u_ready = sem("u_ready")
        log_ready = sem("log_ready")
        dt_ready = sem("dt_ready")
        dtu_ready = sem("dtu_ready")
        log_a_ready = sem("log_a_ready")
        rate_ready = sem("rate_ready")
        neg_a_ready = sem("neg_a_ready")
        diag_ready = sem("diag_ready")
        parts_ready = sem("parts_ready")
        decay_zeroed = sem("decay_zeroed")
        b_bank_ready = sem("b_bank_ready")
        c_bank_ready = sem("c_bank_ready")
        c_row_ready = sem("c_row_ready")
        decay_ready = sem("decay_ready")
        inflow_ready = sem("inflow_ready")
        scan_done = sem("scan_done")
        product_ready = sem("product_ready")
        y_summed = sem("y_summed")
        last_product = [sem(f"last_product_of_tile{c}") for c in range(CT)]
        last_sum = sem("last_sum")
        y_gated = sem("y_gated")
        probs_zeroed = sem("probs_zeroed")
        q_blk_ready = sem("q_blk_ready")
        q_high = sem("q_high")
        k_high = sem("k_high")
        kv_split = sem("kv_split")
        ctx_split = sem("ctx_split")
        k_done = sem("k_done")
        v_done = sem("v_done")
        k_copied = sem("k_copied")
        v_copied = sem("v_copied")
        scores_ready = sem("scores_ready")
        max_ready = sem("max_ready")
        shift_ready = sem("shift_ready")
        probs_ready = sem("probs_ready")
        probsT_ready = sem("probsT_ready")
        probsT_copied = [sem("probsT_copied_by_dve"), sem("probsT_copied_by_act")]
        pv_done = sem("pv_done")
        inv_mass_ready = sem("inv_mass_ready")
        heads_ready = sem("heads_ready")
        headsT_done = sem("headsT_done")
        headsT_copied = sem("headsT_copied")
        wo_done = sem("wo_done")
        x2_ready = sem("x2_ready")
        sel_ready = sem("sel_ready")
        logits_ready = sem("logits_ready")
        cwT_done = sem("cwT_done")
        cwT_ready = sem("cwT_ready")
        spread_done = sem("spread_done")
        spread_copied = [sem("spread_copied_by_dve"), sem("spread_copied_by_act")]
        xn3_high = sem("xn3_high")
        bias_ready = sem("bias_ready")
        turned_back = sem("turned_back")
        shifted_ready = sem("shifted_ready")
        exp_ready = sem("exp_ready")
        cw_ready = sem("cw_ready")
        hid_ready = sem("hid_ready")
        silu_done = sem("silu_done")
        hid_split = sem("hid_split")
        hid_used = sem("hid_used")
        y_taken = sem("y_taken")
        yT_ready = sem("yT_ready")
        out_ready = sem("out_ready")

        def bank(key):
            return ps[:, JOB[key] % 8, :]

        def job_bank_free(eng, key):
            before = JOB[key] - 8
            if before >= 0:
                eng.wait_ge(copied[OWNER[before]], COPIED[before])

        def job_result(eng, key):
            eng.wait_ge(job_done, JOB[key] + 1)

        def job_copied(eng, key):
            eng.wait_ge(copied[OWNER[JOB[key]]], COPIED[JOB[key]])

        def chunk(q):
            return slice(q * TQ, (q + 1) * TQ)

        def pair(h):
            return slice(2 * h, 2 * h + 2)

        def tile(k):
            return slice(k * P, (k + 1) * P)

        def spread_to(t, q):
            if 1 <= t <= KD:
                return yT[:, t - 1, chunk(q)]
            e = max(t - KD, 0)
            return cw_b[:, e * T + q * TQ:e * T + (q + 1) * TQ]

        def seqs(ap):
            return ap.rearrange("p (b t) -> p b t", t=L)

        def spread(per_token, width):
            return per_token.broadcast_to([L, B, width])

        block = stack.enter_context(nc.Block())

        @block.sync
        def _(sp):
            for q in range(Q):
                half = slice(q * BQ, (q + 1) * BQ)
                sp.dma_start(x_tok[:, half, :], x[half].rearrange("b l d -> l b d")).then_inc(x_in[q], 16)
            for d in range(DIRS):
                sp.dma_start(win_sb[d][:], winT[d].rearrange("(k p) e -> p k e", p=P)).then_inc(win_in[d], 16)
                sp.dma_start(vec_sb[d][:], vec[d]).then_inc(vec_in, 16)
            for d in range(DIRS):
                sp.dma_start(wx_sb[d][:], wxT[d].rearrange("(c p) e -> p c e", p=P)).then_inc(mixw_in, 16)
                sp.dma_start(wdt_sb[d][:], wdtT[d]).then_inc(mixw_in, 16)
                sp.dma_start(wout_sb[d][:], woutT[d].rearrange("(c p) e -> p c e", p=P)).then_inc(mixw_in, 16)
            sp.dma_start(wfuse_sb[:], wfuseT.rearrange("(k p) e -> p k e", p=P)).then_inc(mixw_in, 16)
            sp.dma_start(lng_sb[:], ln_g).then_inc(mixw_in, 16)
            sp.dma_start(lnb_sb[:], ln_b).then_inc(mixw_in, 16)
            sp.dma_start(bias_tok[:, 0, :], bfuse.partition_broadcast(L)).then_inc(mixw_in, 16)
            sp.dma_start(bias_tok[:, 1, :], bo.partition_broadcast(L)).then_inc(mixw_in, 16)
            job_result(sp, ("mix", DIRS - 1, B // 2 - 1))
            for w_dram, w_sbuf in ((wqT, wq_sb), (wkT, wk_sb), (wvT, wv_sb), (woT, wo_sb)):
                sp.dma_start(w_sbuf[:], w_dram.rearrange("(k p) e -> p k e", p=P)).then_inc(attnw_in, 16)
            for b in range(2):
                sp.dma_start(ctx_sb[b][:], ctxT[b].rearrange("(k p) s -> p k s", p=P)).then_inc(ctx_in[b], 16)

            def load_expert(e):
                at = bass.ds(e, 1)
                sp.dma_start(w1_raw[:], w1[at].rearrange("e (k p) f -> p (e k) f", p=P)).then_inc(raw_in, 16)
                sp.dma_start(w2_raw[:], w2[at].rearrange("e (f p) d -> p (e f) d", p=P)).then_inc(raw_in, 16)

            job_copied(sp, ("fuse", B // 2 - 1))
            load_expert(0)
            sp.dma_start(b1_sb[:], b1.rearrange("e p f -> p e f")).then_inc(moew_in, 16)
            sp.dma_start(wg_sb[:], wg.rearrange("(k p) e -> p k e", p=P)).then_inc(moew_in, 16)
            sp.dma_start(b2_sb[:], b2).then_inc(moew_in, 16)
            with sp.Fori(1, B // 2) as i:
                for r in range(2):
                    sp.wait_ge(ctx_split, 4 * i + (2 * r - 2))
                    sp.dma_start(ctx_sb[r][:], ctxT[bass.ds(2 * i + r, 1)].rearrange("b (k p) s -> p (b k) s", p=P)
                                 ).then_inc(ctx_in[r], 16)
            for e in (1, 2):
                sp.wait_ge(split_done, PIECES * e)
                load_expert(e)
            with sp.Fori(1, E // 2) as i:
                for j in range(2):
                    sp.wait_ge(split_done, 2 * PIECES * i + PIECES * (j + 1))
                    load_expert(2 * i + (j + 1))
            for h in range(B // 2):
                sp.wait_ge(out_ready, h + 1)
                sp.dma_start(out[pair(h)].rearrange("b l d -> l b d"), out_tok[:, pair(h), :]).then_inc(out_stored, 16)
            sp.wait_ge(out_stored, 16 * (B // 2))

        @block.gpsimd
        def _(pool):
            made = 0

            def fill(t, value):
                nonlocal made
                nc.gpsimd.memset(t, value).then_inc(consts, 1)
                made += 1
                pool.wait_ge(consts, made)

            def where(t, compare, value, base, pattern, step):
                nonlocal made
                nc.gpsimd.affine_select(out=t, in_=t, compare_op=compare, fill=value, base=base, pattern=pattern,
                                        channel_multiplier=step).then_inc(consts, 1)
                made += 1
                pool.wait_ge(consts, made)

            fill(ident[:], 0.0)
            where(ident[:], ALU.not_equal, 1.0, 0, [[-1, P]], 1)
            fill(flip[:], 0.0)
            where(flip[:], ALU.not_equal, 1.0, 1 - L, [[1, L]], 1)
            fill(row_sel[:], 0.0)
            for part in range(3):
                where(row_sel[:], ALU.not_equal, 1.0, -part * N, [[-1, N], [0, P]], 1)
            fill(head_mask[:], 1.0)
            where(head_mask[:], ALU.is_ge, 0.0, 0, [[-HD, HT]], 1)
            where(head_mask[:], ALU.is_ge, 0.0, HD - 1, [[HD, HT]], -1)
            fill(one[:], 1.0)
            for e in range(E):
                fill(prefer[:, e:e + 1], float(E - e))
            assert made == CONSTS
            pool.wait_ge(mixw_in, MIXW)
            pool.wait_ge(xn_ready, B)
            nc.gpsimd.tensor_tensor(x_tok[:], x_tok[:], bias_tok[:, 0:1, :].broadcast_to([L, B, D]), ALU.add
                                    ).then_inc(bias_added, 1)
            for d in range(DIRS):
                for c in range(CT):
                    g = d * CT + c
                    pool.wait_ge(soft_ready, g + 1)
                    nc.gpsimd.tensor_tensor(dt_sb[d][:, c, :], dt_sb[d][:, c, :], dtu[d][:, c, :], ALU.add
                                            ).then_inc(dt_ready, 1)
                    pool.wait_ge(dt_ready, g + 1)
                    pool.wait_ge(u_ready, g + 1)
                    nc.gpsimd.tensor_tensor(dtu[d][:, c, :], dt_sb[d][:, c, :], u_sb[d][:, c, :], ALU.mult
                                            ).then_inc(dtu_ready, 1)

            def state_times_c(n, r):
                pool.wait_ge(scan_done, CT * n + CT)
                pool.wait_ge(c_row_ready, n + 1)
                st = states[r][:].rearrange("p (c t) -> p c t", c=CT)
                nc.gpsimd.tensor_tensor(st, st, c_row[r % 2][:].unsqueeze(1).broadcast_to([P, CT, TQ]),
                                        ALU.mult).then_inc(product_ready, 1)

            for s in range(SEG - 1):
                with pool.Fori(0, N // RING) as i:
                    for r in range(RING):
                        state_times_c(i * RING + (s * N + r), r)
            first = (SEG - 1) * N
            with pool.Fori(0, N // RING - 1) as i:
                for r in range(RING):
                    state_times_c(i * RING + (first + r), r)
            for r in range(RING - 1):
                state_times_c(first + N - RING + r, r)
            n = first + N - 1
            pool.wait_ge(c_row_ready, n + 1)
            for c in POOL_TILES:
                pool.wait_ge(scan_done, CT * n + c + 1)
                st = states[RING - 1][:, c * TQ:(c + 1) * TQ]
                nc.gpsimd.tensor_tensor(st, st, c_row[n % 2][:], ALU.mult).then_inc(last_product[c], 1)
            def split_into(part, raw, done, count):
                high, low = part
                nc.gpsimd.tensor_tensor(high, raw, one[:].unsqueeze(2).broadcast_to(raw.shape), ALU.mult
                                        ).then_inc(done, 1)
                pool.wait_ge(done, count + 1)
                nc.gpsimd.tensor_tensor(low, raw, high.bitcast(F32), ALU.subtract).then_inc(done, 1)

            def split_context(b, r, loads):
                pool.wait_ge(ctx_in[r], 16 * loads)
                if not isinstance(b, int) or b >= 2:
                    pool.wait_ge(v_done, 2 * b - 2)
                split_into([part[:, :, 0:S] for part in ctx_part[r]], ctx_sb[r][:], ctx_split, 2 * b)

            def split_expert(e, r):
                pool.wait_ge(raw_in, LOADED * (e + 1))
                if not isinstance(e, int) or e >= 2:
                    pool.wait_ge(hid_used, UNITS * (e - 1))
                pieces = [(w1_part[r], w1_raw, slice(k, k + 1)) for k in range(KD)]
                pieces += [(w2_part[r], w2_raw, slice(f, f + FT // 2)) for f in (0, FT // 2)]
                for n, (part, raw, at) in enumerate(pieces):
                    split_into([t[:, at] for t in part], raw[:, at], split_done, PIECES * e + 2 * n)

            pool.wait_ge(attnw_in, 16 * 4)
            for n, (part, raw) in enumerate(((wk_part, wk_sb), (wv_part, wv_sb))):
                split_into([t[:] for t in part], raw[:], kv_split, 2 * n)
            for r in range(2):
                for part in ctx_part[r]:
                    nc.gpsimd.memset(part[:, :, S:].bitcast(F32), 0.0).then_inc(kv_split, 1)
            for b in range(2):
                split_context(b, b, 1)
            for r in range(2):
                nc.gpsimd.memset(probs[r][:, :, S:], 0.0).then_inc(probs_zeroed, 1)
            def spread_queries(b, r):
                for m in range(KD):
                    if isinstance(b, int):
                        job_copied(pool, ("qT", m, b // BQ))
                    for part, block in zip(qT_part, q_blk[r]):
                        nc.gpsimd.tensor_tensor(
                            block[:, m],
                            part[:, m, bass.ds(b * L, L)].bitcast(F32).unsqueeze(1).broadcast_to([P, HT, L]),
                            head_mask[:].unsqueeze(2).broadcast_to([P, HT, L]), ALU.mult).then_inc(q_blk_ready, 1)

            spread_queries(0, 0)
            pool.wait_ge(xn_ready, (1 + DIRS + 1) * B)
            nc.gpsimd.tensor_tensor(x_tok[:], x_tok[:], bias_tok[:, 1:2, :].broadcast_to([L, B, D]), ALU.add
                                    ).then_inc(bias_added, 1)
            spread_queries(1, 1)
            split_expert(0, 0)
            nc.gpsimd.memset(sel_draft[:], 0.0).then_inc(sel_ready, 1)
            pool.wait_ge(sel_ready, 1)
            nc.gpsimd.affine_select(out=sel_draft[:], in_=sel_draft[:], compare_op=ALU.not_equal, fill=1.0, base=0,
                                    pattern=[[-1, EA], [0, P]], channel_multiplier=1).then_inc(sel_ready, 1)
            pool.wait_ge(sel_ready, 2)
            nc.gpsimd.tensor_copy(expert_sel[:], sel_draft[:]).then_inc(sel_ready, 1)
            split_context(2, 0, 2)

            def prepare(b, r, next_loads=None):
                pool.wait_ge(scores_ready, GROUPS * b - GROUPS)
                spread_queries(b, r)
                if next_loads is not None:
                    split_context(b + 1, 1 - r, next_loads)

            job_copied(pool, ("qT", KD - 1, Q - 1))
            with pool.Fori(1, B // 2 - 1) as i:
                prepare(2 * i, 0, i + 1)
                prepare(2 * i + 1, 1, i + 2)
            prepare(B - 2, 0, B // 2)
            prepare(B - 1, 1)
            pool.wait_ge(x2_ready, B)
            split_expert(1, 1)
            split_expert(2, 0)
            with pool.Fori(1, E // 2) as i:
                for j in range(2):
                    split_expert(2 * i + (j + 1), 1 - j)

        @block.scalar
        def _(act):
            def root(norm, at):
                act.wait_ge(moments_ready, norm)
                nc.scalar.activation(std[:, at:at + BQ], var_eps[:, at:at + BQ], ACT.Sqrt).then_inc(std_ready, 1)

            def copy_out(key, dst, src, func=ACT.Copy, **how):
                job_result(act, key)
                nc.scalar.activation(dst, src, func, **how).then_inc(copied["a"], 1)

            for q in range(Q):
                root(1 + q, q * BQ)
            for q in range(Q):
                for k in range(KD):
                    copy_out(("xnT", 0, k, q), xT[:, k, chunk(q)], bank(("xnT", 0, k, q))[:, 0:TQ])
            act.wait_ge(pad_zeroed, PADS)
            act.wait_ge(vec_in, 16 * DIRS)

            def copy_u(d, c):
                if d * CT + c >= PADS:
                    act.wait_ge(conv_ready, d * CT + c - PADS + 1)
                for q in range(Q):
                    key = ("u", d, c, q)
                    job_result(act, key)
                    nc.scalar.activation(u_sb[d][:, c, chunk(q)], bank(key)[:, 0:TQ], ACT.Identity,
                                         scale=vec_sb[d][:, c, V_TAP + TAPS - 1:V_TAP + TAPS],
                                         bias=vec_sb[d][:, c, V_CONVB:V_CONVB + 1]).then_inc(conv_opened, 1)
                    copy_out(key, u_pad[(d * CT + c) % PADS][:, q * BQ:(q + 1) * BQ, TAPS - 1:],
                             seqs(bank(key)[:, 0:TQ]))

            def silu_u(d, c):
                act.wait_ge(conv_ready, d * CT + c + 1)
                nc.scalar.activation(u_sb[d][:, c, :], u_sb[d][:, c, :], ACT.Silu).then_inc(u_ready, 1)

            def copy_x(d):
                if d:
                    act.wait_ge(parts_ready, 2 * d)
                for q in range(Q):
                    key = ("x", d, q)
                    job_result(act, key)
                    nc.scalar.activation(rank_sb[:, chunk(q)], bank(key)[2 * N:2 * N + R, 0:TQ], ACT.Copy
                                         ).then_inc(rank_ready, 1)
                    nc.scalar.activation(b_rows[:, chunk(q)], bank(key)[0:N, 0:TQ], ACT.Copy).then_inc(rows_ready, 1)
                    copy_out(key, c_rows[:, chunk(q)], bank(key)[N:2 * N, 0:TQ])

            def softplus_parts(d, c):
                nonlocal steps
                v, e = gate[d][:, c, :], dtu[d][:, c, :]
                for q in range(Q):
                    copy_out(("dt", d, c, q), v[:, chunk(q)], bank(("dt", d, c, q))[:, 0:TQ], ACT.Identity,
                             bias=vec_sb[d][:, c, V_BDT:V_BDT + 1])
                job_copied(act, ("dt", d, c, Q - 1))
                nc.scalar.activation(e, v, ACT.Abs).then_inc(act_step, 1)
                act.wait_ge(act_step, steps + 1)
                nc.scalar.activation(e, e, ACT.Exp, scale=-1.0).then_inc(act_step, 1)
                act.wait_ge(act_step, steps + 2)
                steps += 2
                nc.scalar.activation(dt_sb[d][:, c, :], e, ACT.Ln, bias=1.0).then_inc(log_ready, 1)

            def gates(d):
                for c in range(CT):
                    act.wait_ge(soft_ready, d * CT + c + 1)
                    for q in range(Q):
                        copy_out(("z", d, c, q), gate[d][:, c, chunk(q)], bank(("z", d, c, q))[:, 0:TQ], ACT.Silu)

            steps = 0
            for g in range(DIRS * CT):
                copy_u(*divmod(g, CT))
                if 1 <= g <= DIRS * CT - 2:
                    silu_u(*divmod(g - 1, CT))
            nc.scalar.preload_act_table_set("natural_log_exp_and_others")
            copy_x(0)
            for d in range(DIRS):
                act.wait_ge(log_a_ready, d + 1)
                nc.scalar.activation(neg_a[d][:], neg_a[d][:], ACT.Exp).then_inc(rate_ready, 1)
            for c in range(CT):
                softplus_parts(0, c)
            for c in (CT - 2, CT - 1):
                silu_u(1, c)
            gates(0)
            nc.scalar.preload_act_table_set("natural_log_exp_and_others")
            copy_x(1)
            for c in range(CT):
                softplus_parts(1, c)
            gates(1)

            act.wait_ge(decay_zeroed, CT)
            act.wait_ge(dt_ready, CT)

            def decays(d, q, first, n, r):
                for c in range(CT):
                    act.wait_ge(neg_a_ready, DIRS)
                    if not (isinstance(n, int) and n < 1):
                        act.wait_ge(scan_done, CT * n + (c - CT + 1))
                    nc.scalar.activation(
                        seqs(decay[c])[:, :, 1:], seqs(dt_sb[d][:, c, chunk(q)])[:, :, 1:],
                        ACT.Exp, scale=neg_a[d][:, bass.ds(n + (c * N - first), 1)]).then_inc(decay_ready, 1)
                act.wait_ge(c_bank_ready, n + 1)
                if not (isinstance(n, int) and n < 2):
                    act.wait_ge(product_ready, n - 1)
                nc.scalar.activation(c_row[r % 2][:], ps[:, 7, 0:TQ], ACT.Copy).then_inc(c_row_ready, 1)

            for r in range(RING):
                decays(0, 0, 0, r, r)
            for s in range(SEG):
                if s == Q:
                    act.wait_ge(dt_ready, DIRS * CT)
                with act.Fori(s == 0, N // RING) as i:
                    for r in range(RING):
                        decays(*divmod(s, Q), s * N, i * RING + (s * N + r), r)

            for d in range(DIRS):
                for h in range(B // 2):
                    copy_out(("mix", d, h), mix_tok[d][:, pair(h), :].rearrange("l b d -> l (b d)"),
                             bank(("mix", d, h))[0:L, :])
                    j = d * (B // 2) + h - 2
                    if j >= 0 and j % 2 == 0:
                        root(Q + 1 + j // 2, j // 2 * BQ)
            root(Q + DIRS * Q, (DIRS * Q - 1) * BQ)

            def copy_mixed(d, k, q):
                j, key = d * KD + k, ("mixT", d, k, q)
                copy_out(key, xT[:, j, chunk(q)], bank(key)[:, 0:TQ], ACT.Identity,
                         scale=lng_sb[:, j:j + 1], bias=lnb_sb[:, j:j + 1])

            for q in range(Q):
                for d in range(DIRS):
                    copy_mixed(d, 0, q)
            def high_queries(m, q):
                job_result(act, ("qT", m, q))
                nc.scalar.activation(qT_part[0][:, m, chunk(q)], bank(("qT", m, q))[:, 0:TQ], ACT.Copy
                                     ).then_inc(q_high, 1)

            root(Q + DIRS * Q + 1, 0)
            for k in range(KD):
                copy_out(("xn2T", k, 0), xn2T[:, k, chunk(0)], bank(("xn2T", k, 0))[:, 0:TQ])
            root(Q + DIRS * Q + 2, BQ)
            for m in range(KD):
                high_queries(m, 0)

            def high_keys(b, r, m, at=KEY_BANK):
                act.wait_ge(k_done, 2 * b + (m + 1))
                nc.scalar.activation(kT_part[r][0][:, m, :], ps[:, at, 0:SE], ACT.Copy).then_inc(k_high, 1)

            def exponentials(b, r, g):
                act.wait_ge(shift_ready, GROUPS * b + (g + 1))
                if not isinstance(b, int) or GROUPS * b + g >= 2:
                    act.wait_ge(probsT_ready, GROUPS * b + (g - 1))
                for j in range(2):
                    h = 2 * g + j
                    nc.scalar.activation(probs[g % 2][:, j, 0:S], ps[0:L, g % 2 * 2 + j, 0:S], ACT.Exp,
                                         bias=shift[:, r, h:h + 1], scale=HD ** -0.5,
                                         accum_out=mass[:, r, h:h + 1]).then_inc(probs_ready, 1)

            def copy_probs(b, g):
                act.wait_ge(probsT_ready, GROUPS * b + (g + 1))
                if not isinstance(b, int) or GROUPS * b + g >= 2:
                    act.wait_ge(pv_done, GROUPS * b + (g - 1))
                nc.scalar.activation(probsT[g % 2][1][:], ps[:, 5, 0:KT * L], ACT.Copy).then_inc(probsT_copied[1], 1)

            def attend(b, r, last=False):
                for g in range(2, GROUPS):
                    copy_probs(b, g)
                    if g + 2 < GROUPS:
                        exponentials(b, r, g + 2)
                    elif not last:
                        exponentials(b + 1, 1 - r, g + 2 - GROUPS)
                    if g - 2 in range(KD) and not last:
                        high_keys(b + 1, 1 - r, g - 2)
                for g in range(0 if last else 2):
                    copy_probs(b + 1, g)
                    exponentials(b + 1, 1 - r, g + 2)

            for m in range(KD):
                high_keys(0, 0, m, FIRST_KEYS[m])
            act.wait_ge(probs_zeroed, 2)
            exponentials(0, 0, 0)
            exponentials(0, 0, 1)
            for m in range(KD):
                high_queries(m, 1)
            for g in range(2):
                copy_probs(0, g)
                exponentials(0, 0, g + 2)
            with act.Fori(0, B // 2 - 1) as i:
                for r in range(2):
                    attend(2 * i + r, r)
            attend(B - 2, 0)
            attend(B - 1, 1, last=True)
            for q in range(Q):
                root(2 * Q + DIRS * Q + q + 1, q * BQ)
            for q in range(Q):
                for k in range(KD):
                    job_result(act, ("xn3T", k, q))
                    nc.scalar.activation(xn3_part[0][:, k, chunk(q)], bank(("xn3T", k, q))[:, 0:TQ], ACT.Copy
                                         ).then_inc(xn3_high, 1)
                    copy_out(("xn3T", k, q), xn3T[:, k, chunk(q)], bank(("xn3T", k, q))[:, 0:TQ])

            def take_bias(e, r):
                nc.scalar.activation(bias[r][:], b1_sb[:, bass.ds(e, 1), :].rearrange("p e f -> p (e f)"), ACT.Copy
                                     ).then_inc(bias_ready, 1)
                act.wait_ge(bias_ready, e + 1)

            def silu_unit(e, r, u):
                ft = u % FT
                act.wait_ge(hid_ready, UNITS * e + (u + 1))
                if not (isinstance(e, int) and e == 0 and u < HRING):
                    act.wait_ge(hid_used, UNITS * e + (u - HRING + 1))
                for dst in (hidden[u % HRING], hid_part[u % HRING][0]):
                    nc.scalar.activation(dst[:], ps[:, u % 2, 0:TQ], ACT.Silu, bias=bias[r][:, ft:ft + 1]
                                         ).then_inc(silu_done, 1)

            act.wait_ge(moew_in, MOEW)
            take_bias(0, 0)
            for u in range(UNITS):
                silu_unit(0, 0, u)
                if u == EXP_AT:
                    act.wait_ge(shifted_ready, 2)
                    nc.scalar.activation(route["exp"][:], route["shifted"][:], ACT.Exp).then_inc(exp_ready, 1)
                for t in SPREAD_AT.get(u, ()):
                    act.wait_ge(spread_done, t + 1)
                    nc.scalar.activation(spread_to(t, 1), ps[:, 3, 0:TQ], ACT.Copy).then_inc(spread_copied[1], 1)
            with act.Fori(0, E // 2) as i:
                for j in range(2):
                    take_bias(2 * i + (j + 1), 1 - j)
                    for u in range(UNITS):
                        silu_unit(2 * i + (j + 1), 1 - j, u)

        @block.tensor
        def _(pe):
            def turned(key, src, how):
                job_bank_free(pe, key)
                q = key[-1]
                for b in range(BQ):
                    mm = nc.tensor.matmul(bank(key)[:, b * L:(b + 1) * L], src(q * BQ + b), how, start=True, stop=True)
                mm.then_inc(job_done, 1)

            def product(key, rows, cols, pairs):
                job_bank_free(pe, key)
                for n, (lhsT, rhs) in enumerate(pairs):
                    mm = nc.tensor.matmul(bank(key)[0:rows, 0:cols], lhsT, rhs, start=(n == 0),
                                          stop=(n == len(pairs) - 1))
                mm.then_inc(job_done, 1)

            def pair_product(key, pairs):
                job_bank_free(pe, key)
                for j in range(2):
                    b = 2 * key[-1] + j
                    for n, (lhsT, rhs) in enumerate(pairs):
                        mm = nc.tensor.matmul(bank(key)[0:L, j * D:(j + 1) * D], lhsT[:, b * L:(b + 1) * L], rhs,
                                              start=(n == 0), stop=(n == len(pairs) - 1))
                mm.then_inc(job_done, 1)

            def three(to, w, x, first, last):
                for n, (i, j) in enumerate(((0, 0), (0, 1), (1, 0))):
                    mm = nc.tensor.matmul(to, w[i], x[j], start=(first and n == 0), stop=(last and n == 2))
                return mm

            order = (ident[0:L, 0:L], flip[:])
            pe.wait_ge(consts, TURNS)
            for q in range(Q):
                pe.wait_ge(xn_ready, (q + 1) * BQ)
                for d in range(DIRS):
                    for k in range(KD):
                        turned(("xnT", d, k, q), lambda b: xn_tok[:, b, tile(k)], order[d])

            def in_product(name, half, d):
                for c in range(CT):
                    for q in range(Q):
                        product((name, d, c, q), P, TQ, [
                            (win_sb[d][:, k, half * DI + c * P:half * DI + (c + 1) * P],
                             xT[:, d * KD + k, chunk(q)]) for k in range(KD)])

            for d in range(DIRS):
                pe.wait_ge(win_in[d], 16)
                for k in range(KD):
                    for q in range(Q):
                        job_copied(pe, ("xnT", d, k, q))
                in_product("u", 0, d)
            pe.wait_ge(mixw_in, MIXW)
            for d in range(DIRS):
                pe.wait_ge(u_ready, (d + 1) * CT)
                for q in range(Q):
                    product(("x", d, q), 2 * N + R, TQ, [
                        (wx_sb[d][:, c, :], u_sb[d][:, c, chunk(q)]) for c in range(CT)])
                pe.wait_ge(rank_ready, Q * (d + 1))
                for c in range(CT):
                    for q in range(Q):
                        product(("dt", d, c, q), P, TQ, [(wdt_sb[d][:, tile(c)], rank_sb[:, chunk(q)])])
                in_product("z", 1, d)

            pe.wait_ge(consts, CONSTS)
            for key, _ in JOBS[JOB[("z", DIRS - 1, CT - 1, Q - 1)] - 7:][:8]:
                job_copied(pe, key)
            pe.wait_ge(parts_ready, 2 * DIRS)
            pe.wait_ge(diag_ready, DIRS)

            def row_of(parts, ring_bank, d, q, first, n):
                return nc.tensor.matmul(ps[:, ring_bank, 0:TQ],
                                        row_sel[:, bass.ds(n - first, 1), :].rearrange("p n m -> p (n m)"),
                                        parts[d][:, chunk(q)], start=True, stop=True)

            def b_row(n, s):
                if not (isinstance(n, int) and n < 1):
                    pe.wait_ge(inflow_ready, n)
                row_of(b_parts, 6, *divmod(s, Q), s * N, n).then_inc(b_bank_ready, 1)

            def c_row_bank(n, s):
                if not (isinstance(n, int) and n < 1):
                    pe.wait_ge(c_row_ready, n)
                row_of(c_parts, 7, *divmod(s, Q), s * N, n).then_inc(c_bank_ready, 1)

            def sum_last_state(r):
                for c in range(CT):
                    pe.wait_ge(last_product[c], 1)
                    nc.tensor.matmul(ps[:, c, 0:TQ], ident[:], states[r][:, c * TQ:(c + 1) * TQ],
                                     start=False, stop=True, skip_group_check=True).then_inc(last_sum, 1)

            def sum_state(n, r, last=False):
                pe.wait_ge(product_ready, n + 1)
                for c in range(CT):
                    mm = nc.tensor.matmul(ps[:, c, 0:TQ], ident[:], states[r][:, c * TQ:(c + 1) * TQ],
                                          start=False, stop=last, skip_group_check=True)
                mm.then_inc(y_summed, 1)

            def step_of(n, r, s, opening=False, closing=False):
                left = N - RING + r if closing else r if isinstance(n, int) else 0
                for lead, row in ((3, b_row), (2, c_row_bank)):
                    ahead = s + (left + lead >= N)
                    if ahead < SEG:
                        row(n + lead, ahead)
                if opening:
                    if s:
                        pe.wait_ge(y_gated, CT * s)
                    d, q = divmod(s, Q)
                    for c in range(CT):
                        nc.tensor.matmul(ps[:, c, 0:TQ], diag_d[d][:, c, :], u_sb[d][:, c, chunk(q)], start=True,
                                         stop=False, skip_group_check=True)
                if closing and r == RING - 1 and s == SEG - 1:
                    sum_last_state(r)
                else:
                    sum_state(n, r, closing and r == RING - 1)

            for n in range(3):
                b_row(n, 0)
                if n < 2:
                    c_row_bank(n, 0)
            for s in range(SEG):
                for r in range(RING):
                    step_of(s * N + r, r, s, opening=r == 0)
                with pe.Fori(1, N // RING - 1) as i:
                    for r in range(RING):
                        step_of(i * RING + (s * N + r), r, s)
                for r in range(RING):
                    step_of(s * N + N - RING + r, r, s, closing=True)

            pe.wait_ge(y_gated, CT * SEG)
            for d in range(DIRS):
                for h in range(B // 2):
                    pair_product(("mix", d, h), [(u_sb[d][:, c, :], wout_sb[d][:, c, :]) for c in range(CT)])
            for q in range(Q):
                for d in range(DIRS):
                    pe.wait_ge(xn_ready, B + d * B + (q + 1) * BQ)
                    for k in range(KD):
                        turned(("mixT", d, k, q), lambda b: mix_tok[d][:, b, tile(k)], order[d])
            for q in range(Q):
                for d in range(DIRS):
                    for k in range(KD):
                        job_copied(pe, ("mixT", d, k, q))
                for h in range(q * BQ // 2, (q + 1) * BQ // 2):
                    pair_product(("fuse", h), [(xT[:, j, :], wfuse_sb[:, j, :]) for j in range(DIRS * KD)])
            pe.wait_ge(attnw_in, 16 * 4)

            def turn_x2(q):
                pe.wait_ge(xn_ready, (1 + DIRS) * B + (q + 1) * BQ)
                for k in range(KD):
                    turned(("xn2T", k, q), lambda b: xn_tok[:, b, tile(k)], order[0])

            def queries(q):
                for k in range(KD):
                    job_copied(pe, ("xn2T", k, q))
                for m in range(KD):
                    product(("qT", m, q), P, TQ, [(wq_sb[:, k, tile(m)], xn2T[:, k, chunk(q)]) for k in range(KD)])

            def keys(b, r, m, at=KEY_BANK):
                if m == 0:
                    pe.wait_ge(ctx_split, 2 * b + 2)
                    if not isinstance(b, int) or b > 1:
                        pe.wait_ge(x2_ready, b - 1)
                elif at == KEY_BANK:
                    pe.wait_ge(k_copied, 2 * b + m)
                for k in range(KD):
                    mm = three(ps[:, at, 0:SE], [part[:, k, tile(m)] for part in wk_part],
                               [part[:, k, :] for part in ctx_part[r]], k == 0, k == KD - 1)
                mm.then_inc(k_done, 1)

            def values(b, r, part, at=KEY_BANK):
                if at == KEY_BANK:
                    if part == 0:
                        pe.wait_ge(k_copied, 2 * b + KD)
                    else:
                        pe.wait_ge(v_copied, 2 * b + part)
                for kt in ((0, 1), (2,))[part]:
                    size = P if kt < KT - 1 else SL
                    for k in range(KD):
                        mm = three(ps[0:size, at, kt % 2 * D:(kt % 2 + 1) * D],
                                   [part[:, k, kt * P:kt * P + size] for part in ctx_part[r]],
                                   [part[:, k, :] for part in wv_part], k == 0, k == KD - 1)
                mm.then_inc(v_done, 1)

            def scores(b, r, g):
                m = 2 * g // HT
                pe.wait_ge(q_blk_ready, 2 * KD * b + 2 * (m + 1))
                if g % (GROUPS // KD) == 0:
                    pe.wait_ge(k_copied, 2 * b + (m + 1))
                if not isinstance(b, int) or GROUPS * b + g >= 2:
                    pe.wait_ge(probs_ready, 2 * GROUPS * b + (2 * g - 2))
                for j in range(2):
                    mm = three(ps[0:L, g % 2 * 2 + j, 0:SE], [part[:, m, (2 * g + j) % HT, :] for part in q_blk[r]],
                               [part[:, m, :] for part in kT_part[r]], True, True)
                mm.then_inc(scores_ready, 1)

            def turn_probs(b, g):
                pe.wait_ge(probs_ready, 2 * GROUPS * b + (2 * g + 2))
                if not isinstance(b, int) or GROUPS * b + g >= 1:
                    for by in probsT_copied:
                        pe.wait_ge(by, GROUPS * b + g)
                for j in range(2):
                    for kt in range(KT):
                        mm = nc.tensor.transpose(ps[:, 4 + j, kt * L:(kt + 1) * L], probs[g % 2][:, j, tile(kt)],
                                                 ident[0:L, 0:L])
                mm.then_inc(probsT_ready, 1)

            def weigh_values(b, r, g):
                for by in probsT_copied:
                    pe.wait_ge(by, GROUPS * b + (g + 1))
                if g == 0:
                    pe.wait_ge(v_copied, 2 * b + 2)
                    if not isinstance(b, int) or b > 0:
                        pe.wait_ge(heads_ready, b)
                for j in range(2):
                    h = 2 * g + j
                    for kt in range(KT):
                        size = P if kt < KT - 1 else SL
                        mm = nc.tensor.matmul(ps[0:L, 6, h * HD:(h + 1) * HD],
                                              probsT[g % 2][j][0:size, kt * L:(kt + 1) * L],
                                              v_sb[r][0:size, kt, h * HD:(h + 1) * HD],
                                              start=(kt == 0), stop=(kt == KT - 1))
                mm.then_inc(pv_done, 1)

            def turn_heads(b):
                pe.wait_ge(heads_ready, b + 1)
                for m in range(KD):
                    mm = nc.tensor.transpose(ps[:, KEY_BANK, m * L:(m + 1) * L], heads_tok[:, tile(m)],
                                             ident[0:L, 0:L])
                mm.then_inc(headsT_done, 1)

            def project_heads(b):
                pe.wait_ge(headsT_copied, b + 1)
                for m in range(KD):
                    mm = nc.tensor.matmul(ps[0:L, KEY_BANK, 0:D], headsT[:, m, :], wo_sb[:, m, :], start=(m == 0),
                                          stop=(m == KD - 1))
                mm.then_inc(wo_done, 1)

            def attend(b, r, last=False):
                nxt = (b + 1, 1 - r)
                for g in range(2, GROUPS):
                    turn_probs(b, g)
                    if g + 2 < GROUPS:
                        scores(b, r, g + 2)
                    elif not last:
                        scores(*nxt, g + 2 - GROUPS)
                    if not last:
                        if g - 2 < KD:
                            keys(*nxt, g - 2)
                        elif g - 4 < 2:
                            values(*nxt, g - 4)
                    weigh_values(b, r, g)
                if last:
                    turn_heads(b)
                    project_heads(b)
                else:
                    turn_probs(b + 1, 0)
                    scores(*nxt, 2)
                    turn_heads(b)
                    weigh_values(*nxt, 0)
                    turn_probs(b + 1, 1)
                    scores(*nxt, 3)
                    project_heads(b)
                    weigh_values(*nxt, 1)

            turn_x2(0)
            queries(0)
            pe.wait_ge(kv_split, 4 + 4)
            for m in range(KD):
                keys(0, 0, m, FIRST_KEYS[m])
            turn_x2(1)
            for m in range(KD):
                job_copied(pe, ("qT", m, 0))
            pe.wait_ge(k_copied, KD)
            scores(0, 0, 0)
            scores(0, 0, 1)
            for k in range(KD):
                job_copied(pe, ("xn2T", k, 1))
            for part in range(2):
                values(0, 0, part, FIRST_VALUES[part])
            queries(1)
            pe.wait_ge(v_copied, 2)
            for m in range(KD):
                job_copied(pe, ("qT", m, 1))
            for g in range(2):
                turn_probs(0, g)
                scores(0, 0, g + 2)
                weigh_values(0, 0, g)
            attend(0, 0)
            with pe.Fori(0, B // 2 - 1) as i:
                attend(2 * i + 1, 1)
                attend(2 * i + 2, 0)
            attend(B - 1, 1, last=True)

            for q in range(Q):
                pe.wait_ge(xn_ready, (1 + DIRS + 1) * B + (q + 1) * BQ)
                for k in range(KD):
                    turned(("xn3T", k, q), lambda b: xn_tok[:, b, tile(k)], order[0])

            def logits():
                for k in range(KD):
                    job_copied(pe, ("xn3T", k, 1))
                pe.wait_ge(moew_in, MOEW)
                for b in range(B):
                    for k in range(KD):
                        mm = nc.tensor.matmul(ps[0:L, 2, b * E:(b + 1) * E], xn3T[:, k, b * L:(b + 1) * L],
                                              wg_sb[:, k, :], start=(k == 0), stop=(k == KD - 1))
                mm.then_inc(logits_ready, 1)

            def weight_rows():
                pe.wait_ge(cw_ready, 1)
                for q in range(Q):
                    for b in range(BQ):
                        mm = nc.tensor.matmul(ps[0:EA, 2 + q, b * L:(b + 1) * L], cw_tok[:, q * BQ + b, :],
                                              ident[0:L, 0:L], start=True, stop=True)
                mm.then_inc(cwT_done, 1)

            def spread_row(t):
                if t == 0:
                    pe.wait_ge(cwT_ready, 3 * Q)
                    pe.wait_ge(sel_ready, 3)
                else:
                    for by in spread_copied:
                        pe.wait_ge(by, t)
                for q in range(Q):
                    to = ps[:, 2 + q, 0:TQ]
                    if 1 <= t <= KD:
                        mm = nc.tensor.matmul(to, b2_sb[:, tile(t - 1)], cwT[:, chunk(q)], start=True, stop=True)
                    else:
                        for part in cwT_part:
                            mm = nc.tensor.matmul(to, expert_sel[:, max(t - KD, 0), :], part[:, chunk(q)],
                                                  start=(part is cwT_part[0]), stop=(part is cwT_part[1]))
                mm.then_inc(spread_done, 1)

            def into_hidden(e, r, u):
                q, ft = divmod(u, FT)
                if u == 0:
                    pe.wait_ge(split_done, PIECES * e + PIECES)
                if isinstance(e, int) and e == 0:
                    if ft == 0:
                        pe.wait_ge(xn3_split, KD * (q + 1))
                if not (isinstance(e, int) and e == 0 and u < 2):
                    pe.wait_ge(silu_done, 2 * UNITS * e + 2 * (u - 1))
                for k in range(KD):
                    mm = three(ps[:, u % 2, 0:TQ], [part[:, k, tile(ft)] for part in w1_part[r]],
                               [part[:, k, chunk(q)] for part in xn3_part], k == 0, k == KD - 1)
                mm.then_inc(hid_ready, 1)

            def out_of_hidden(e, r, u):
                q, ft = divmod(u, FT)
                if ft == 0 and not (isinstance(e, int) and e == 0):
                    pe.wait_ge(y_taken, Q * e + (q + 1 - Q))
                pe.wait_ge(hid_split, UNITS * e + (u + 1))
                for m in range(KD):
                    mm = three(ps[:, 4 + 2 * q + m, 0:TQ], [part[:, ft, tile(m)] for part in w2_part[r]],
                               [part[:] for part in hid_part[u % HRING]], ft == 0, ft == FT - 1)
                mm.then_inc(hid_used, 1)

            for k in range(KD):
                job_copied(pe, ("xn3T", k, 0))
            for u in range(UNITS):
                into_hidden(0, 0, u)
                if u == LOGITS_AT:
                    logits()
                if u == ROWS_AT:
                    weight_rows()
                for n, t in enumerate(SPREAD_AT.get(u, (None,))):
                    if t is not None:
                        spread_row(t)
                    if n == 0 and u >= LAG:
                        out_of_hidden(0, 0, u - LAG)
            with pe.Fori(0, E // 2) as i:
                for j in range(2):
                    for u in range(UNITS):
                        into_hidden(2 * i + (j + 1), 1 - j, u)
                        if u >= LAG:
                            out_of_hidden(2 * i + (j + 1), 1 - j, u - LAG)
                        else:
                            out_of_hidden(2 * i + j, j, UNITS + u - LAG)
            for u in range(UNITS - LAG, UNITS):
                out_of_hidden(E, 0, u)
            for h in range(B // 2):
                pe.wait_ge(yT_ready, Q * EA - Q + 1 + 2 * h // BQ)
                for j in range(2):
                    b = 2 * h + j
                    for m in range(KD):
                        mm = nc.tensor.transpose(ps[0:L, h, j * D + m * P:j * D + (m + 1) * P],
                                                 yT[:, m, b * L:(b + 1) * L], ident[:])
                mm.then_inc(turned_back, 1)

        @block.vector
        def _(dve):
            steps = 0

            def step(ins):
                nonlocal steps
                ins.then_inc(dve_step, 1)
                steps += 1
                dve.wait_ge(dve_step, steps)

            def later(ins):
                nonlocal steps
                ins.then_inc(dve_step, 1)
                steps += 1

            norms = 0

            def layer_norm(at, pairs):
                nonlocal norms
                norms += 1
                cols = slice(at, at + BQ)
                for j, (src, _) in enumerate(pairs):
                    later(nc.vector.bn_stats(stats[:, at + j, :], src))
                dve.wait_ge(dve_step, steps)
                for j in range(BQ):
                    later(nc.vector.bn_aggr(moments[:, at + j, :], stats[:, at + j, :]))
                dve.wait_ge(dve_step, steps)
                nc.vector.tensor_scalar(var_eps[:, cols], moments[:, cols, 1], EPS, None, ALU.add
                                        ).then_inc(moments_ready, 1)
                dve.wait_ge(std_ready, norms)
                step(nc.vector.reciprocal(rstd[:, cols], std[:, cols]))
                for j, (src, dst) in enumerate(pairs):
                    nc.vector.tensor_scalar(dst, src, moments[:, at + j, 0:1], rstd[:, at + j:at + j + 1],
                                            ALU.subtract, ALU.mult).then_inc(xn_ready, 1)

            def norm_x(q):
                layer_norm(q * BQ, [(x_tok[:, b, :], xn_tok[:, b, :]) for b in range(q * BQ, (q + 1) * BQ)])

            def copy_out(key, dst, src):
                job_result(dve, key)
                nc.vector.tensor_copy(dst, src).then_inc(copied["v"], 1)

            for r in range(PADS):
                nc.vector.memset(u_pad[r][:, :, 0:TAPS - 1], 0.0).then_inc(pad_zeroed, 1)
            for q in range(Q):
                dve.wait_ge(x_in[q], 16)
                norm_x(q)
            for q in range(Q):
                for k in range(KD):
                    copy_out(("xnT", 1, k, q), xT[:, KD + k, chunk(q)], bank(("xnT", 1, k, q))[:, 0:TQ])
            dve.wait_ge(vec_in, 16 * DIRS)
            dve.wait_ge(consts, TURNS)
            for d in range(DIRS):
                for c in range(CT):
                    ins = nc.vector.tensor_scalar(diag_d[d][:, c, :], ident[:], vec_sb[d][:, c, V_D:V_D + 1], None,
                                                  ALU.mult)
                ins.then_inc(diag_ready, 1)
            for d in range(DIRS):
                nc.vector.tensor_scalar(neg_a[d][:].rearrange("p (c n) -> p c n", c=CT), vec_sb[d][:, :, V_ALOG:],
                                        LOG_MAX, None, ALU.min).then_inc(log_a_ready, 1)
            dve.wait_ge(pad_zeroed, PADS)
            for d in range(DIRS):
                for c in range(CT):
                    g = d * CT + c
                    dve.wait_ge(conv_opened, Q * (g + 1))
                    for q in range(Q):
                        job_copied(dve, ("u", d, c, q))
                    padded, to = u_pad[g % PADS], seqs(u_sb[d][:, c, :])
                    for k in range(TAPS - 1):
                        tap = vec_sb[d][:, c, V_TAP + k:V_TAP + k + 1]
                        ins = nc.vector.scalar_tensor_tensor(to, padded[:, :, k:k + L], tap, to, ALU.mult, ALU.add)
                        if k < TAPS - 2:
                            step(ins)
                    ins.then_inc(conv_ready, 1)
            for d in range(DIRS):
                dve.wait_ge(rate_ready, d + 1)
                nc.vector.tensor_scalar(neg_a[d][:], neg_a[d][:], -1.0, None, ALU.mult
                                        ).then_inc(neg_a_ready, 1)

            def step_size(d, c):
                v, e, l = gate[d][:, c, :], dtu[d][:, c, :], dt_sb[d][:, c, :]
                dve.wait_ge(log_ready, d * CT + c + 1)
                step(nc.vector.scalar_tensor_tensor(l, v, 0.0, l, ALU.max, ALU.add))
                step(nc.vector.tensor_scalar(v, e, 1.0, -1.0, ALU.add, ALU.add))
                nc.vector.tensor_tensor(e, e, v, ALU.subtract).then_inc(soft_ready, 1)

            def split_rows(rows, part):
                step(nc.vector.tensor_copy(part[0:N, :], rows))
                step(nc.vector.tensor_tensor(rows, rows, part[0:N, :], ALU.subtract))
                step(nc.vector.tensor_copy(part_mid[:], rows))
                later(nc.vector.tensor_copy(part[N:2 * N, :], part_mid[:]))
                dve.wait_ge(dve_step, steps)
                nc.vector.tensor_tensor(part[2 * N:3 * N, :], rows, part_mid[:], ALU.subtract
                                        ).then_inc(parts_ready, 1)

            for d in range(DIRS):
                dve.wait_ge(rows_ready, Q * (d + 1))
                job_copied(dve, ("x", d, Q - 1))
                split_rows(b_rows, b_parts[d])
                split_rows(c_rows[:], c_parts[d])
                for c in range(CT):
                    step_size(d, c)
            for key, _ in JOBS[JOB[("z", DIRS - 1, CT - 1, Q - 1)] - 7:][:8]:
                job_copied(dve, key)
            for c in range(CT):
                nc.vector.memset(seqs(decay[c])[:, :, 0:1], 0.0).then_inc(decay_zeroed, 1)
            dve.wait_ge(decay_zeroed, CT)

            def inflow(d, q, n, r):
                dve.wait_ge(b_bank_ready, n + 1)
                if not (isinstance(n, int) and n < RING):
                    dve.wait_ge(y_summed, n - (RING - 1))
                nc.vector.tensor_tensor(states[r][:].rearrange("p (c t) -> p c t", c=CT), dtu[d][:, :, chunk(q)],
                                        ps[:, 6:7, 0:TQ].broadcast_to([P, CT, TQ]), ALU.mult
                                        ).then_inc(inflow_ready, 1)

            def recur(n, r):
                dve.wait_ge(inflow_ready, n + 1)
                for c in range(CT):
                    dve.wait_ge(decay_ready, CT * n + (c + 1))
                    st = states[r][:, c * TQ:(c + 1) * TQ]
                    nc.vector.tensor_tensor_scan(st, decay[c], st, 0.0, ALU.mult, ALU.add).then_inc(scan_done, 1)

            def gated(s):
                d, q = divmod(s, Q)
                if s < SEG - 1:
                    dve.wait_ge(y_summed, (s + 1) * N)
                for c in range(CT):
                    if s == SEG - 1:
                        dve.wait_ge(last_sum, c + 1)
                    nc.vector.tensor_tensor(u_sb[d][:, c, chunk(q)], ps[:, c, 0:TQ], gate[d][:, c, chunk(q)], ALU.mult
                                            ).then_inc(y_gated, 1)

            dve.wait_ge(dtu_ready, CT)
            inflow(0, 0, 0, 0)
            for s in range(SEG):
                d, q = divmod(s, Q)
                if s == Q - 1:
                    dve.wait_ge(dtu_ready, DIRS * CT)
                for r in range(RING):
                    inflow(d, q, s * N + r + 1, (r + 1) % RING)
                    recur(s * N + r, r)
                    if s and r == 1:
                        gated(s - 1)
                with dve.Fori(1, N // RING - 1) as i:
                    for r in range(RING):
                        inflow(d, q, i * RING + (s * N + r + 1), (r + 1) % RING)
                        recur(i * RING + (s * N + r), r)
                for r in range(RING):
                    n = s * N + N - RING + r
                    if r + 1 < RING:
                        inflow(d, q, n + 1, r + 1)
                    elif s + 1 < SEG:
                        inflow(*divmod(s + 1, Q), n + 1, 0)
                    recur(n, r)
            n = SEG * N - 1
            dve.wait_ge(c_row_ready, n + 1)
            for c in range(CT):
                if c not in POOL_TILES:
                    dve.wait_ge(scan_done, CT * n + c + 1)
                    st = states[RING - 1][:, c * TQ:(c + 1) * TQ]
                    nc.vector.tensor_tensor(st, st, c_row[n % 2][:], ALU.mult).then_inc(last_product[c], 1)
            gated(SEG - 1)

            for d in range(DIRS):
                for q in range(Q):
                    half = range(q * BQ, (q + 1) * BQ)
                    for h in half[::2]:
                        job_copied(dve, ("mix", d, h // 2))
                    layer_norm((d * Q + q) * BQ, [(mix_tok[d][:, b, :], mix_tok[d][:, b, :]) for b in half])
            for q in range(Q):
                for d in range(DIRS):
                    j, key = d * KD + 1, ("mixT", d, 1, q)
                    job_result(dve, key)
                    nc.vector.tensor_scalar(xT[:, j, chunk(q)], bank(key)[:, 0:TQ], lng_sb[:, j:j + 1],
                                            lnb_sb[:, j:j + 1], ALU.mult, ALU.add).then_inc(copied["v"], 1)

            def add_fused(h):
                job_result(dve, ("fuse", h))
                x_pair = x_tok[:, pair(h), :].rearrange("l b d -> l (b d)")
                nc.vector.tensor_tensor(x_pair, x_pair, bank(("fuse", h))[0:L, :], ALU.add
                                        ).then_inc(copied["v"], 1)

            dve.wait_ge(bias_added, 1)
            for q in range(Q):
                for h in range(q * BQ // 2, (q + 1) * BQ // 2):
                    add_fused(h)
                job_copied(dve, ("fuse", h))
                norm_x(q)

            def low_queries(m, q):
                dve.wait_ge(q_high, q * KD + m + 1)
                nc.vector.tensor_tensor(qT_part[1][:, m, chunk(q)], bank(("qT", m, q))[:, 0:TQ],
                                        qT_part[0][:, m, chunk(q)].bitcast(F32), ALU.subtract
                                        ).then_inc(copied["v"], 1)

            for m in range(KD):
                low_queries(m, 0)

            def low_keys(b, r, m, at=KEY_BANK):
                dve.wait_ge(k_high, 2 * b + (m + 1))
                nc.vector.tensor_tensor(kT_part[r][1][:, m, :], ps[:, at, 0:SE],
                                        kT_part[r][0][:, m, :].bitcast(F32), ALU.subtract).then_inc(k_copied, 1)

            def copy_values(b, r, part, at=KEY_BANK):
                dve.wait_ge(v_done, 2 * b + (part + 1))
                if part == 0:
                    ins = nc.vector.tensor_copy(v_sb[r][:, 0:2, :].rearrange("p k d -> p (k d)"), ps[:, at, :])
                else:
                    ins = nc.vector.tensor_copy(v_sb[r][0:SL, 2, :], ps[0:SL, at, 0:D])
                ins.then_inc(v_copied, 1)

            def maxima(b, r, g):
                dve.wait_ge(scores_ready, GROUPS * b + (g + 1))
                nc.vector.tensor_reduce(neg_max[:, r, 2 * g:2 * g + 2], ps[0:L, g % 2 * 2:g % 2 * 2 + 2, 0:S],
                                        AX.X, ALU.max).then_inc(max_ready, 1)
                dve.wait_ge(max_ready, GROUPS * b + (g + 1))
                nc.vector.tensor_scalar(shift[:, r, 2 * g:2 * g + 2], neg_max[:, r, 2 * g:2 * g + 2],
                                        -HD ** -0.5, None, ALU.mult).then_inc(shift_ready, 1)

            def copy_probs(b, g):
                dve.wait_ge(probsT_ready, GROUPS * b + (g + 1))
                if not isinstance(b, int) or GROUPS * b + g >= 2:
                    dve.wait_ge(pv_done, GROUPS * b + (g - 1))
                nc.vector.tensor_copy(probsT[g % 2][0][:], ps[:, 4, 0:KT * L]).then_inc(probsT_copied[0], 1)

            def normalise_heads(b, r):
                dve.wait_ge(probs_ready, 2 * GROUPS * b + 2 * GROUPS)
                nc.vector.reciprocal(inv_mass[:, r, :], mass[:, r, :]).then_inc(inv_mass_ready, 1)
                dve.wait_ge(inv_mass_ready, b + 1)
                dve.wait_ge(pv_done, GROUPS * b + GROUPS)
                nc.vector.tensor_tensor(heads_tok[:].rearrange("l (h e) -> l h e", h=H),
                                        ps[0:L, 6, 0:D].rearrange("l (h e) -> l h e", h=H),
                                        inv_mass[:, r, :].unsqueeze(2).broadcast_to([L, H, HD]), ALU.mult
                                        ).then_inc(heads_ready, 1)

            def copy_heads(b):
                dve.wait_ge(headsT_done, b + 1)
                nc.vector.tensor_copy(headsT[:].rearrange("p m t -> p (m t)"), ps[:, KEY_BANK, 0:KD * L]
                                      ).then_inc(headsT_copied, 1)

            def add_attention(b):
                dve.wait_ge(bias_added, 2)
                dve.wait_ge(wo_done, b + 1)
                x2 = x_tok[:, bass.ds(b, 1), :].rearrange("l b d -> l (b d)")
                nc.vector.tensor_tensor(x2, x2, ps[0:L, KEY_BANK, 0:D], ALU.add).then_inc(x2_ready, 1)

            def attend(b, r, last=False):
                for g in range(2, GROUPS):
                    copy_probs(b, g)
                    if g + 2 < GROUPS:
                        maxima(b, r, g + 2)
                    elif not last:
                        maxima(b + 1, 1 - r, g + 2 - GROUPS)
                    if g - 2 in range(KD) and not last:
                        low_keys(b + 1, 1 - r, g - 2)
                    if g - 4 in range(2) and not last:
                        copy_values(b + 1, 1 - r, g - 4)
                normalise_heads(b, r)
                if not last:
                    copy_probs(b + 1, 0)
                    maxima(b + 1, 1 - r, 2)
                copy_heads(b)
                if last:
                    norm_x(0)
                if not last:
                    copy_probs(b + 1, 1)
                    maxima(b + 1, 1 - r, 3)
                add_attention(b)

            for m in range(KD):
                low_keys(0, 0, m, FIRST_KEYS[m])
            for k in range(KD):
                copy_out(("xn2T", k, 1), xn2T[:, k, chunk(1)], bank(("xn2T", k, 1))[:, 0:TQ])
            maxima(0, 0, 0)
            maxima(0, 0, 1)
            for part in range(2):
                copy_values(0, 0, part, FIRST_VALUES[part])
            for m in range(KD):
                low_queries(m, 1)
            for g in range(2):
                copy_probs(0, g)
                maxima(0, 0, g + 2)
            with dve.Fori(0, B // 2 - 1) as i:
                for r in range(2):
                    attend(2 * i + r, r)
            attend(B - 2, 0)
            attend(B - 1, 1, last=True)
            dve.wait_ge(x2_ready, B)
            norm_x(1)
            for q in range(Q):
                for k in range(KD):
                    dve.wait_ge(xn3_high, q * KD + k + 1)
                    job_copied(dve, ("xn3T", k, q))
                    nc.vector.tensor_tensor(xn3_part[1][:, k, chunk(q)], xn3T[:, k, chunk(q)],
                                            xn3_part[0][:, k, chunk(q)].bitcast(F32), ALU.subtract
                                            ).then_inc(xn3_split, 1)

            logits = ps[0:L, 2, 0:B * E].rearrange("l (b e) -> l b e", e=E)
            rt, tk = route, per_tok
            prefer_all = prefer[:].unsqueeze(1).broadcast_to([L, B, E])

            def shift_logits():
                dve.wait_ge(logits_ready, 1)
                nc.vector.memset(cw_tok[:, :, E:EA], SHARED).then_inc(shifted_ready, 1)
                step(nc.vector.tensor_reduce(tk["max"][:, :, 0], logits, AX.X, ALU.max))
                nc.vector.tensor_tensor(rt["shifted"][:], logits, spread(tk["max"][:], E), ALU.subtract
                                        ).then_inc(shifted_ready, 1)

            def probabilities():
                dve.wait_ge(exp_ready, 1)
                step(nc.vector.tensor_reduce(tk["sum"][:, :, 0], rt["exp"][:], AX.X, ALU.add))
                step(nc.vector.reciprocal(tk["inv"][:], tk["sum"][:]))
                step(nc.vector.tensor_tensor(rt["prob"][:], rt["exp"][:], spread(tk["inv"][:], E), ALU.mult))

            def largest(src, top, pick, chosen):
                step(nc.vector.tensor_reduce(top[:, :, 0], src, AX.X, ALU.max))
                step(nc.vector.tensor_tensor(rt["tie"][:], src, spread(top[:], E), ALU.is_equal))
                step(nc.vector.tensor_tensor(rt["tie"][:], rt["tie"][:], prefer_all, ALU.mult))
                step(nc.vector.tensor_reduce(pick[:, :, 0], rt["tie"][:], AX.X, ALU.max))
                step(nc.vector.tensor_tensor(chosen, rt["tie"][:], spread(pick[:], E), ALU.is_equal))

            def second_largest():
                step(nc.vector.scalar_tensor_tensor(rt["rest"][:], rt["first"][:], -4.0, rt["prob"][:],
                                                    ALU.mult, ALU.add))
                largest(rt["rest"][:], tk["top2"], tk["pick2"], rt["second"][:])

            def weights():
                step(nc.vector.tensor_tensor(rt["both"][:], rt["first"][:], rt["second"][:], ALU.add))
                step(nc.vector.tensor_tensor(rt["kept"][:], rt["both"][:], rt["prob"][:], ALU.mult))
                step(nc.vector.scalar_tensor_tensor(tk["den"][:, :, 0], tk["top1"][:, :, 0], 1e-9,
                                                    tk["top2"][:, :, 0], ALU.add, ALU.add))
                step(nc.vector.reciprocal(tk["inv_den"][:], tk["den"][:]))
                nc.vector.tensor_tensor(cw_tok[:, :, 0:E], rt["kept"][:], spread(tk["inv_den"][:], E), ALU.mult
                                        ).then_inc(cw_ready, 1)

            def copy_rows():
                dve.wait_ge(cwT_done, 1)
                for q in range(Q):
                    for to in (cwT, cwT_part[0]):
                        nc.vector.tensor_copy(to[:, chunk(q)], ps[0:EA, 2 + q, 0:TQ]).then_inc(cwT_ready, 1)
                    dve.wait_ge(cwT_ready, 3 * q + 2)
                    nc.vector.tensor_tensor(cwT_part[1][:, chunk(q)], cwT[:, chunk(q)],
                                            cwT_part[0][:, chunk(q)].bitcast(F32), ALU.subtract
                                            ).then_inc(cwT_ready, 1)

            def split_hidden(e, u):
                dve.wait_ge(silu_done, 2 * UNITS * e + 2 * (u + 1))
                high, low = hid_part[u % HRING]
                nc.vector.tensor_tensor(low[:], hidden[u % HRING][:], high[:].bitcast(F32), ALU.subtract
                                        ).then_inc(hid_split, 1)

            def add_expert(e, q):
                dve.wait_ge(hid_used, UNITS * e + FT * (q + 1))
                nc.vector.tensor_tensor(
                    weighted[:], ps[:, 4 + 2 * q:6 + 2 * q, 0:TQ],
                    cw_b[:, bass.ds(T * e + TQ * q, TQ)].unsqueeze(1).broadcast_to([P, KD, TQ]), ALU.mult
                    ).then_inc(y_taken, 1)
                dve.wait_ge(y_taken, Q * e + (q + 1))
                nc.vector.tensor_tensor(yT[:, :, chunk(q)], yT[:, :, chunk(q)], weighted[:], ALU.add
                                        ).then_inc(yT_ready, 1)

            def copy_spread(t):
                dve.wait_ge(spread_done, t + 1)
                nc.vector.tensor_copy(spread_to(t, 0), ps[:, 2, 0:TQ]).then_inc(spread_copied[0], 1)

            for u in range(UNITS):
                for t in SPREAD_AT.get(u, ())[:1]:
                    copy_spread(t)
                split_hidden(0, u)
                if u == LOGITS_AT:
                    shift_logits()
                elif u == EXP_AT + 1:
                    probabilities()
                elif u == EXP_AT + 2:
                    largest(rt["prob"][:], tk["top1"], tk["pick1"], rt["first"][:])
                elif u == EXP_AT + 3:
                    second_largest()
                elif u == EXP_AT + 4:
                    weights()
                elif u == ROWS_AT:
                    copy_rows()
                for t in SPREAD_AT.get(u, ())[1:]:
                    copy_spread(t)
                if u == FIRST_SUM_AT:
                    for by in spread_copied:
                        dve.wait_ge(by, KD + 1)
                    add_expert(0, 0)
            for by in spread_copied:
                dve.wait_ge(by, SPREADS)
            with dve.Fori(0, E // 2) as i:
                for j in range(2):
                    for u in range(UNITS):
                        split_hidden(2 * i + (j + 1), u)
                        if u == LAG:
                            add_expert(2 * i + j, 1)
                        if u == FT + LAG:
                            add_expert(2 * i + (j + 1), 0)
            add_expert(E, 1)
            for h in range(B // 2):
                dve.wait_ge(turned_back, h + 1)
                nc.vector.tensor_tensor(out_tok[:, pair(h), :].rearrange("l b d -> l (b d)"),
                                        x_tok[:, pair(h), :].rearrange("l b d -> l (b d)"), ps[0:L, h, :], ALU.add
                                        ).then_inc(out_ready, 1)


_OUT = (B, L, D)


def _laid_out(inputs):
    a = {k: np.asarray(v) for k, v in inputs.items()}

    def per_channel(*columns):
        rows = np.concatenate([c.reshape(DI, -1) for c in columns], axis=1)
        return rows.reshape(CT, P, -1).transpose(1, 0, 2)

    def both(make):
        return np.stack([make(lambda name: a[f"L0_attn_{name}_{s}"]) for s in "fb"])

    def per_feature(name):
        return both(lambda w: w(name)).reshape(DIRS * KD, P).T

    def with_shared(routed, shared):
        return np.concatenate([a[f"L0_ffn_{routed}"], a[f"L0_ffn_{shared}"][None]])

    arrays = {
        "x": a["x"],
        "ctxT": a["ctx_1024"].transpose(0, 2, 1),
        "winT": both(lambda w: w("Win").T),
        "wxT": both(lambda w: np.roll(w("Wx").T, -R, axis=1)),
        "wdtT": both(lambda w: w("Wdt").T),
        "woutT": both(lambda w: w("Wout").T),
        "vec": both(lambda w: per_channel(w("convw"), w("convb"), w("bdt"), w("Dp"), w("Alog"))),
        "ln_g": per_feature("ln_g"),
        "ln_b": per_feature("ln_b"),
        "wfuseT": a["L0_attn_Wfuse"].T,
        "bfuse": a["L0_attn_bfuse"],
        "wqT": a["L0_xattn_Wq"].T,
        "wkT": a["L0_xattn_Wk"].T,
        "wvT": a["L0_xattn_Wv"].T,
        "woT": a["L0_xattn_Wo"].T,
        "bo": a["L0_xattn_bo"],
        "wg": a["L0_ffn_Wg"],
        "w1": with_shared("W1", "Ws1"),
        "b1": with_shared("b1", "bs1").reshape(EA, FT, P).transpose(0, 2, 1),
        "w2": with_shared("W2", "Ws2"),
        "b2": with_shared("b2", "bs2"),
    }
    return {k: np.ascontiguousarray(v) for k, v in arrays.items()}


def kernel(**inputs):
    from concourse import bacc
    from concourse.bass_utils import run_bass_kernel_spmd

    arrays = _laid_out(inputs)
    nc = bacc.Bacc("TRN2", target_bir_lowering=False, num_devices=1)
    aps = {k: nc.dram_tensor(f"in_{k}", v.shape, mybir.dt.from_np(v.dtype), kind="ExternalInput").ap()
           for k, v in arrays.items()}
    out = nc.dram_tensor("out_x", _OUT, F32, kind="ExternalOutput").ap()
    decoder_layer(nc, **aps, out=out)
    result = run_bass_kernel_spmd(nc, [{f"in_{k}": v for k, v in arrays.items()}], core_ids=[0])
    return result.results[0]["out_x"]
```
